# Optimizing a Trainium2 kernel written in Bass

```python
import numpy as np
import jax
import jax.numpy as jnp

def _softmax(x, axis=-1):
    return jax.nn.softmax(x, axis=axis)

def _gelu(x):
    return jax.nn.gelu(x, approximate=True)

def _silu(x):
    return jax.nn.silu(x)

def _sigmoid(x):
    return jax.nn.sigmoid(x)

def _layernorm(x, axis=-1, eps=1e-05):
    m = jnp.mean(x, axis=axis, keepdims=True)
    v = jnp.var(x, axis=axis, keepdims=True)
    return (x - m) / jnp.sqrt(v + eps)

def _scatter_add(tgt, idx, src, axis=0):
    return tgt.at[idx].add(src)

def _segment_sum(src, seg, n):
    return jax.ops.segment_sum(src, seg, n)
kernel_name = 'mk_recurrent_d1_jaxref_r4_080bb4'

def setup_inputs(seed: int=0):
    np.random.seed(seed)
    _w = jnp.asarray

    def _L0_attn_setup():
        import jax, jax.numpy as jnp
        import numpy as np
        B, N, E, H = (1, 1024, 512, 16)
        D = E // H
        DEGREE = 4
        LN_EPS = 1e-05
        ROPE_BASE = 10000.0

        def rope_cos_sin(n, d):
            inv_freq = 1.0 / ROPE_BASE ** (jnp.arange(0, d, 2, dtype=jnp.float32) / d)
            t = jnp.arange(n, dtype=jnp.float32)[:, None] * inv_freq[None, :]
            return (jnp.cos(t), jnp.sin(t))

        def apply_rope(x, cos, sin):
            x1, x2 = jnp.split(x, 2, axis=-1)
            c = cos[None, :, None, :]
            s = sin[None, :, None, :]
            return jnp.concatenate([x1 * c - x2 * s, x1 * s + x2 * c], axis=-1)

        def layernorm(x, scale, bias, eps=LN_EPS):
            m = jnp.mean(x, axis=-1, keepdims=True)
            v = jnp.var(x, axis=-1, keepdims=True)
            return (x - m) * jax.lax.rsqrt(v + eps) * scale + bias

        def polynomial_attention(q, k, v, degree, is_causal):
            a = jnp.einsum('bhnd,bhmd->bhnm', q, k) ** degree
            if is_causal:
                a = jnp.tril(a)
            denom = jnp.sum(a, axis=-1, keepdims=True)
            return jnp.einsum('bhnm,bhmd->bhnd', a / denom, v)
        key = jax.random.key(seed)
        k0, k1, k2 = jax.random.split(key, 3)
        x = jax.random.normal(k0, (B, N, E), dtype=jnp.float32)
        w_qkv = jax.random.normal(k1, (E, 3 * E), dtype=jnp.float32) * (1.0 / np.sqrt(E))
        w_out = jax.random.normal(k2, (E, E), dtype=jnp.float32) * (1.0 / np.sqrt(E))
        ln_scale = jnp.ones((D,), dtype=jnp.float32)
        ln_bias = jnp.zeros((D,), dtype=jnp.float32)
        return {'x': x, 'w_qkv': w_qkv, 'w_out': w_out, 'ln_scale': ln_scale, 'ln_bias': ln_bias}
    _L0_attn_in = _L0_attn_setup()

    def _L0_ffn_setup():
        import jax, jax.numpy as jnp
        import numpy as np
        E = 64
        K = 4
        H = 512
        I = 384
        C = 64
        B, S = (1, 512)
        key = jax.random.key(seed)
        ks = jax.random.split(key, 8)
        sh = 1.0 / np.sqrt(H).astype(np.float32)
        si = 1.0 / np.sqrt(I).astype(np.float32)
        return {'x': jax.random.normal(ks[0], (B, S, H), jnp.float32), 'w_router': jax.random.normal(ks[1], (E, H), jnp.float32) * sh, 'w_gate': jax.random.normal(ks[2], (E, H, I), jnp.float32) * sh, 'w_up': jax.random.normal(ks[3], (E, H, I), jnp.float32) * sh, 'w_down': jax.random.normal(ks[4], (E, I, H), jnp.float32) * si, 'w_sh_gate': jax.random.normal(ks[5], (H, I), jnp.float32) * sh, 'w_sh_up': jax.random.normal(ks[6], (H, I), jnp.float32) * sh, 'w_sh_down': jax.random.normal(ks[7], (I, H), jnp.float32) * si}
    _L0_ffn_in = _L0_ffn_setup()
    _d = {'L0_attn_x': _L0_attn_in['x'], 'L0_attn_w_qkv': _L0_attn_in['w_qkv'], 'L0_attn_w_out': _L0_attn_in['w_out'], 'L0_attn_ln_scale': _L0_attn_in['ln_scale'], 'L0_attn_ln_bias': _L0_attn_in['ln_bias'], 'L0_ffn_w_router': _L0_ffn_in['w_router'], 'L0_ffn_w_gate': _L0_ffn_in['w_gate'], 'L0_ffn_w_up': _L0_ffn_in['w_up'], 'L0_ffn_w_down': _L0_ffn_in['w_down'], 'L0_ffn_w_sh_gate': _L0_ffn_in['w_sh_gate'], 'L0_ffn_w_sh_up': _L0_ffn_in['w_sh_up'], 'L0_ffn_w_sh_down': _L0_ffn_in['w_sh_down']}
    _x0 = _d['L0_attn_x']
    _d['L0_attn_x'] = jax.random.normal(jax.random.fold_in(jax.random.key(seed), 1), (4, 1024, 512), dtype=_x0.dtype)
    del _x0
    return _d

def reference(L0_attn_x, L0_attn_w_qkv, L0_attn_w_out, L0_attn_ln_scale, L0_attn_ln_bias, L0_ffn_w_router, L0_ffn_w_gate, L0_ffn_w_up, L0_ffn_w_down, L0_ffn_w_sh_gate, L0_ffn_w_sh_up, L0_ffn_w_sh_down):

    def _L0_attn_ref(x, w_qkv, w_out, ln_scale, ln_bias):
        import jax, jax.numpy as jnp
        import numpy as np
        B, N, E, H = (1, 1024, 512, 16)
        D = E // H
        DEGREE = 4
        LN_EPS = 1e-05
        ROPE_BASE = 10000.0

        def rope_cos_sin(n, d):
            inv_freq = 1.0 / ROPE_BASE ** (jnp.arange(0, d, 2, dtype=jnp.float32) / d)
            t = jnp.arange(n, dtype=jnp.float32)[:, None] * inv_freq[None, :]
            return (jnp.cos(t), jnp.sin(t))

        def apply_rope(x, cos, sin):
            x1, x2 = jnp.split(x, 2, axis=-1)
            c = cos[None, :, None, :]
            s = sin[None, :, None, :]
            return jnp.concatenate([x1 * c - x2 * s, x1 * s + x2 * c], axis=-1)

        def layernorm(x, scale, bias, eps=LN_EPS):
            m = jnp.mean(x, axis=-1, keepdims=True)
            v = jnp.var(x, axis=-1, keepdims=True)
            return (x - m) * jax.lax.rsqrt(v + eps) * scale + bias

        def polynomial_attention(q, k, v, degree, is_causal):
            a = jnp.einsum('bhnd,bhmd->bhnm', q, k) ** degree
            if is_causal:
                a = jnp.tril(a)
            denom = jnp.sum(a, axis=-1, keepdims=True)
            return jnp.einsum('bhnm,bhmd->bhnd', a / denom, v)
        b, n, e = x.shape
        proj = x @ w_qkv
        q, k, v = jnp.split(proj, 3, axis=-1)
        q = q.reshape(b, n, H, D)
        k = k.reshape(b, n, H, D)
        v = v.reshape(b, n, H, D)
        cos, sin = rope_cos_sin(n, D)
        q = apply_rope(q, cos, sin)
        k = apply_rope(k, cos, sin)
        q = q.transpose(0, 2, 1, 3)
        k = k.transpose(0, 2, 1, 3)
        v = v.transpose(0, 2, 1, 3)
        q = layernorm(q, ln_scale, ln_bias)
        k = layernorm(k, ln_scale, ln_bias)
        out = polynomial_attention(q, k, v, DEGREE, True)
        out = out.transpose(0, 2, 1, 3).reshape(b, n, e)
        out = out @ w_out
        return out

    def _L0_ffn_ref(x, w_router, w_gate, w_up, w_down, w_sh_gate, w_sh_up, w_sh_down):
        import jax, jax.numpy as jnp
        import numpy as np
        E = 64
        K = 4
        H = 512
        I = 384
        C = 64
        B, S = (1, 512)
        b, s, h = x.shape
        xf = x.reshape(-1, h)
        T = xf.shape[0]
        P = T * K
        logits = xf @ w_router.T
        top_vals, top_idx = jax.lax.top_k(logits, K)
        w_tok = jax.nn.softmax(top_vals.astype(jnp.float32), axis=-1)
        e_flat = top_idx.reshape(-1)
        tok_flat = jnp.repeat(jnp.arange(T), K)
        w_flat = w_tok.reshape(-1)
        order = jnp.argsort(e_flat)
        tok_s = tok_flat[order]
        w_s = w_flat[order]
        counts = jnp.zeros((E,), jnp.int32).at[e_flat].add(1)
        offsets = jnp.cumsum(counts) - counts
        pos = offsets[:, None] + jnp.arange(C)[None, :]
        valid = jnp.arange(C)[None, :] < counts[:, None]
        pos_c = jnp.clip(pos, 0, P - 1)
        tok_ec = tok_s[pos_c]
        w_ec = jnp.where(valid, w_s[pos_c], 0.0)
        x_ec = xf[tok_ec]
        g = jax.nn.silu(jnp.einsum('ech,ehi->eci', x_ec, w_gate))
        u = jnp.einsum('ech,ehi->eci', x_ec, w_up)
        y = jnp.einsum('eci,eih->ech', g * u, w_down)
        contrib = (y * w_ec[..., None]).reshape(-1, h)
        combined = jnp.zeros_like(xf).at[tok_ec.reshape(-1)].add(contrib)
        sg = jax.nn.silu(xf @ w_sh_gate)
        su = xf @ w_sh_up
        combined = combined + sg * su @ w_sh_down
        return combined.reshape(b, s, h)
    x = L0_attn_x
    xn = _layernorm(x, axis=-1)
    s = _L0_attn_ref(xn, L0_attn_w_qkv, L0_attn_w_out, L0_attn_ln_scale, L0_attn_ln_bias)
    g = _silu(_L0_ffn_ref(xn, L0_ffn_w_router, L0_ffn_w_gate, L0_ffn_w_up, L0_ffn_w_down, L0_ffn_w_sh_gate, L0_ffn_w_sh_up, L0_ffn_w_sh_down))
    x = x + s * g
    return x

_drawn_inputs = setup_inputs


def setup_inputs(seed=0):
    import zlib

    import numpy as np

    out = dict(_drawn_inputs(seed))
    spreads = {'L0_attn_ln_scale': (1.0, 0.546), 'L0_attn_ln_bias': (0.0, 0.642)}
    factors = {}
    for name, (base, spread) in spreads.items():
        noise = np.random.default_rng([zlib.crc32(name.encode()), seed]).standard_normal(out[name].shape)
        drawn = base * np.exp(spread * noise) if base else spread * noise
        out[name] = jnp.asarray(drawn.astype(out[name].dtype))
    for name, factor in factors.items():
        out[name] = (out[name] * factor).astype(out[name].dtype)
    return out
```

```python
import numpy as np
import concourse.bass as bass
from concourse import mybir
from contextlib import ExitStack

F32 = mybir.dt.float32
F32R = mybir.dt.float32r
U32 = mybir.dt.uint32
I32 = mybir.dt.int32
ALU = mybir.AluOpType
ACT = mybir.ActivationFunctionType
AX = mybir.AxisListType

P = 128
B, N, E = 4, 1024, 512
T = B * N
HEADS = 16
D = E // HEADS
C = E // P
GT = 512
TPG = GT // P
G = T // GT
NT = T // P
PAIRS = HEADS // 2
VW = D + 1
NE, TOPK, CAP = 64, 4, 64
I = 384
IC = I // P
XW = E + NE
EPS = 1e-5


class Links:

    def __init__(self, eng, sem, base, passed):
        self.eng, self.sem, self.base, self.passed, self.n = eng, sem, base, passed, 0

    def __call__(self, ins, apart=False):
        self.n += 1
        ins.then_inc(self.sem, 1)
        self.eng.wait_ge(self.sem, self.base + self.n)
        if apart:
            self.eng.sem_inc(self.passed, 1)




def rope_tables():
    inv = (np.float32(1.0) / np.float32(10000.0) ** (np.arange(0, D, 2, dtype=np.float32) / np.float32(D))).astype(np.float32)
    t = (np.arange(N, dtype=np.float32)[:, None] * inv[None, :]).astype(np.float32)
    c, s = np.cos(t.astype(np.float64)), np.sin(t.astype(np.float64))
    cc = np.concatenate([c, c], 1).astype(np.float32)
    ss = np.concatenate([-s, s], 1).astype(np.float32)

    def lay(a):
        a = a.reshape(N // P, P, D).transpose(1, 0, 2)
        return np.ascontiguousarray(np.concatenate([a] * B, 1))

    return lay(cc), lay(ss)


def split_weights(nc, dram, w):
    parts = [("qkv", C * 3 * E), ("gu", C * 2 * I), ("down", IC * E), ("router", C * NE)]
    with ExitStack() as ctx:
        full = {k: ctx.enter_context(nc.sbuf_tensor(f"full_{k}", [P, n], F32)) for k, n in parts}
        loaded = {k: ctx.enter_context(nc.semaphore(f"w_loaded_{k}")) for k, _ in parts}
        high_done = ctx.enter_context(nc.semaphore("w_high_done"))
        tables = ctx.enter_context(nc.semaphore("tables_loaded"))
        made = ctx.enter_context(nc.semaphore("constants_made"))
        block = ctx.enter_context(nc.Block())

        @block.sync
        def _(sp):
            sp.dma_start(full["qkv"][:].rearrange("p (c n) -> p c n", c=C),
                         dram["w_qkv"].rearrange("(c p) n -> p c n", p=P)).then_inc(loaded["qkv"], 16)
            gu = full["gu"][:].rearrange("p (c two n) -> p c two n", c=C, two=2)
            sp.dma_start(gu[:, :, 0, :], dram["w_sh_gate"].rearrange("(c p) n -> p c n", p=P)).then_inc(loaded["gu"], 16)
            sp.dma_start(gu[:, :, 1, :], dram["w_sh_up"].rearrange("(c p) n -> p c n", p=P)).then_inc(loaded["gu"], 16)
            sp.dma_start(full["down"][:].rearrange("p (c n) -> p c n", c=IC),
                         dram["w_sh_down"].rearrange("(c p) n -> p c n", p=P)).then_inc(loaded["down"], 16)
            sp.dma_start(full["router"][:].rearrange("p (c n) -> p c n", c=C), dram["router"].rearrange("(c p) n -> p c n", p=P)).then_inc(loaded["router"], 16)
            sp.dma_start(w["cos"][:], dram["cos"]).then_inc(tables, 16)
            sp.dma_start(w["sin"][:], dram["sin"]).then_inc(tables, 16)
            for r in range(P // D):
                sp.dma_start(w["ln_scale"][r * D:(r + 1) * D, :], dram["ln_scale"].rearrange("(d a) -> d a", a=1)).then_inc(tables, 16)
                sp.dma_start(w["ln_bias"][r * D:(r + 1) * D, :], dram["ln_bias"].rearrange("(d a) -> d a", a=1)).then_inc(tables, 16)
            sp.wait_ge(tables, 16 * (2 + 2 * P // D))

        @block.scalar
        def _(act):
            for k, _n in parts:
                act.wait_ge(loaded[k], 32 if k == "gu" else 16)
                nc.scalar.activation(w[k + "_hi"][:], full[k][:], ACT.Copy).then_inc(high_done, 1)

        @block.vector
        def _(dve):
            for i, (k, _n) in enumerate(parts):
                dve.wait_ge(high_done, i + 1)
                nc.vector.tensor_tensor(w[k + "_lo"][:], full[k][:], w[k + "_hi"][:].bitcast(F32), ALU.subtract)

        @block.gpsimd
        def _(pool):
            nc.gpsimd.memset(w["ident"][:], 0.0).then_inc(made, 1)
            pool.wait_ge(made, 1)
            nc.gpsimd.affine_select(out=w["ident"][:], in_=w["ident"][:], compare_op=ALU.not_equal, fill=1.0,
                                    base=0, pattern=[[-1, P]], channel_multiplier=1)
            nc.gpsimd.iota(w["expert_i"][:], pattern=[[1, NE]], base=0, channel_multiplier=0).then_inc(made, 1)
            pool.wait_ge(made, 2)
            nc.gpsimd.tensor_copy(w["expert"][:], w["expert_i"][:])
            nc.gpsimd.memset(w["minus_half"][:], -0.5)


def project(nc, dram, w):
    with ExitStack() as ctx:
        sb = lambda name, shape, dt=F32: ctx.enter_context(nc.sbuf_tensor(name, shape, dt))
        sem = lambda name: ctx.enter_context(nc.semaphore(name))
        bank = lambda name: ctx.enter_context(nc.psum_tensor(name, [P, 512], F32))

        x = sb("x_group", [P, TPG, E])
        stats = sb("x_stats", [P, TPG, 6])
        mv = sb("x_mean_var", [P, TPG, 2])
        xvar = sb("x_var", [P, TPG])
        xrstd = sb("x_rstd", [P, TPG])
        xT_hi = sb("xT_hi", [P, C, GT], F32R)
        xT_lo = sb("xT_lo", [P, C, GT], F32R)
        rope = sb("rope_a", [P, 2 * E])
        rope_b = sb("rope_b", [P, 2 * E])
        cen = sb("centred", [P, 2 * E])
        y = sb("qk_normed", [P, 2 * E])
        hsum = sb("head_sum", [P, 2 * HEADS])
        hmean = sb("head_mean", [P, 2 * HEADS])
        hvar = sb("head_var", [P, 2 * HEADS])
        hrstd = sb("head_rstd", [P, 2 * HEADS])
        qkT = sb("qkT_full", [P, 2, C, P])
        qkT_hi = sb("qkT_hi", [P, 2, C, P], F32R)
        qkT_lo = sb("qkT_lo", [P, 2, C, P], F32R)
        v = sb("v_group", [P, PAIRS, TPG, 2, VW])
        sg = sb("sh_silu", [P, GT])
        hf = sb("sh_hidden", [P, GT])
        hT_hi = sb("sh_hT_hi", [P, IC, GT], F32R)
        hT_lo = sb("sh_hT_lo", [P, IC, GT], F32R)
        ffn = sb("sh_out", [P, 2, E])
        lgT = sb("logitsT", [NE, GT])
        lg = sb("logits", [P, TPG, NE])
        top = sb("top8", [P, TPG, 8])
        topi = sb("top8_index", [P, TPG, 8], U32)
        topf = sb("top8_index_f", [P, TPG, 8])
        hit = sb("hit", [P, TPG, NE])
        hits = sb("hits", [P, TPG, NE])

        TR = [bank("tr0"), bank("tr1")]
        QK = ctx.enter_context(nc.psum_tensor("qk", [P, 2 * E], F32))
        V = bank("v")
        GATE, UP, DN = bank("gate"), bank("up"), bank("down")
        DOWN = [DN, GATE, UP, DN]

        x_loaded, x_stored, x_transposed = sem("x_loaded"), sem("x_stored"), sem("x_transposed")
        var_ready, rstd_ready, xn_ready = sem("x_var_ready"), sem("x_rstd_ready"), sem("xn_ready")
        xT_high, xT_low = sem("xT_high"), sem("xT_low")
        qk_full, v_full, v_copied, v_stored, v_ones = sem("qk_full"), sem("v_full"), sem("v_copied"), sem("v_stored"), sem("v_ones")
        rope_parts, roped, centred, squared = sem("rope_parts"), sem("roped"), sem("centred"), sem("squared")
        hvar_ready, hrstd_ready, y_ready = sem("hvar_ready"), sem("hrstd_ready"), sem("y_ready")
        q_transposed, k_transposed = sem("q_transposed"), sem("k_transposed")
        q_copied, k_copied = sem("q_copied"), sem("k_copied")
        qkT_high, qkT_low, qkT_stored = sem("qkT_high"), sem("qkT_low"), sem("qkT_stored")
        gate_full, up_full = sem("gate_full"), sem("up_full")
        silu_done, hidden_done, hidden_high, hidden_low = sem("silu_done"), sem("hidden_done"), sem("hidden_high"), sem("hidden_low")
        down_full, ffn_copied = sem("down_full"), sem("ffn_copied")
        ffn_stored = [sem("ffn_stored0"), sem("ffn_stored1")]
        logitsT_full, logitsT_copied = sem("logitsT_full"), sem("logitsT_copied")
        logits_full, logits_copied = sem("logits_full"), sem("logits_copied")
        dve_order, passed = sem("dve_order"), sem("passed")

        x_dram = dram["x"].rearrange("(g j p) e -> g p j e", p=P, j=TPG)
        xw_dram = dram["xw"].rearrange("(g j p) e -> g p j e", p=P, j=TPG)
        ffn_dram = dram["ffn"][0:T, :].rearrange("(t p) e -> t p e", p=P)
        qk_dram = [[dram[s][h].rearrange("(c p) n -> p c n", p=P) for h in range(2)] for s in ("qT", "kT")]

        block = ctx.enter_context(nc.Block())

        def groups(eng, first, body):
            first()
            with eng.Fori(0, G - 1) as g:
                body(g, True)
            body(G - 1, False)

        @block.sync
        def _(sp):
            def load_x(g):
                sp.dma_start(x[:], x_dram[bass.ds(g, 1)].rearrange("a p j e -> p (a j) e")).then_inc(x_loaded, 16)

            def store_xn(g):
                sp.wait_ge(xn_ready, g + 1)
                sp.dma_start(xw_dram[bass.ds(g, 1)].rearrange("a p j e -> p (a j) e")[:, :, 0:E], x[:]).then_inc(x_stored, 16)

            def store_qk(g, j):
                n = TPG * g + j
                sp.wait_ge(qkT_high, n + 1)
                sp.wait_ge(qkT_low, n + 1)
                for s in range(2):
                    for h, src in enumerate((qkT_hi, qkT_lo)):
                        sp.dma_start(qk_dram[s][h][:, :, bass.ds(n * P, P)], src[:, s].bitcast(F32)).then_inc(qkT_stored, 16)

            def body(g, has_next):
                if has_next:
                    sp.wait_ge(x_transposed, C * (g + 1))
                    sp.sem_inc(passed, 1)
                    sp.wait_ge(x_stored, 16 * (g + 1))
                    sp.sem_inc(passed, 1)
                    load_x(g + 1)
                store_qk(g, 0)
                store_qk(g, 1)
                if has_next:
                    store_xn(g + 1)
                sp.wait_ge(v_copied, TPG * (g + 1))
                sp.dma_start(dram["v"][bass.ds(g, 1)].rearrange("a q p n -> p (a q) n"),
                             v[:].rearrange("p q j h d -> p q (j h d)")).then_inc(v_stored, 16)
                store_qk(g, 2)
                for j in range(TPG):
                    sp.wait_ge(ffn_copied, TPG * g + j + 1)
                    sp.dma_start(ffn_dram[bass.ds(TPG * g + j, 1)].rearrange("a p e -> p (a e)"),
                                 ffn[:, j % 2]).then_inc(ffn_stored[j % 2], 16)
                store_qk(g, 3)

            def first():
                load_x(0)
                store_xn(0)

            groups(sp, first, body)
            sp.wait_ge(x_stored, 16 * G)
            sp.wait_ge(qkT_stored, 16 * 4 * NT)
            sp.wait_ge(v_stored, 16 * G)
            for s in ffn_stored:
                sp.wait_ge(s, 16 * NT // 2)

        @block.gpsimd
        def _(pool):
            nc.gpsimd.memset(v[:], 1.0).then_inc(v_ones, 1)

            def x_rstd(g):
                pool.wait_ge(var_ready, g + 1)
                nc.gpsimd.tensor_tensor(xrstd[:], xvar[:], w["minus_half"][:, 0:TPG], ALU.pow).then_inc(rstd_ready, 1)

            def body(g, has_next):
                for j in range(TPG):
                    n = TPG * g + j
                    if j == 3 and has_next:
                        x_rstd(g + 1)
                    pool.wait_ge(rope_parts, n + 1)
                    nc.gpsimd.tensor_tensor(rope[:], rope[:], rope_b[:], ALU.add).then_inc(roped, 1)
                    pool.wait_ge(hvar_ready, n + 1)
                    nc.gpsimd.tensor_tensor(hrstd[:], hvar[:], w["minus_half"][:], ALU.pow).then_inc(hrstd_ready, 1)

            groups(pool, lambda: x_rstd(0), body)

        @block.scalar
        def _(act):
            def x_high(g):
                act.wait_ge(v_full, TPG * g)
                for c in range(C):
                    act.wait_ge(x_transposed, C * g + c + 1)
                    nc.scalar.activation(xT_hi[:, c], TR[c % 2][:], ACT.Copy).then_inc(xT_high, 1)

            def copy_logitsT(g):
                act.wait_ge(logitsT_full, g + 1)
                act.wait_ge(logits_full, g)
                nc.scalar.activation(lgT[:], TR[0][0:NE, :], ACT.Copy).then_inc(logitsT_copied, 1)

            def qk_out(g, j):
                n = TPG * g + j
                act.wait_ge(qkT_low, n)
                for s, (full, copied) in enumerate(((q_transposed, q_copied), (k_transposed, k_copied))):
                    act.wait_ge(full, n + 1)
                    nc.scalar.activation(qkT[:, s], TR[s][:].rearrange("p (c t) -> p c t", c=C), ACT.Identity,
                                         scale=w["ln_scale"][:, 0:1], bias=w["ln_bias"][:, 0:1]).then_inc(copied, 1)
                act.wait_ge(q_copied, n + 1)
                act.wait_ge(k_copied, n + 1)
                act.wait_ge(qkT_stored, 16 * 4 * n)
                nc.scalar.activation(qkT_hi[:], qkT[:], ACT.Copy).then_inc(qkT_high, 1)

            def body(g, has_next):
                for j in range(TPG):
                    n, m = TPG * g + j, IC * g + j
                    act.wait_ge(v_full, n + 1)
                    if j == 0:
                        act.wait_ge(v_ones, 1)
                        act.wait_ge(v_stored, 16 * g)
                    nc.scalar.activation(v[:, :, j, :, 0:D], V[:].rearrange("p (q h d) -> p q h d", q=PAIRS, h=2),
                                         ACT.Copy).then_inc(v_copied, 1)
                    if j < IC:
                        act.wait_ge(gate_full, m + 1)
                        act.wait_ge(hidden_done, m)
                        nc.scalar.activation(sg[:], GATE[:], ACT.Silu).then_inc(silu_done, 1)
                    elif has_next:
                        x_high(g + 1)
                    if j >= 1:
                        qk_out(g, j - 1)
                    act.wait_ge(centred, n + 1)
                    nc.scalar.activation(rope_b[:], cen[:], ACT.Square).then_inc(squared, 1)
                    if j < IC:
                        act.wait_ge(hidden_done, m + 1)
                        act.wait_ge(down_full, TPG * g)
                        nc.scalar.activation(hT_hi[:, j], hf[:], ACT.Copy).then_inc(hidden_high, 1)
                for j in range(TPG):
                    act.wait_ge(down_full, TPG * g + j + 1)
                    act.wait_ge(ffn_stored[j % 2], 16 * (2 * g + j // 2))
                    nc.scalar.activation(ffn[:, j % 2], DOWN[j][:], ACT.Copy).then_inc(ffn_copied, 1)
                if has_next:
                    copy_logitsT(g + 1)
                qk_out(g, TPG - 1)

            def first():
                x_high(0)
                copy_logitsT(0)

            groups(act, first, body)

        @block.vector
        def _(dve):
            def x_stats(g, tiles, link):
                for j in tiles:
                    if j == 0:
                        dve.wait_ge(x_loaded, 16 * (g + 1))
                    link(nc.vector.bn_stats(stats[:, j], x[:, j]), apart=True)
                    link(nc.vector.bn_aggr(mv[:, j], stats[:, j]))
                if 3 in tiles:
                    nc.vector.tensor_scalar(xvar[:], mv[:, :, 1], EPS, None, ALU.add).then_inc(var_ready, 1)

            def x_norm(g):
                dve.wait_ge(rstd_ready, g + 1)
                for j in range(TPG):
                    last = nc.vector.tensor_scalar(x[:, j], x[:, j], mv[:, j, 0:1], xrstd[:, j:j + 1],
                                                   ALU.subtract, ALU.mult)
                last.then_inc(xn_ready, 1)

            def x_low(g):
                for c in range(C):
                    dve.wait_ge(xT_high, C * g + c + 1)
                    nc.vector.tensor_tensor(xT_lo[:, c], TR[c % 2][:], xT_hi[:, c].bitcast(F32),
                                            ALU.subtract).then_inc(xT_low, 1)

            def route(g, link):
                dve.wait_ge(logits_full, g + 1)
                nc.vector.tensor_copy(lg[:], TR[1][:, 0:TPG * NE].rearrange("p (j n) -> p j n", j=TPG)).then_inc(logits_copied, 1)
                dve.wait_ge(logits_copied, g + 1)
                dve.sem_inc(passed, 1)
                for j in range(TPG):
                    last = nc.vector.max(top[:, j], lg[:, j])
                link(last, apart=True)
                for j in range(TPG):
                    last = nc.vector.max_index(topi[:, j], top[:, j], lg[:, j])
                link(last)
                link(nc.vector.tensor_copy(topf[:], topi[:]))
                nums = w["expert"][:].unsqueeze(1).broadcast_to([P, TPG, NE])
                for k in range(TOPK):
                    link(nc.vector.tensor_tensor((hit if k else hits)[:], nums, topf[:, :, k:k + 1].broadcast_to([P, TPG, NE]), ALU.is_equal))
                    if k:
                        dst = hits[:] if k < TOPK - 1 else w["mask"][:, bass.ds(TPG * g, TPG), :]
                        link(nc.vector.tensor_tensor(dst, hits[:], hit[:], ALU.add))
                nc.vector.tensor_tensor(w["ldiff"][:, bass.ds(TPG * g, TPG), :], lg[:],
                                        top[:, :, 0:1].broadcast_to([P, TPG, NE]), ALU.subtract)

            heads = lambda t: t[:].rearrange("p (h d) -> p h d", d=D)
            wide = lambda t: t[:].unsqueeze(2).broadcast_to([P, 2 * HEADS, D])
            half = D // 2

            def rotate(g, j):
                n = TPG * g + j
                dve.wait_ge(qk_full, n + 1)
                cos = w["cos"][:, bass.ds(n, 1), :].broadcast_to([P, 2 * HEADS, D])
                sin = w["sin"][:, bass.ds(n, 1), :].broadcast_to([P, 2 * HEADS, D])
                q = heads(QK)
                nc.vector.tensor_tensor(heads(rope), q, cos, ALU.mult)
                nc.vector.tensor_tensor(heads(rope_b)[:, :, 0:half], q[:, :, half:D], sin[:, :, 0:half], ALU.mult)
                nc.vector.tensor_tensor(heads(rope_b)[:, :, half:D], q[:, :, 0:half], sin[:, :, half:D],
                                        ALU.mult).then_inc(rope_parts, 1)

            def centre(g, j, link):
                dve.wait_ge(roped, TPG * g + j + 1)
                link(nc.vector.tensor_reduce(hsum[:], heads(rope), AX.X, ALU.add))
                link(nc.vector.tensor_scalar(hmean[:], hsum[:], 1.0 / D, None, ALU.mult))
                nc.vector.tensor_tensor(heads(cen), heads(rope), wide(hmean), ALU.subtract).then_inc(centred, 1)

            def norm(g, j, link):
                n = TPG * g + j
                dve.wait_ge(squared, n + 1)
                link(nc.vector.tensor_reduce(hsum[:], heads(rope_b), AX.X, ALU.add))
                nc.vector.tensor_scalar(hvar[:], hsum[:], 1.0 / D, EPS, ALU.mult, ALU.add).then_inc(hvar_ready, 1)
                dve.wait_ge(hrstd_ready, n + 1)
                dve.wait_ge(k_transposed, n)
                nc.vector.tensor_tensor(heads(y), heads(cen), wide(hrstd), ALU.mult).then_inc(y_ready, 1)

            def qk_low(g, j):
                n = TPG * g + j
                dve.wait_ge(qkT_high, n + 1)
                dve.wait_ge(qkT_stored, 16 * 4 * n)
                nc.vector.tensor_tensor(qkT_lo[:], qkT[:], qkT_hi[:].bitcast(F32), ALU.subtract).then_inc(qkT_low, 1)

            def hidden(g, j):
                m = IC * g + j
                dve.wait_ge(silu_done, m + 1)
                dve.wait_ge(up_full, m + 1)
                dve.wait_ge(hidden_low, m)
                nc.vector.tensor_tensor(hf[:], sg[:], UP[:], ALU.mult).then_inc(hidden_done, 1)

            def hidden_rest(g, j):
                dve.wait_ge(hidden_high, IC * g + j + 1)
                nc.vector.tensor_tensor(hT_lo[:, j], hf[:], hT_hi[:, j].bitcast(F32), ALU.subtract).then_inc(hidden_low, 1)

            FIRST_LINKS, ROUTE_LINKS = 2 * TPG, 3 + 2 * TOPK - 1
            GROUP_LINKS = 2 * TPG + ROUTE_LINKS + 3 * TPG

            def body(g, has_next):
                link = Links(dve, dve_order, FIRST_LINKS + GROUP_LINKS * g, passed)
                for j in range(TPG):
                    if j == 3 and has_next:
                        x_norm(g + 1)
                    rotate(g, j)
                    if j == 0:
                        route(g, link)
                    if has_next and j < 3:
                        x_stats(g + 1, ([0], [1], [2, 3])[j], link)
                    if j == 3 and has_next:
                        x_low(g + 1)
                    centre(g, j, link)
                    if j < IC:
                        hidden(g, j)
                    if j == 3:
                        qk_low(g, 2)
                    norm(g, j, link)
                    if 1 <= j < 3:
                        qk_low(g, j - 1)
                    if j < IC:
                        hidden_rest(g, j)
                qk_low(g, 3)
                if has_next:
                    assert link.n == GROUP_LINKS, link.n

            def first():
                link = Links(dve, dve_order, 0, passed)
                x_stats(0, [0, 1, 2, 3], link)
                x_norm(0)
                x_low(0)
                assert link.n == FIRST_LINKS, link.n

            groups(dve, first, body)

        @block.tensor
        def _(pe):
            def three(out, hi, lo, w_hi, w_lo, start, stop):
                nc.tensor.matmul(out, hi, w_hi, start=start, stop=False)
                nc.tensor.matmul(out, hi, w_lo, start=False, stop=False)
                return nc.tensor.matmul(out, lo, w_hi, start=False, stop=stop)

            def transposes_x(g):
                pe.wait_ge(xn_ready, g + 1)
                for c in range(C):
                    if c < 2:
                        if not (isinstance(g, int) and g == 0):
                            pe.wait_ge((q_copied, k_copied)[c], TPG * g - 2)
                    else:
                        pe.wait_ge(xT_low, C * g + c - 1)
                    for j in range(TPG):
                        last = nc.tensor.transpose(TR[c % 2][:, j * P:(j + 1) * P], x[:, j, c * P:(c + 1) * P], w["ident"][:])
                    last.then_inc(x_transposed, 1)

            wr = [w["router_" + s][:].rearrange("p (c n) -> p c n", c=C) for s in ("hi", "lo")]
            wq = [w["qkv_" + s][:].rearrange("p (c k n) -> p c k n", c=C, k=3) for s in ("hi", "lo")]
            wg = [w["gu_" + s][:].rearrange("p (c two n) -> p c two n", c=C, two=2) for s in ("hi", "lo")]
            wd = [w["down_" + s][:].rearrange("p (c n) -> p c n", c=IC) for s in ("hi", "lo")]

            def logitsT(g):
                pe.wait_ge(xT_low, C * (g + 1))
                if not (isinstance(g, int) and g == 0):
                    pe.wait_ge(q_copied, TPG * g - 1)
                for c in range(C):
                    last = three(TR[0][0:NE, :], wr[0][:, c], wr[1][:, c], xT_hi[:, c], xT_lo[:, c], c == 0, c == C - 1)
                last.then_inc(logitsT_full, 1)

            def logits(g):
                pe.wait_ge(k_copied, TPG * g)
                pe.wait_ge(logitsT_copied, g + 1)
                pe.sem_inc(passed, 1)
                for j in range(TPG):
                    last = nc.tensor.transpose(TR[1][:, j * NE:(j + 1) * NE], lgT[:, j * P:(j + 1) * P], w["ident"][0:NE, 0:NE])
                last.then_inc(logits_full, 1)

            def qkv(g, j):
                n = TPG * g + j
                pe.wait_ge(xT_low, C * (g + 1))
                pe.wait_ge(rope_parts, n)
                for k in range(3):
                    if k == 2:
                        pe.wait_ge(v_copied, n)
                    out = QK[:, k * E:(k + 1) * E] if k < 2 else V[:]
                    for c in range(C):
                        t = slice(j * P, (j + 1) * P)
                        last = three(out, xT_hi[:, c, t], xT_lo[:, c, t], wq[0][:, c, k], wq[1][:, c, k], c == 0, c == C - 1)
                    if k > 0:
                        last.then_inc((qk_full, v_full)[k - 1], 1)

            def gate_up(g, m):
                t = slice(m * P, (m + 1) * P)
                if m == 0:
                    pe.wait_ge(ffn_copied, TPG * g)
                for k, (out, full, free) in enumerate(((GATE, gate_full, silu_done), (UP, up_full, hidden_done))):
                    pe.wait_ge(free, IC * g + m)
                    for c in range(C):
                        nc.tensor.matmul(out[:], wg[0][:, c, k, t], xT_hi[:, c], start=(c == 0), stop=False)
                        nc.tensor.matmul(out[:], wg[0][:, c, k, t], xT_lo[:, c], start=False, stop=False)
                        last = nc.tensor.matmul(out[:], wg[1][:, c, k, t], xT_hi[:, c], start=False, stop=(c == C - 1))
                    last.then_inc(full, 1)

            def qk_transposes(g, j, has_next):
                n = TPG * g + j
                pe.wait_ge(y_ready, n + 1)
                pe.wait_ge(q_copied, n)
                if j == 0:
                    pe.wait_ge(logitsT_copied, g + 1)
                if j == 2 and has_next:
                    pe.wait_ge(xT_low, C * (g + 1) + 4)
                if j == 3 and has_next:
                    pe.wait_ge(logitsT_copied, g + 2)
                for c in range(C):
                    last = nc.tensor.transpose(TR[0][:, c * P:(c + 1) * P], y[:, c * P:(c + 1) * P], w["ident"][:])
                last.then_inc(q_transposed, 1)
                pe.wait_ge(k_copied, n)
                if j == 0:
                    pe.wait_ge(logits_copied, g + 1)
                for c in range(C):
                    last = nc.tensor.transpose(TR[1][:, c * P:(c + 1) * P], y[:, E + c * P:E + (c + 1) * P], w["ident"][:])
                last.then_inc(k_transposed, 1)

            def down(g, j):
                if j == 0:
                    pe.wait_ge(hidden_low, IC * (g + 1))
                    pe.wait_ge(ffn_copied, TPG * g)
                elif j == 1:
                    pe.wait_ge(silu_done, IC * (g + 1))
                elif j == 2:
                    pe.wait_ge(hidden_done, IC * (g + 1))
                else:
                    pe.wait_ge(ffn_copied, TPG * g + 1)
                t = slice(j * P, (j + 1) * P)
                for c in range(IC):
                    last = three(DOWN[j][:], hT_hi[:, c, t], hT_lo[:, c, t], wd[0][:, c], wd[1][:, c], c == 0, c == IC - 1)
                last.then_inc(down_full, 1)

            def body(g, has_next):
                for j in range(TPG):
                    qkv(g, j)
                    if j < IC:
                        gate_up(g, j)
                    if j == 0:
                        logits(g)
                    if j == 3 and has_next:
                        transposes_x(g + 1)
                    if j >= 1:
                        qk_transposes(g, j - 1, has_next)
                for j in range(TPG):
                    down(g, j)
                if has_next:
                    logitsT(g + 1)
                qk_transposes(g, 3, has_next)

            def first():
                transposes_x(0)
                logitsT(0)

            groups(pe, first, body)


def list_tokens(nc, dram, w):
    HALF_T, HALF_NT = T // 2, NT // 2
    with ExitStack() as ctx:
        sb = lambda name, shape, dt=F32: ctx.enter_context(nc.sbuf_tensor(name, shape, dt))
        sem = lambda name: ctx.enter_context(nc.semaphore(name))
        total, rtotal = sb("weight_total", [P, NT]), sb("weight_rtotal", [P, NT])
        wide = lambda t: t[:].unsqueeze(2).broadcast_to([P, NT, NE])
        down_i, down_f = sb("downcount_i", [P, HALF_T], I32), sb("downcount", [P, HALF_T])
        pairs = sb("mark_pairs", [P, HALF_NT, 2, NE])
        key = sb("key", [P, HALF_T])
        found = sb("found", [P, CAP])
        both = sb("found_both", [NE, 2 * CAP])
        first = sb("first", [NE, CAP])
        token = sb("token", [CAP, NE])
        empty = sb("empty", [CAP, NE])
        slot_i, slot = sb("slot_i", [CAP, 1], I32), sb("slot", [CAP, 1])
        zeros = sb("zero_rows", [CAP, E])
        banks = [ctx.enter_context(nc.psum_tensor(f"mask_bank{i}", [P, 512], F32)) for i in range(4)]
        lists = ctx.enter_context(nc.psum_tensor("lists", [P, 512], F32))

        marks_paired, counted, exp_done, weights_done, masks_turned = sem("marks_paired"), sem("counted"), sem("exp_done"), sem("weights_done"), sem("masks_turned")
        first_done, lists_turned, zeroed, stored, order = sem("first_done"), sem("lists_turned"), sem("zeroed"), sem("rows_stored"), sem("order")
        block = ctx.enter_context(nc.Block())

        @block.gpsimd
        def _(pool):
            nc.gpsimd.memset(zeros[:], 0.0).then_inc(zeroed, 1)
            for h in range(2):
                nc.gpsimd.iota(down_i[h * NE:(h + 1) * NE, :], pattern=[[-1, HALF_T]], base=T - h * HALF_T,
                               channel_multiplier=0)
            nc.gpsimd.iota(slot_i[:], pattern=[[1, 1]], base=0, channel_multiplier=1).then_inc(counted, 1)

        @block.tensor
        def _(pe):
            for q in range(4):
                for t in range(4):
                    if t == 0:
                        pe.wait_ge(marks_paired, q + 1)
                    last = nc.tensor.transpose(banks[q][:, t * P:(t + 1) * P], pairs[:, 4 * q + t].rearrange("p h n -> p (h n)"), w["ident"][:])
                last.then_inc(masks_turned, 1)
            pe.wait_ge(first_done, 1)
            nc.tensor.transpose(lists[0:CAP, 0:NE], first[:], w["ident"][0:NE, 0:NE]).then_inc(lists_turned, 1)

        @block.scalar
        def _(act):
            by_half = w["mask"][:].rearrange("p (h t) n -> p t h n", h=2)
            for q in range(4):
                part = slice(4 * q, 4 * q + 4)
                nc.scalar.activation(pairs[:, part], by_half[:, part], ACT.Copy).then_inc(marks_paired, 1)
            nc.scalar.activation(w["ldiff"][:], w["ldiff"][:], ACT.Exp).then_inc(exp_done, 1)

        @block.vector
        def _(dve):
            link = Links(dve, order, 0, None)
            dve.wait_ge(counted, 1)
            link(nc.vector.tensor_copy(down_f[:], down_i[:]))
            for q in range(4):
                dve.wait_ge(masks_turned, q + 1)
                last = nc.vector.tensor_tensor(key[:, q * 512:(q + 1) * 512], banks[q][:], down_f[:, q * 512:(q + 1) * 512], ALU.mult)
            link(last)
            dve.wait_ge(exp_done, 1)
            link(nc.vector.tensor_tensor(w["ldiff"][:], w["ldiff"][:], w["mask"][:], ALU.mult))
            link(nc.vector.tensor_reduce(total[:], w["ldiff"][:], AX.X, ALU.add))
            link(nc.vector.reciprocal(rtotal[:], total[:]))
            nc.vector.tensor_tensor(w["ldiff"][:], w["ldiff"][:], wide(rtotal), ALU.mult).then_inc(weights_done, 1)
            for r in range(CAP // 8):
                eight = found[:, 8 * r:8 * r + 8]
                link(nc.vector.max(eight, key[:]))
                link(nc.vector.match_replace(out=key[:], in_to_replace=eight, in_values=key[:], imm_value=0.0))
            nc.vector.tensor_copy(both[:, 0:CAP], found[0:NE, :])
            link(nc.vector.tensor_copy(both[:, CAP:], found[NE:, :]))
            for r in range(CAP // 8):
                eight = first[:, 8 * r:8 * r + 8]
                ins = nc.vector.max(eight, both[:])
                if r == CAP // 8 - 1:
                    ins.then_inc(first_done, 1)
                else:
                    link(ins)
                    link(nc.vector.match_replace(out=both[:], in_to_replace=eight, in_values=both[:], imm_value=0.0))
            dve.wait_ge(lists_turned, 1)
            link(nc.vector.tensor_scalar(token[:], lists[0:CAP, 0:NE], -1.0, float(T), ALU.mult, ALU.add))
            link(nc.vector.tensor_copy(slot[:], slot_i[:]))
            link(nc.vector.tensor_scalar(empty[:], token[:], float(T), slot[:, 0:1], ALU.is_equal, ALU.mult))
            nc.vector.tensor_tensor(w["scatter_to"][:], token[:], empty[:], ALU.add)
            two = token[:].rearrange("s (q h) -> s h q", h=2)
            for h in range(2):
                last = nc.vector.tensor_scalar(w["gather_from"][h * CAP:(h + 1) * CAP, 0:NE // 2], two[:, h], float(T - 1), None, ALU.min)
            link(last)
            nc.vector.tensor_copy(w["gather_from"][:, NE // 2:], w["gather_from"][:, 0:1])

        @block.sync
        def _(sp):
            sp.wait_ge(zeroed, 1)
            sp.dma_start(dram["ffn"][T:, :], zeros[:]).then_inc(stored, 16)
            sp.wait_ge(weights_done, 1)
            sp.dma_start(dram["xw"].rearrange("(t p) e -> p t e", p=P)[:, :, E:], w["ldiff"][:]).then_inc(stored, 16)
            sp.wait_ge(stored, 32)


def attend(nc, dram, w):
    K3 = 3 * D
    EP = NE // 2
    with ExitStack() as ctx:
        sb = lambda name, shape, dt=F32: ctx.enter_context(nc.sbuf_tensor(name, shape, dt))
        sem = lambda name: ctx.enter_context(nc.semaphore(name))
        two = lambda f: [f(0), f(1)]
        qs = two(lambda u: sb(f"q_stack{u}", [K3, 2, N], F32R))
        ks = two(lambda u: sb(f"k_stack{u}", [K3, 2, N], F32R))
        vs = two(lambda u: sb(f"v_pair{u}", [P, N // P, 2 * VW]))
        wg = two(lambda u: sb(f"w_gate{u}", [P, 2, C, I]))
        wu = two(lambda u: sb(f"w_up{u}", [P, 2, C, I]))
        wd = sb("w_down", [P, 2, IC, E])
        a = two(lambda h: two(lambda r: sb(f"probs{h}{r}", [P, N])))
        o_raw = two(lambda u: sb(f"o_raw{u}", [P, N]))
        oT = sb("oT", [P, C, N])
        den, rden = sb("den", [2 * HEADS, N]), sb("rden", [2 * HEADS, N])
        rden_parts = sb("rden_parts", [4 * HEADS, N], F32R)
        on_hi, on_lo = sb("on_hi", [P, C, 512], F32R), sb("on_lo", [P, C, 512], F32R)
        wo_hi, wo_lo = sb("w_out_hi", [P, C, E], F32R), sb("w_out_lo", [P, C, E], F32R)
        sel_f, sel = sb("sel_f", [4 * HEADS, C, P]), sb("sel", [4 * HEADS, C, P], F32R)
        gi = two(lambda u: sb(f"gather_now{u}", [P, 1], U32))
        si = two(lambda u: sb(f"scatter_now{u}", [CAP, 2], U32))
        wt = two(lambda u: sb(f"weight_now{u}", [P, 1]))
        xg = two(lambda u: sb(f"x_rows{u}", [P, XW]))
        xgT = sb("x_rowsT", [P, C, P])
        esg, eh = sb("e_silu", [P, I]), sb("e_hidden", [P, I])
        ehT = sb("e_hiddenT", [P, IC, P])
        ey = two(lambda u: sb(f"e_out{u}", [P, E]))
        s_out = two(lambda u: sb(f"s_out{u}", [P, E]))

        S = two(lambda h: ctx.enter_context(nc.psum_tensor(f"scores{h}", [P, N], F32)))
        O = ctx.enter_context(nc.psum_tensor("o_acc", [P, N], F32))
        P1 = ctx.enter_context(nc.psum_tensor("e_bank1", [P, 512], F32))
        P2 = ctx.enter_context(nc.psum_tensor("e_bank2", [P, 512], F32))

        qkv_loaded = two(lambda u: sem(f"qkv_loaded{u}"))
        gu_loaded = two(lambda u: sem(f"gate_up_loaded{u}"))
        d_loaded, wo_loaded, wo_high, wo_low = sem("down_loaded"), sem("w_out_loaded"), sem("w_out_high"), sem("w_out_low")
        s_full, squared = two(lambda h: sem(f"scores_full{h}")), two(lambda h: sem(f"squared{h}"))
        masked, a_ready = two(lambda h: sem(f"masked{h}")), two(lambda h: sem(f"probs_ready{h}"))
        o_copied, den_loaded = sem("o_copied"), sem("den_loaded")
        index_ready, x_gathered = sem("index_ready"), two(lambda u: sem(f"x_gathered{u}"))
        xgT_full, xgT_copied = sem("x_rowsT_full"), sem("x_rowsT_copied")
        e_gate_full, e_silu_done, e_hidden_done = sem("e_gate_full"), sem("e_silu_done"), sem("e_hidden_done")
        ehT_full, ehT_copied, ey_full, ey_ready, scattered = sem("e_hT_full"), sem("e_hT_copied"), sem("e_out_full"), sem("e_out_ready"), sem("scattered")
        rden_high, rden_low, spread, normed, on_high, on_low_done = sem("rden_high"), sem("rden_low"), sem("rden_spread"), sem("o_normed"), sem("on_high"), sem("on_low_done")
        o_full_u, o_moved_u, e_up_u = two(lambda u: sem(f"o_full{u}")), two(lambda u: sem(f"o_moved{u}")), two(lambda u: sem(f"e_up_full{u}"))
        s_ready, s_copied, s_stored = sem("s_full"), sem("s_copied"), two(lambda u: sem(f"s_stored{u}"))
        passed, made, weight_ready, rden_done, sel_ready = sem("attend_passed"), sem("made"), sem("weight_ready"), sem("rden_done"), sem("sel_ready")
        block = ctx.enter_context(nc.Block())

        NK = N // P

        def pieces(j):
            return [(P * j, 512), (512, N)] if P * j < 512 else [(P * j, N)]

        def loop(eng, pair, sequence):
            with eng.Fori(0, B) as b:
                with eng.Fori(0, PAIRS // 2) as i:
                    for u in range(2):
                        pair(b, i, u, 8 * b + 2 * i + u, 4 * b + i)
                sequence(b)

        qk_src = [dram["qT"], dram["kT"]]
        wgate = dram["w_gate"].rearrange("(q e) (p c) n -> q p e (c n)", e=2, c=C)
        wup = dram["w_up"].rearrange("(q e) (p c) n -> q p e (c n)", e=2, c=C)
        wdown = dram["w_down"].rearrange("(q e) (p c) n -> q p e (c n)", e=2, c=IC)

        @block.sync
        def _(sp):
            sp.dma_start(oT[:, :, 0:E], dram["w_out"].rearrange("(c p) n -> p c n", p=P)).then_inc(wo_loaded, 16)

            def pair(b, i, u, it, k):
                sp.wait_ge(o_full_u[u], k)
                for h in range(2):
                    row = (2 * (2 * i + u) + h) * D
                    rows = lambda src, part: src[part, bass.ds(row, D), bass.ds(b * N, N)]
                    for g, part in enumerate((0, 0, 1)):
                        sp.dma_start(qs[u][g * D:(g + 1) * D, h].bitcast(F32), rows(qk_src[0], part)).then_inc(qkv_loaded[u], 16)
                    for g, part in enumerate((0, 1, 0)):
                        sp.dma_start(ks[u][g * D:(g + 1) * D, h].bitcast(F32), rows(qk_src[1], part)).then_inc(qkv_loaded[u], 16)
                for half in range(2):
                    sp.dma_start(vs[u][:, half * TPG:(half + 1) * TPG].rearrange("p j n -> p (j n)"),
                                 dram["v"][bass.ds(2 * b + half, 1), bass.ds(2 * i + u, 1)].rearrange("a q p n -> p (a q n)")).then_inc(qkv_loaded[u], 16)
                sp.wait_ge(e_up_u[u], k)
                for dst, src in ((wg[u], wgate), (wu[u], wup)):
                    sp.dma_start(dst[:].rearrange("p e c n -> p e (c n)"),
                                 src[bass.ds(it, 1)].rearrange("a p e n -> p (a e) n")).then_inc(gu_loaded[u], 16)
                sp.wait_ge(ey_full, it)
                sp.dma_start(wd[:].rearrange("p e c n -> p e (c n)"),
                             wdown[bass.ds(it, 1)].rearrange("a p e n -> p (a e) n")).then_inc(d_loaded, 16)

            def sequence(b):
                for t in range(NK):
                    sp.wait_ge(s_copied, NK * b + t + 1)
                    sp.dma_start(dram["s"][bass.ds(b * N + t * P, P), :], s_out[t % 2][:]).then_inc(s_stored[t % 2], 16)

            loop(sp, pair, sequence)
            for u in range(2):
                sp.wait_ge(s_stored[u], 16 * NT // 2)

        @block.gpsimd
        def _(pool):
            nc.gpsimd.memset(sel_f[:], 0.0).then_inc(made, 1)
            nc.gpsimd.memset(ey[1][:], 0.0)
            nc.gpsimd.memset(den[:], 1.0).then_inc(made, 1)
            pool.wait_ge(made, 2)
            for h in range(2):
                part = sel_f[2 * HEADS * h:2 * HEADS * (h + 1)].rearrange("r c (g d) -> r c g d", d=D)
                nc.gpsimd.affine_select(out=part, in_=part, compare_op=ALU.not_equal, fill=1.0, base=0,
                                        pattern=[[-4, C], [-1, P // D], [0, D]], channel_multiplier=1).then_inc(sel_ready, 1)
                pool.wait_ge(sel_ready, h + 1)
            nc.gpsimd.iota(si[1][:].bitcast(I32), pattern=[[0, 2]], base=T, channel_multiplier=1).then_inc(made, 1)
            pool.wait_ge(made, 3)

            def gather(u, n):
                pool.wait_ge(index_ready, n)
                pool.sem_inc(passed, 1)
                nc.gpsimd.indirect_dma_start(out=xg[u][:], out_offset=None, in_=dram["xw"],
                                             in_offset=bass.IndirectOffsetOnAxis(ap=gi[u][:, 0:1], axis=0),
                                             bounds_check=T - 1).then_inc(x_gathered[u], 16)

            def scatter(u, e, n):
                pool.wait_ge(scattered, 16 * n)
                pool.sem_inc(passed, 1)
                nc.gpsimd.indirect_dma_start(out=dram["ffn"], out_offset=bass.IndirectOffsetOnAxis(ap=si[u][:, e:e + 1], axis=0),
                                             in_=ey[u][e * CAP:(e + 1) * CAP, :], in_offset=None,
                                             bounds_check=T + CAP - 1, compute_op=ALU.add).then_inc(scattered, 16)

            gather(0, 1)

            def pair(b, i, u, it, k):
                for j in range(NK):
                    for h in range(2):
                        pool.wait_ge(squared[h], NK * it + j + 1)
                        pool.sem_inc(passed, 1)
                        d = a[h][j % 2][:, j * P:(j + 1) * P]
                        nc.gpsimd.affine_select(out=d, in_=d, compare_op=ALU.is_ge, fill=0.0, base=0,
                                                pattern=[[1, P]], channel_multiplier=-1).then_inc(masked[h], 1)
                    if j == 1:
                        pool.wait_ge(ey_ready, it)
                        scatter(1 - u, 0, 2 * it)
                    if j == 4:
                        scatter(1 - u, 1, 2 * it + 1)
                    if j == 5:
                        gather(1 - u, it + 2)

            loop(pool, pair, lambda b: None)
            pool.wait_ge(ey_ready, EP)
            scatter(1, 0, 2 * EP)
            scatter(1, 1, 2 * EP + 1)
            pool.wait_ge(scattered, 16 * (2 * EP + 2))
            for u in range(2):
                pool.wait_ge(x_gathered[u], 16 * (EP // 2 + 1 - u))

        @block.scalar
        def _(act):
            act.wait_ge(wo_loaded, 16)
            nc.scalar.activation(wo_hi[:], oT[:, :, 0:E], ACT.Copy).then_inc(wo_high, 1)

            def pair(b, i, u, it, k):
                for j in range(NK):
                    for h in range(2):
                        act.wait_ge(s_full[h], NK * it + j + 1)
                        nc.scalar.activation(a[h][j % 2][:, P * j:], S[h][:, P * j:], ACT.Square).then_inc(squared[h], 1)
                    if j == 0:
                        act.wait_ge(xgT_full, it + 1)
                        nc.scalar.activation(xgT[:], P1[:].rearrange("p (c t) -> p c t", c=C), ACT.Copy).then_inc(xgT_copied, 1)
                    if j == 5:
                        act.wait_ge(e_gate_full, it + 1)
                        nc.scalar.activation(esg[:], P1[:, 0:I], ACT.Silu).then_inc(e_silu_done, 1)
                    if j == 6:
                        act.wait_ge(ehT_full, it + 1)
                        nc.scalar.activation(ehT[:], P1[:, 0:IC * P].rearrange("p (c t) -> p c t", c=IC), ACT.Copy).then_inc(ehT_copied, 1)
                act.wait_ge(o_full_u[u], k + 1)
                act.wait_ge(o_moved_u[u], 64 * k)
                nc.scalar.activation(o_raw[u][0:VW], O[0:VW], ACT.Copy)
                nc.scalar.activation(o_raw[u][64:64 + VW], O[64:64 + VW], ACT.Copy).then_inc(o_copied, 1)
                act.wait_ge(o_copied, it + 1)
                if u == 0:
                    act.wait_ge(on_low_done, 2 * C * b)
                    act.wait_ge(wo_low, 1)
                for h in range(2):
                    r = 2 * u + h
                    act.dma_start(oT[r * D:(r + 1) * D, bass.ds(i, 1)].rearrange("p a n -> p (a n)"),
                                  o_raw[u][64 * h:64 * h + D]).then_inc(o_moved_u[u], 16)
                    act.dma_start(dram["den"][bass.ds(b, 1), bass.ds(4 * i + r, 1)].rearrange("a h n -> (a h) n"),
                                  o_raw[u][64 * h + D:64 * h + VW]).then_inc(o_moved_u[u], 16)

            def sequence(b):
                for u in range(2):
                    act.wait_ge(o_moved_u[u], 64 * 4 * (b + 1))
                act.wait_ge(rden_done, b)
                act.dma_start(den[0:HEADS], dram["den"][bass.ds(b, 1)].rearrange("a h n -> (a h) n")).then_inc(den_loaded, 16)
                act.wait_ge(rden_done, b + 1)
                nc.scalar.activation(rden_parts[0:2 * HEADS], rden[:], ACT.Copy).then_inc(rden_high, 1)
                for half in range(2):
                    for c in range(C):
                        n = 2 * C * b + C * half + c
                        act.wait_ge(normed, n + 1)
                        if half == 1 and c == 0:
                            act.wait_ge(s_ready, NK * b + TPG)
                        nc.scalar.activation(on_hi[:, c], oT[:, c, 512 * half:512 * (half + 1)], ACT.Copy).then_inc(on_high, 1)
                    for t in range(TPG):
                        m = TPG * half + t
                        act.wait_ge(s_ready, NK * b + m + 1)
                        act.wait_ge(s_stored[m % 2], 16 * (TPG * b + m // 2))
                        nc.scalar.activation(s_out[m % 2][:], S[1][:, 512 * (m % 2):512 * (m % 2) + 512], ACT.Copy).then_inc(s_copied, 1)

            loop(act, pair, sequence)
            for u in range(2):
                act.wait_ge(o_moved_u[u], 64 * EP // 2)

        @block.vector
        def _(dve):
            dve.wait_ge(wo_high, 1)
            nc.vector.tensor_tensor(wo_lo[:], oT[:, :, 0:E], wo_hi[:].bitcast(F32), ALU.subtract).then_inc(wo_low, 1)
            dve.wait_ge(sel_ready, 2)
            nc.vector.tensor_copy(sel[:], sel_f[:])
            nc.vector.tensor_copy(gi[0][:], w["gather_from"][:, 0:1]).then_inc(index_ready, 1)

            def pair(b, i, u, it, k):
                for j in range(NK):
                    for h in range(2):
                        dve.wait_ge(masked[h], NK * it + j + 1)
                        part = a[h][j % 2][:, P * j:]
                        nc.vector.tensor_tensor(part, part, part, ALU.mult).then_inc(a_ready[h], 1)
                    if j == 2:
                        dve.wait_ge(x_gathered[u], 16 * (k + 1))
                        dve.wait_ge(scattered, 16 * 2 * it)
                        nc.vector.tensor_copy(si[u][:], w["scatter_to"][:, bass.ds(2 * it, 2)])
                        for h in range(2):
                            part = slice(h * CAP, (h + 1) * CAP)
                            last = nc.vector.tensor_copy(wt[u][part, :], xg[u][part, bass.ds(2 * it + E + h, 1)])
                        last.then_inc(weight_ready, 1)
                        dve.wait_ge(x_gathered[1 - u], 16 * (k + u))
                        nc.vector.tensor_copy(gi[1 - u][:], w["gather_from"][:, bass.ds(it + 1, 1)]).then_inc(index_ready, 1)
                    if j == 5:
                        dve.wait_ge(e_silu_done, it + 1)
                        dve.wait_ge(e_up_u[u], k + 1)
                        dve.wait_ge(ehT_full, it)
                        nc.vector.tensor_tensor(eh[:], esg[:], P2[:, 0:I], ALU.mult).then_inc(e_hidden_done, 1)
                dve.wait_ge(ey_full, it + 1)
                dve.wait_ge(scattered, 16 * 2 * it)
                dve.wait_ge(weight_ready, it + 1)
                nc.vector.tensor_scalar(ey[u][:], P2[:], wt[u][:, 0:1], None, ALU.mult).then_inc(ey_ready, 1)

            def sequence(b):
                dve.wait_ge(den_loaded, 16 * (b + 1))
                dve.wait_ge(rden_high, b)
                nc.vector.reciprocal(rden[:], den[:]).then_inc(rden_done, 1)
                dve.wait_ge(rden_high, b + 1)
                nc.vector.tensor_tensor(rden_parts[2 * HEADS:], rden[:], rden_parts[0:2 * HEADS].bitcast(F32),
                                        ALU.subtract).then_inc(rden_low, 1)
                for half in range(2):
                    for c in range(C):
                        n = 2 * C * b + C * half + c
                        dve.wait_ge(spread, n + 1)
                        part = oT[:, c, 512 * half:512 * (half + 1)]
                        nc.vector.tensor_tensor(part, part, S[0][:, 512 * (c % 2):512 * (c % 2) + 512], ALU.mult).then_inc(normed, 1)
                        dve.wait_ge(on_high, n + 1)
                        nc.vector.tensor_tensor(on_lo[:, c], part, on_hi[:, c].bitcast(F32), ALU.subtract).then_inc(on_low_done, 1)

            loop(dve, pair, sequence)

        @block.tensor
        def _(pe):
            pe.wait_ge(wo_low, 1)

            def scores(u, it, j, b, i, k):
                for h in range(2):
                    pe.wait_ge(squared[h], NK * it + j)
                    if j == 0 and u == 0:
                        pe.wait_ge(s_copied, NK * b)
                        pe.wait_ge(on_low_done, 2 * C * b)
                    for n0, n1 in pieces(j):
                        last = nc.tensor.matmul(S[h][:, n0:n1], ks[u][:, h, P * j:P * (j + 1)], qs[u][:, h, n0:n1], start=True, stop=True)
                    last.then_inc(s_full[h], 1)

            def values(u, it, j, k):
                for h in range(2):
                    pe.wait_ge(a_ready[h], NK * it + j + 1)
                if j == 0:
                    pe.wait_ge(o_copied, it)
                for n0, n1 in pieces(j):
                    for h in range(2):
                        last = nc.tensor.matmul(O[64 * h:64 * h + VW, n0:n1], vs[u][:, j, VW * h:VW * (h + 1)],
                                                a[h][j % 2][:, n0:n1], start=(j == 0), stop=(j == (3 if n0 < 512 else 7)))
                if j == NK - 1:
                    last.then_inc(o_full_u[u], 1)

            def expert(u, it, j, k):
                if j == 0:
                    pe.wait_ge(x_gathered[u], 16 * (k + 1))
                    pe.wait_ge(ehT_copied, it)
                    for c in range(C):
                        last = nc.tensor.transpose(P1[:, c * P:(c + 1) * P], xg[u][:, c:E:C], w["ident"][:])
                    last.then_inc(xgT_full, 1)
                elif j <= C:
                    c = j - 1
                    if c == 0:
                        pe.wait_ge(gu_loaded[u], 32 * (k + 1))
                        pe.wait_ge(xgT_copied, it + 1)
                        pe.wait_ge(ey_ready, it)
                    for out, wts, full in ((P1, wg[u], e_gate_full), (P2, wu[u], e_up_u[u])):
                        for h in range(2):
                            t = slice(h * CAP, (h + 1) * CAP)
                            last = nc.tensor.matmul(out[t, 0:I], xgT[:, c, t], wts[:, h, c], start=(c == 0), stop=(c == C - 1))
                        if c == C - 1:
                            last.then_inc(full, 1)
                elif j == 6:
                    pe.wait_ge(e_hidden_done, it + 1)
                    for c in range(IC):
                        last = nc.tensor.transpose(P1[:, c * P:(c + 1) * P], eh[:, c:I:IC], w["ident"][:])
                    last.then_inc(ehT_full, 1)
                elif j == 7:
                    pe.wait_ge(ehT_copied, it + 1)
                    pe.wait_ge(d_loaded, 16 * (it + 1))
                    for c in range(IC):
                        for h in range(2):
                            t = slice(h * CAP, (h + 1) * CAP)
                            last = nc.tensor.matmul(P2[t, :], ehT[:, c, t], wd[:, h, c], start=(c == 0), stop=(c == IC - 1))
                    last.then_inc(ey_full, 1)

            def pair(b, i, u, it, k):
                pe.wait_ge(qkv_loaded[u], 14 * 16 * (k + 1))
                for j in range(NK):
                    scores(u, it, j, b, i, k)
                    expert(u, it, j, k)
                    if j:
                        values(u, it, j - 1, k)
                values(u, it, NK - 1, k)

            def sequence(b):
                pe.wait_ge(rden_low, b + 1)
                for h in range(2):
                    pe.wait_ge(squared[h], NK * PAIRS * (b + 1))
                for half in range(2):
                    for c in range(C):
                        n = 2 * C * b + C * half + c
                        if c >= 2 or half:
                            pe.wait_ge(normed, n - 1)
                        nc.tensor.matmul(S[0][:, 512 * (c % 2):512 * (c % 2) + 512], sel[:, c], rden_parts[:, 512 * half:512 * (half + 1)],
                                         start=True, stop=True).then_inc(spread, 1)
                    pe.wait_ge(on_low_done, 2 * C * b + C * (half + 1))
                    for t in range(TPG):
                        m = TPG * half + t
                        if m >= 2:
                            pe.wait_ge(s_copied, NK * b + m - 1)
                        out = S[1][:, 512 * (m % 2):512 * (m % 2) + 512]
                        tok = slice(t * P, (t + 1) * P)
                        for c in range(C):
                            nc.tensor.matmul(out, on_hi[:, c, tok], wo_hi[:, c], start=(c == 0), stop=False)
                            nc.tensor.matmul(out, on_hi[:, c, tok], wo_lo[:, c], start=False, stop=False)
                            last = nc.tensor.matmul(out, on_lo[:, c, tok], wo_hi[:, c], start=False, stop=(c == C - 1))
                        last.then_inc(s_ready, 1)

            loop(pe, pair, sequence)


def combine(nc, dram, w):
    W2 = 2
    with ExitStack() as ctx:
        sb = lambda name, shape, dt=F32: ctx.enter_context(nc.sbuf_tensor(name, shape, dt))
        sem = lambda name: ctx.enter_context(nc.semaphore(name))
        two = lambda f: [f(0), f(1)]
        xt, st, ft, yt = (two(lambda u: sb(f"c_{n}{u}", [P, W2, E])) for n in ("x", "s", "ffn", "out"))
        loaded, stored = two(lambda u: sem(f"c_loaded{u}")), two(lambda u: sem(f"c_stored{u}"))
        gated, product, done_u = sem("c_gated"), sem("c_product"), two(lambda u: sem(f"c_done{u}"))
        block = ctx.enter_context(nc.Block())
        view = lambda name: dram[name][0:T, :].rearrange("(q p w) e -> q p w e", p=P, w=W2)
        STEPS = NT // W2

        def steps(eng, body):
            with eng.Fori(0, STEPS // 2) as i:
                for u in range(2):
                    body(i, u, 2 * i + u)

        @block.sync
        def _(sp):
            def body(i, u, n):
                sp.wait_ge(done_u[u], i)
                for dst, name in ((ft, "ffn"), (st, "s"), (xt, "x")):
                    sp.dma_start(dst[u][:], view(name)[bass.ds(n, 1)].rearrange("a p w e -> p (a w) e")).then_inc(loaded[u], 16)
            steps(sp, body)

        @block.scalar
        def _(act):
            def body(i, u, n):
                act.wait_ge(loaded[u], 48 * (i + 1))
                nc.scalar.activation(ft[u][:], ft[u][:], ACT.Silu).then_inc(gated, 1)
            steps(act, body)

        @block.vector
        def _(dve):
            def body(i, u, n):
                dve.wait_ge(gated, n + 1)
                nc.vector.tensor_tensor(st[u][:], st[u][:], ft[u][:], ALU.mult).then_inc(product, 1)
                dve.wait_ge(product, n + 1)
                dve.wait_ge(stored[u], 16 * i)
                nc.vector.tensor_tensor(yt[u][:], st[u][:], xt[u][:], ALU.add).then_inc(done_u[u], 1)
            steps(dve, body)

        @block.gpsimd
        def _(pool):
            def body(i, u, n):
                pool.wait_ge(done_u[u], i + 1)
                pool.dma_start(view("out")[bass.ds(n, 1)].rearrange("a p w e -> p (a w) e"), yt[u][:]).then_inc(stored[u], 16)
            steps(pool, body)
            for u in range(2):
                pool.wait_ge(stored[u], 16 * STEPS // 2)


def build(nc, x, w_qkv, w_out, ln_scale, ln_bias, w_router, w_gate, w_up, w_down, w_sh_gate, w_sh_up, w_sh_down, out, upto=9):
    cos, sin = rope_tables()
    scratch = lambda name, shape: nc.dram_tensor(name, shape, F32, kind="Internal").ap()
    dram = {
        "x": x.rearrange("b n e -> (b n) e"), "out": out.rearrange("b n e -> (b n) e"),
        "w_qkv": w_qkv, "w_out": w_out, "ln_scale": ln_scale, "ln_bias": ln_bias,
        "router": w_router, "w_gate": w_gate, "w_up": w_up, "w_down": w_down,
        "w_sh_gate": w_sh_gate, "w_sh_up": w_sh_up, "w_sh_down": w_sh_down,
        "cos": nc.inline_tensor(cos, "rope_cos").ap(), "sin": nc.inline_tensor(sin, "rope_sin").ap(),
        "xw": scratch("xw_rows", [T, XW]),
        "ffn": scratch("ffn_rows", [T + CAP, E]),
        "qT": scratch("qT_parts", [2, E, T]), "kT": scratch("kT_parts", [2, E, T]),
        "v": scratch("v_parts", [G, PAIRS, P, TPG * 2 * VW]),
        "den": scratch("denominators", [B, HEADS, N]), "s": scratch("attention_out", [T, E]),
    }
    with ExitStack() as keep:
        sb = lambda stack, name, shape, dt=F32: stack.enter_context(nc.sbuf_tensor(name, shape, dt))
        w = {"ident": sb(keep, "ident", [P, P]), "gather_from": sb(keep, "gather_from", [P, NE // 2 + 1], U32),
             "scatter_to": sb(keep, "scatter_to", [CAP, NE], U32)}
        with ExitStack() as marks:
            w |= {"mask": sb(marks, "mask", [P, NT, NE]), "ldiff": sb(marks, "ldiff", [P, NT, NE])}
            with ExitStack() as ctx:
                for k, n in (("qkv", C * 3 * E), ("gu", C * 2 * I), ("down", IC * E), ("router", C * NE)):
                    w[k + "_hi"], w[k + "_lo"] = sb(ctx, k + "_hi", [P, n], F32R), sb(ctx, k + "_lo", [P, n], F32R)
                w |= {"cos": sb(ctx, "cos", [P, NT, D]), "sin": sb(ctx, "sin", [P, NT, D]),
                      "ln_scale": sb(ctx, "ln_scale_col", [P, 1]), "ln_bias": sb(ctx, "ln_bias_col", [P, 1]),
                      "expert_i": sb(ctx, "expert_i", [P, NE], I32), "expert": sb(ctx, "expert", [P, NE]),
                      "minus_half": sb(ctx, "minus_half", [P, 2 * HEADS])}
                split_weights(nc, dram, w)
                project(nc, dram, w)
            if upto > 1:
                list_tokens(nc, dram, w)
        if upto > 2:
            attend(nc, dram, w)
        if upto > 3:
            combine(nc, dram, w)


_INS = ["L0_attn_x", "L0_attn_w_qkv", "L0_attn_w_out", "L0_attn_ln_scale", "L0_attn_ln_bias", "L0_ffn_w_router",
        "L0_ffn_w_gate", "L0_ffn_w_up", "L0_ffn_w_down", "L0_ffn_w_sh_gate", "L0_ffn_w_sh_up", "L0_ffn_w_sh_down"]


def kernel(**inputs):
    import numpy as _np
    import concourse.bacc as _bacc
    from concourse.bass_utils import run_bass_kernel_spmd as _run

    nc = _bacc.Bacc("TRN2", target_bir_lowering=False, num_devices=1)
    arrays, args = {}, []
    for name in _INS:
        a = _np.ascontiguousarray(inputs[name].T if name == "L0_ffn_w_router" else inputs[name])
        arrays[f"in_{name}"] = a
        args.append(nc.dram_tensor(f"in_{name}", a.shape, mybir.dt.from_np(a.dtype), kind="ExternalInput").ap())
    args.append(nc.dram_tensor("out_0", (B, N, E), F32, kind="ExternalOutput").ap())
    build(nc, *args)
    r = _run(nc, [arrays], core_ids=[0])
    return r.results[0]["out_0"]
```

```python
import numpy as np
import concourse.bass as bass
from concourse import mybir
from contextlib import ExitStack

F32 = mybir.dt.float32
F32R = mybir.dt.float32r
U32 = mybir.dt.uint32
I32 = mybir.dt.int32
ALU = mybir.AluOpType
ACT = mybir.ActivationFunctionType
AX = mybir.AxisListType

P = 128
B, N, E = 4, 1024, 512
T = B * N
HEADS = 16
D = E // HEADS
C = E // P
GT = 512
TPG = GT // P
G = T // GT
NT = T // P
PAIRS = HEADS // 2
VW = D + 1
NE, TOPK, CAP = 64, 4, 64
I = 384
IC = I // P
XW = E + NE
EPS = 1e-5
NEVER = 3e38
ONE = 1


class Links:

    def __init__(self, eng, sem, base, passed):
        self.eng, self.sem, self.base, self.passed, self.n = eng, sem, base, passed, 0

    def __call__(self, ins, apart=False):
        self.n += 1
        ins.then_inc(self.sem, 1)
        self.eng.wait_ge(self.sem, self.base + self.n)
        if apart:
            self.eng.sem_inc(self.passed, 1)




def start_at_one(nc, sems):
    with nc.Block() as block:
        @block.sync
        def _(sp):
            for s in sems:
                sp.sem_inc(s, ONE)


def rope_tables():
    inv = (np.float32(1.0) / np.float32(10000.0) ** (np.arange(0, D, 2, dtype=np.float32) / np.float32(D))).astype(np.float32)
    t = (np.arange(N, dtype=np.float32)[:, None] * inv[None, :]).astype(np.float32)
    c, s = np.cos(t.astype(np.float64)), np.sin(t.astype(np.float64))
    cc = np.concatenate([c, c], 1).astype(np.float32)
    ss = np.concatenate([-s, s], 1).astype(np.float32)

    def lay(a):
        return np.ascontiguousarray(a.reshape(N // P, P, D).transpose(1, 0, 2))

    return lay(cc), lay(ss)


def split_weights(nc, dram, w):
    parts = [("qkv", C * 3 * E), ("gu", C * 2 * I), ("down", IC * E), ("router", C * NE)]
    with ExitStack() as ctx:
        full = {k: ctx.enter_context(nc.sbuf_tensor(f"full_{k}", [P, n], F32)) for k, n in parts}
        loaded = {k: ctx.enter_context(nc.semaphore(f"w_loaded_{k}")) for k, _ in parts}
        high_done = ctx.enter_context(nc.semaphore("w_high_done"))
        tables = ctx.enter_context(nc.semaphore("tables_loaded"))
        made = ctx.enter_context(nc.semaphore("constants_made"))
        block = ctx.enter_context(nc.Block())

        @block.sync
        def _(sp):
            sp.dma_start(full["qkv"][:].rearrange("p (c n) -> p c n", c=C),
                         dram["w_qkv"].rearrange("(c p) n -> p c n", p=P)).then_inc(loaded["qkv"], 16)
            gu = full["gu"][:].rearrange("p (c two n) -> p c two n", c=C, two=2)
            sp.dma_start(gu[:, :, 0, :], dram["w_sh_gate"].rearrange("(c p) n -> p c n", p=P)).then_inc(loaded["gu"], 16)
            sp.dma_start(gu[:, :, 1, :], dram["w_sh_up"].rearrange("(c p) n -> p c n", p=P)).then_inc(loaded["gu"], 16)
            sp.dma_start(full["down"][:].rearrange("p (c n) -> p c n", c=IC),
                         dram["w_sh_down"].rearrange("(c p) n -> p c n", p=P)).then_inc(loaded["down"], 16)
            sp.dma_start(full["router"][:].rearrange("p (c n) -> p c n", c=C), dram["router"].rearrange("(c p) n -> p c n", p=P)).then_inc(loaded["router"], 16)
            sp.dma_start(w["cos"][:], dram["cos"]).then_inc(tables, 16)
            sp.dma_start(w["sin"][:], dram["sin"]).then_inc(tables, 16)
            for r in range(P // D):
                sp.dma_start(w["ln_scale"][r * D:(r + 1) * D, :], dram["ln_scale"].rearrange("(d a) -> d a", a=1)).then_inc(tables, 16)
                sp.dma_start(w["ln_bias"][r * D:(r + 1) * D, :], dram["ln_bias"].rearrange("(d a) -> d a", a=1)).then_inc(tables, 16)
            sp.wait_ge(tables, 16 * (2 + 2 * P // D))

        @block.scalar
        def _(act):
            for k, _n in parts:
                act.wait_ge(loaded[k], 32 if k == "gu" else 16)
                nc.scalar.activation(w[k + "_hi"][:], full[k][:], ACT.Copy).then_inc(high_done, 1)

        @block.vector
        def _(dve):
            for i, (k, _n) in enumerate(parts):
                dve.wait_ge(high_done, i + 1)
                nc.vector.tensor_tensor(w[k + "_lo"][:], full[k][:], w[k + "_hi"][:].bitcast(F32), ALU.subtract)

        @block.gpsimd
        def _(pool):
            nc.gpsimd.memset(w["ident"][:], 0.0).then_inc(made, 1)
            pool.wait_ge(made, 1)
            nc.gpsimd.affine_select(out=w["ident"][:], in_=w["ident"][:], compare_op=ALU.not_equal, fill=1.0,
                                    base=0, pattern=[[-1, P]], channel_multiplier=1)
            nc.gpsimd.memset(w["minus_half"][:], -0.5)


def project(nc, dram, w):
    with ExitStack() as ctx:
        sb = lambda name, shape, dt=F32: ctx.enter_context(nc.sbuf_tensor(name, shape, dt))
        sems = []

        def sem(name):
            sems.append(ctx.enter_context(nc.semaphore(name)))
            return sems[-1]


        bank = lambda name: ctx.enter_context(nc.psum_tensor(name, [P, 512], F32))

        x = sb("x_group", [P, TPG, E])
        stats = sb("x_stats", [P, TPG, 6])
        mv = sb("x_mean_var", [P, TPG, 2])
        xvar = sb("x_var", [P, TPG])
        xrstd = sb("x_rstd", [P, TPG])
        xT_hi = sb("xT_hi", [P, C, GT], F32R)
        xT_lo = sb("xT_lo", [P, C, GT], F32R)
        rope = sb("rope_a", [P, 2 * E])
        rope_b = sb("rope_b", [P, 2 * E])
        cen = sb("centred", [P, 2 * E])
        y = sb("qk_normed", [P, 2 * E])
        hsum = sb("head_sum", [P, 2 * HEADS])
        hmean = sb("head_mean", [P, 2 * HEADS])
        hvar = sb("head_var", [P, 2 * HEADS])
        hrstd = sb("head_rstd", [P, 2 * HEADS])
        qkT = sb("qkT_full", [P, 2, C, P])
        qkT_hi = [sb(f"qkT_hi{u}", [P, 2, C, P], F32R) for u in range(2)]
        qkT_lo = [sb(f"qkT_lo{u}", [P, 2, C, P], F32R) for u in range(2)]
        v = sb("v_group", [P, PAIRS, TPG, 2, VW])
        sg = sb("sh_silu", [P, GT])
        hf = sb("sh_hidden", [P, GT])
        hT_hi = sb("sh_hT_hi", [P, IC, GT], F32R)
        hT_lo = sb("sh_hT_lo", [P, IC, GT], F32R)
        ffn = sb("sh_out", [P, TPG, E])
        lgT = sb("logitsT", [NE, GT])
        lg = sb("logits", [P, TPG, NE])
        top = sb("top8", [P, TPG, 8])
        unmarked = sb("logits_unmarked", [P, TPG, NE])
        xneg = sb("x_minus_mean", [P, TPG])
        xbias = sb("x_bias", [P, TPG])

        TR = [bank("tr0"), bank("tr1")]
        QK = ctx.enter_context(nc.psum_tensor("qk", [P, 2 * E], F32))
        V = bank("v")
        GATE, UP, DN = bank("gate"), bank("up"), bank("down")
        DOWN = [DN, GATE, UP, DN]

        x_loaded, x_stored, x_transposed = sem("x_loaded"), sem("x_stored"), sem("x_transposed")
        var_ready, rstd_ready, bias_ready, xn_ready = sem("x_var_ready"), sem("x_rstd_ready"), sem("x_bias_ready"), sem("xn_ready")
        xT_high, xT_low = sem("xT_high"), sem("xT_low")
        qk_full, v_full, v_copied, v_stored, v_ones = sem("qk_full"), sem("v_full"), sem("v_copied"), sem("v_stored"), sem("v_ones")
        rope_parts, roped, centred, squared = sem("rope_parts"), sem("roped"), sem("centred"), sem("squared")
        hvar_ready, hrstd_ready, y_ready = sem("hvar_ready"), sem("hrstd_ready"), sem("y_ready")
        q_transposed, k_transposed = sem("q_transposed"), sem("k_transposed")
        q_copied, k_copied = sem("q_copied"), sem("k_copied")
        qkT_high, qkT_low, qkT_stored = sem("qkT_high"), sem("qkT_low"), [sem("qkT_stored0"), sem("qkT_stored1")]
        gate_full, up_full = sem("gate_full"), sem("up_full")
        silu_done, hidden_done, hidden_high, hidden_low = sem("silu_done"), sem("hidden_done"), sem("hidden_high"), sem("hidden_low")
        down_full, ffn_copied = sem("down_full"), sem("ffn_copied")
        ffn_stored = sem("ffn_stored")
        logitsT_full, logitsT_copied = sem("logitsT_full"), sem("logitsT_copied")
        logits_full, logits_copied = sem("logits_full"), sem("logits_copied")
        dve_order, passed = sem("dve_order"), sem("passed")

        x_dram = dram["x"].rearrange("(g j p) e -> g p j e", p=P, j=TPG)
        xw_dram = dram["xw"].rearrange("(g j p) e -> g p j e", p=P, j=TPG)
        ffn_dram = dram["ffn"][0:T, :].rearrange("(g j p) e -> g p j e", p=P, j=TPG)
        qk_dram = [[dram[s][h].rearrange("(c p) n -> p c n", p=P) for h in range(2)] for s in ("qT", "kT")]

        start_at_one(nc, sems)
        block = ctx.enter_context(nc.Block())

        def groups(eng, first, body):
            first()
            with eng.Fori(0, G - 1) as g:
                body(g, True)
            body(G - 1, False)

        @block.sync
        def _(sp):
            def load_x(g):
                sp.dma_start(x[:], x_dram[bass.ds(g, 1)].rearrange("a p j e -> p (a j) e")).then_inc(x_loaded, 16)

            def store_xn(g):
                sp.wait_ge(xn_ready, ONE + g + 1)
                sp.dma_start(xw_dram[bass.ds(g, 1)].rearrange("a p j e -> p (a j) e")[:, :, 0:E], x[:]).then_inc(x_stored, 16)

            def store_qk(g, j):
                n = TPG * g + j
                sp.wait_ge(qkT_high, ONE + n + 1)
                sp.wait_ge(qkT_low, ONE + n + 1)
                for s in range(2):
                    for h, src in enumerate((qkT_hi, qkT_lo)):
                        sp.dma_start(qk_dram[s][h][:, :, bass.ds(n * P, P)], src[j % 2][:, s].bitcast(F32)).then_inc(qkT_stored[j % 2], 16)

            def body(g, has_next):
                if has_next:
                    sp.wait_ge(x_transposed, ONE + C * (g + 1))
                    sp.sem_inc(passed, 1)
                    sp.wait_ge(x_stored, ONE + 16 * (g + 1))
                    sp.sem_inc(passed, 1)
                    load_x(g + 1)
                store_qk(g, 0)
                store_qk(g, 1)
                if has_next:
                    store_xn(g + 1)
                sp.wait_ge(v_copied, ONE + TPG * (g + 1))
                sp.dma_start(dram["v"][bass.ds(g, 1)].rearrange("a q p n -> p (a q) n"),
                             v[:].rearrange("p q j h d -> p q (j h d)")).then_inc(v_stored, 16)
                store_qk(g, 2)
                sp.wait_ge(ffn_copied, ONE + TPG * (g + 1))
                sp.dma_start(ffn_dram[bass.ds(g, 1)].rearrange("a p j e -> p (a j) e"), ffn[:]).then_inc(ffn_stored, 16)
                store_qk(g, 3)

            def first():
                load_x(0)
                store_xn(0)

            groups(sp, first, body)
            sp.wait_ge(x_stored, ONE + 16 * G)
            for stored in qkT_stored:
                sp.wait_ge(stored, ONE + 16 * 4 * NT // 2)
            sp.wait_ge(v_stored, ONE + 16 * G)
            sp.wait_ge(ffn_stored, ONE + 16 * G)

        @block.gpsimd
        def _(pool):
            nc.gpsimd.memset(v[:], 1.0).then_inc(v_ones, 1)

            def x_rstd(g):
                pool.wait_ge(var_ready, ONE + g + 1)
                nc.gpsimd.tensor_tensor(xrstd[:], xvar[:], w["minus_half"][:, 0:TPG], ALU.pow).then_inc(rstd_ready, 1)
                pool.wait_ge(rstd_ready, ONE + g + 1)
                nc.gpsimd.tensor_tensor(xbias[:], xneg[:], xrstd[:], ALU.mult).then_inc(bias_ready, 1)

            def hidden_rest(g, j):
                pool.wait_ge(hidden_high, ONE + IC * g + j + 1)
                nc.gpsimd.tensor_tensor(hT_lo[:, j], hf[:], hT_hi[:, j].bitcast(F32), ALU.subtract).then_inc(hidden_low, 1)

            def body(g, has_next):
                for j in range(TPG):
                    n = TPG * g + j
                    pool.wait_ge(rope_parts, ONE + n + 1)
                    nc.gpsimd.tensor_tensor(rope[:], rope[:], rope_b[:], ALU.add).then_inc(roped, 1)
                    if j >= 1:
                        hidden_rest(g, j - 1)
                    pool.wait_ge(hvar_ready, ONE + n + 1)
                    nc.gpsimd.tensor_tensor(hrstd[:], hvar[:], w["minus_half"][:], ALU.pow).then_inc(hrstd_ready, 1)
                    if j == 2 and has_next:
                        x_rstd(g + 1)

            groups(pool, lambda: x_rstd(0), body)

        @block.scalar
        def _(act):
            def x_norm(g):
                act.wait_ge(bias_ready, ONE + g + 1)
                for j in range(TPG):
                    last = nc.scalar.activation(x[:, j], x[:, j], ACT.Identity, scale=xrstd[:, j:j + 1], bias=xbias[:, j:j + 1])
                last.then_inc(xn_ready, 1)

            def x_high(g, chunks):
                act.wait_ge(v_full, ONE + TPG * g)
                for c in chunks:
                    act.wait_ge(x_transposed, ONE + C * g + c + 1)
                    nc.scalar.activation(xT_hi[:, c], TR[c % 2][:], ACT.Copy).then_inc(xT_high, 1)

            def copy_logitsT(g):
                act.wait_ge(logitsT_full, ONE + g + 1)
                act.wait_ge(logits_full, ONE + g)
                nc.scalar.activation(lgT[:], TR[0][0:NE, :], ACT.Copy).then_inc(logitsT_copied, 1)

            def qk_out(g, j):
                n = TPG * g + j
                act.wait_ge(qkT_low, ONE + n)
                for s, full, copied in ((1, k_transposed, k_copied), (0, q_transposed, q_copied)):
                    act.wait_ge(full, ONE + n + 1)
                    nc.scalar.activation(qkT[:, s], TR[s][:].rearrange("p (c t) -> p c t", c=C), ACT.Identity,
                                         scale=w["ln_scale"][:, 0:1], bias=w["ln_bias"][:, 0:1]).then_inc(copied, 1)
                act.wait_ge(q_copied, ONE + n + 1)
                act.wait_ge(k_copied, ONE + n + 1)
                act.wait_ge(qkT_stored[j % 2], ONE + 16 * 4 * (2 * g + j // 2))
                nc.scalar.activation(qkT_hi[j % 2][:], qkT[:], ACT.Copy).then_inc(qkT_high, 1)

            def copy_out(g, j):
                act.wait_ge(down_full, ONE + TPG * g + j + 1)
                if j == 0:
                    act.wait_ge(ffn_stored, ONE + 16 * g)
                nc.scalar.activation(ffn[:, j], DOWN[j][:], ACT.Copy).then_inc(ffn_copied, 1)

            def body(g, has_next):
                for j in range(TPG):
                    n, m = TPG * g + j, IC * g + j
                    act.wait_ge(v_full, ONE + n + 1)
                    if j == 0:
                        act.wait_ge(v_ones, ONE + 1)
                        act.wait_ge(v_stored, ONE + 16 * g)
                    nc.scalar.activation(v[:, :, j, :, 0:D], V[:].rearrange("p (q h d) -> p q h d", q=PAIRS, h=2),
                                         ACT.Copy).then_inc(v_copied, 1)
                    if j < IC:
                        act.wait_ge(gate_full, ONE + m + 1)
                        act.wait_ge(hidden_done, ONE + m)
                        nc.scalar.activation(sg[:], GATE[:], ACT.Silu).then_inc(silu_done, 1)
                    else:
                        if has_next:
                            x_norm(g + 1)
                        qk_out(g, 2)
                    act.wait_ge(centred, ONE + n + 1)
                    nc.scalar.activation(rope_b[:], cen[:], ACT.Square).then_inc(squared, 1)
                    if j < IC:
                        act.wait_ge(hidden_done, ONE + m + 1)
                        act.wait_ge(down_full, ONE + TPG * g)
                        nc.scalar.activation(hT_hi[:, j], hf[:], ACT.Copy).then_inc(hidden_high, 1)
                        if j >= 1:
                            qk_out(g, j - 1)
                copy_out(g, 0)
                if has_next:
                    x_high(g + 1, (0, 1))
                copy_out(g, 1)
                copy_out(g, 2)
                if has_next:
                    x_high(g + 1, (2, 3))
                copy_out(g, 3)
                if has_next:
                    copy_logitsT(g + 1)
                qk_out(g, 3)

            def first():
                x_norm(0)
                x_high(0, range(C))
                copy_logitsT(0)

            groups(act, first, body)

        @block.vector
        def _(dve):
            def x_stats(g, tiles, link):
                for j in tiles:
                    if j == 0:
                        dve.wait_ge(x_loaded, ONE + 16 * (g + 1))
                    link(nc.vector.bn_stats(stats[:, j], x[:, j]), apart=True)
                    link(nc.vector.bn_aggr(mv[:, j], stats[:, j]))
                if 3 in tiles:
                    nc.vector.tensor_scalar(xneg[:], mv[:, :, 0], -1.0, None, ALU.mult)
                    nc.vector.tensor_scalar(xvar[:], mv[:, :, 1], EPS, None, ALU.add).then_inc(var_ready, 1)

            def x_low(g, chunks):
                for c in chunks:
                    dve.wait_ge(xT_high, ONE + C * g + c + 1)
                    nc.vector.tensor_tensor(xT_lo[:, c], TR[c % 2][:], xT_hi[:, c].bitcast(F32),
                                            ALU.subtract).then_inc(xT_low, 1)

            def route(g, link):
                dve.wait_ge(logits_full, ONE + g + 1)
                nc.vector.tensor_copy(lg[:], TR[1][:, 0:TPG * NE].rearrange("p (j n) -> p j n", j=TPG)).then_inc(logits_copied, 1)
                dve.wait_ge(logits_copied, ONE + g + 1)
                dve.sem_inc(passed, 1)
                for j in range(TPG):
                    last = nc.vector.max(top[:, j], lg[:, j])
                link(last)
                link(nc.vector.memset(top[:, :, TOPK:], NEVER), apart=True)
                for j in range(TPG):
                    last = nc.vector.match_replace(out=unmarked[:, j], in_to_replace=top[:, j], in_values=lg[:, j], imm_value=-NEVER)
                link(last)
                nc.vector.tensor_tensor(w["mask"][:, bass.ds(TPG * g, TPG), :], unmarked[:], lg[:], ALU.not_equal)
                nc.vector.tensor_tensor(w["ldiff"][:, bass.ds(TPG * g, TPG), :], lg[:],
                                        top[:, :, 0:1].broadcast_to([P, TPG, NE]), ALU.subtract)

            heads = lambda t: t[:].rearrange("p (h d) -> p h d", d=D)
            wide = lambda t: t[:].unsqueeze(2).broadcast_to([P, 2 * HEADS, D])
            half = D // 2

            def rotate(g, j):
                n = TPG * g + j
                dve.wait_ge(qk_full, ONE + n + 1)
                place = bass.ds(n % (N // P), 1)
                cos = w["cos"][:, place, :].broadcast_to([P, 2 * HEADS, D])
                sin = w["sin"][:, place, :].broadcast_to([P, 2 * HEADS, D])
                q = heads(QK)
                nc.vector.tensor_tensor(heads(rope), q, cos, ALU.mult)
                nc.vector.tensor_tensor(heads(rope_b)[:, :, 0:half], q[:, :, half:D], sin[:, :, 0:half], ALU.mult)
                nc.vector.tensor_tensor(heads(rope_b)[:, :, half:D], q[:, :, 0:half], sin[:, :, half:D],
                                        ALU.mult).then_inc(rope_parts, 1)

            def centre(g, j, link):
                dve.wait_ge(roped, ONE + TPG * g + j + 1)
                link(nc.vector.tensor_reduce(hsum[:], heads(rope), AX.X, ALU.add))
                link(nc.vector.tensor_scalar(hmean[:], hsum[:], 1.0 / D, None, ALU.mult))
                nc.vector.tensor_tensor(heads(cen), heads(rope), wide(hmean), ALU.subtract).then_inc(centred, 1)

            def variance(g, j, link):
                dve.wait_ge(squared, ONE + TPG * g + j + 1)
                link(nc.vector.tensor_reduce(hsum[:], heads(rope_b), AX.X, ALU.add))
                nc.vector.tensor_scalar(hvar[:], hsum[:], 1.0 / D, EPS, ALU.mult, ALU.add).then_inc(hvar_ready, 1)

            def norm(g, j):
                n = TPG * g + j
                dve.wait_ge(hrstd_ready, ONE + n + 1)
                dve.wait_ge(q_transposed, ONE + n)
                nc.vector.tensor_tensor(heads(y), heads(cen), wide(hrstd), ALU.mult).then_inc(y_ready, 1)

            def qk_low(g, j):
                n = TPG * g + j
                dve.wait_ge(qkT_high, ONE + n + 1)
                dve.wait_ge(qkT_stored[j % 2], ONE + 16 * 4 * (2 * g + j // 2))
                nc.vector.tensor_tensor(qkT_lo[j % 2][:], qkT[:], qkT_hi[j % 2][:].bitcast(F32), ALU.subtract).then_inc(qkT_low, 1)

            def hidden(g, j):
                m = IC * g + j
                dve.wait_ge(silu_done, ONE + m + 1)
                dve.wait_ge(up_full, ONE + m + 1)
                dve.wait_ge(hidden_low, ONE + m)
                nc.vector.tensor_tensor(hf[:], sg[:], UP[:], ALU.mult).then_inc(hidden_done, 1)

            FIRST_LINKS, ROUTE_LINKS = 2 * TPG, 3
            GROUP_LINKS = 2 * TPG + ROUTE_LINKS + 3 * TPG

            def body(g, has_next):
                link = Links(dve, dve_order, ONE + FIRST_LINKS + GROUP_LINKS * g, passed)
                for j in range(TPG):
                    rotate(g, j)
                    if j >= 1:
                        norm(g, j - 1)
                    if j >= 2:
                        qk_low(g, j - 2)
                    centre(g, j, link)
                    variance(g, j, link)
                    if j < IC:
                        hidden(g, j)
                    if j == 0:
                        route(g, link)
                    if j == 1 and has_next:
                        x_stats(g + 1, (0, 1), link)
                    if j == 2 and has_next:
                        x_stats(g + 1, (2, 3), link)
                qk_low(g, 2)
                if has_next:
                    x_low(g + 1, (0, 1))
                    x_low(g + 1, (2, 3))
                norm(g, 3)
                qk_low(g, 3)
                if has_next:
                    assert link.n == GROUP_LINKS, link.n

            def first():
                link = Links(dve, dve_order, ONE, passed)
                x_stats(0, [0, 1, 2, 3], link)
                x_low(0, range(C))
                assert link.n == FIRST_LINKS, link.n

            groups(dve, first, body)

        @block.tensor
        def _(pe):
            def three(out, hi, lo, w_hi, w_lo, start, stop):
                nc.tensor.matmul(out, hi, w_hi, start=start, stop=False)
                nc.tensor.matmul(out, hi, w_lo, start=False, stop=False)
                return nc.tensor.matmul(out, lo, w_hi, start=False, stop=stop)

            def transposes_x(g, chunks):
                pe.wait_ge(xn_ready, ONE + g + 1)
                for c in chunks:
                    if c < 2:
                        if not (isinstance(g, int) and g == 0):
                            pe.wait_ge((q_copied, k_copied)[c], ONE + TPG * g - 1)
                    else:
                        pe.wait_ge(xT_low, ONE + C * g + c - 1)
                    for j in range(TPG):
                        last = nc.tensor.transpose(TR[c % 2][:, j * P:(j + 1) * P], x[:, j, c * P:(c + 1) * P], w["ident"][:])
                    last.then_inc(x_transposed, 1)

            wr = [w["router_" + s][:].rearrange("p (c n) -> p c n", c=C) for s in ("hi", "lo")]
            wq = [w["qkv_" + s][:].rearrange("p (c k n) -> p c k n", c=C, k=3) for s in ("hi", "lo")]
            wg = [w["gu_" + s][:].rearrange("p (c two n) -> p c two n", c=C, two=2) for s in ("hi", "lo")]
            wd = [w["down_" + s][:].rearrange("p (c n) -> p c n", c=IC) for s in ("hi", "lo")]

            def logitsT(g):
                pe.wait_ge(xT_low, ONE + C * (g + 1))
                for c in range(C):
                    last = three(TR[0][0:NE, :], wr[0][:, c], wr[1][:, c], xT_hi[:, c], xT_lo[:, c], c == 0, c == C - 1)
                last.then_inc(logitsT_full, 1)

            def logits(g):
                pe.wait_ge(k_copied, ONE + TPG * g)
                pe.wait_ge(logitsT_copied, ONE + g + 1)
                pe.sem_inc(passed, 1)
                for j in range(TPG):
                    last = nc.tensor.transpose(TR[1][:, j * NE:(j + 1) * NE], lgT[:, j * P:(j + 1) * P], w["ident"][0:NE, 0:NE])
                last.then_inc(logits_full, 1)

            def qkv(g, j):
                n = TPG * g + j
                pe.wait_ge(xT_low, ONE + C * (g + 1))
                pe.wait_ge(rope_parts, ONE + n)
                for k in range(3):
                    if k == 2:
                        pe.wait_ge(v_copied, ONE + n)
                    out = QK[:, k * E:(k + 1) * E] if k < 2 else V[:]
                    for c in range(C):
                        t = slice(j * P, (j + 1) * P)
                        last = three(out, xT_hi[:, c, t], xT_lo[:, c, t], wq[0][:, c, k], wq[1][:, c, k], c == 0, c == C - 1)
                    if k > 0:
                        last.then_inc((qk_full, v_full)[k - 1], 1)

            def gate_up(g, m):
                t = slice(m * P, (m + 1) * P)
                if m == 0:
                    pe.wait_ge(ffn_copied, ONE + TPG * g)
                for k, (out, full, free) in enumerate(((GATE, gate_full, silu_done), (UP, up_full, hidden_done))):
                    pe.wait_ge(free, ONE + IC * g + m)
                    for c in range(C):
                        nc.tensor.matmul(out[:], wg[0][:, c, k, t], xT_hi[:, c], start=(c == 0), stop=False)
                        nc.tensor.matmul(out[:], wg[0][:, c, k, t], xT_lo[:, c], start=False, stop=False)
                        last = nc.tensor.matmul(out[:], wg[1][:, c, k, t], xT_hi[:, c], start=False, stop=(c == C - 1))
                    last.then_inc(full, 1)

            def qk_transposes(g, j, has_next):
                n = TPG * g + j
                pe.wait_ge(y_ready, ONE + n + 1)
                pe.wait_ge(k_copied, ONE + n)
                if j == 0:
                    pe.wait_ge(logits_copied, ONE + g + 1)
                if j == 3 and has_next:
                    pe.wait_ge(xT_low, ONE + C * (g + 2))
                for c in range(C):
                    last = nc.tensor.transpose(TR[1][:, c * P:(c + 1) * P], y[:, E + c * P:E + (c + 1) * P], w["ident"][:])
                last.then_inc(k_transposed, 1)
                pe.wait_ge(q_copied, ONE + n)
                if j == 0:
                    pe.wait_ge(logitsT_copied, ONE + g + 1)
                if j == 3 and has_next:
                    pe.wait_ge(logitsT_copied, ONE + g + 2)
                for c in range(C):
                    last = nc.tensor.transpose(TR[0][:, c * P:(c + 1) * P], y[:, c * P:(c + 1) * P], w["ident"][:])
                last.then_inc(q_transposed, 1)

            def down(g, j):
                if j == 0:
                    pe.wait_ge(hidden_low, ONE + IC * (g + 1))
                    pe.wait_ge(ffn_copied, ONE + TPG * g)
                elif j == 1:
                    pe.wait_ge(silu_done, ONE + IC * (g + 1))
                elif j == 2:
                    pe.wait_ge(hidden_done, ONE + IC * (g + 1))
                else:
                    pe.wait_ge(ffn_copied, ONE + TPG * g + 1)
                t = slice(j * P, (j + 1) * P)
                for c in range(IC):
                    last = three(DOWN[j][:], hT_hi[:, c, t], hT_lo[:, c, t], wd[0][:, c], wd[1][:, c], c == 0, c == IC - 1)
                last.then_inc(down_full, 1)

            def body(g, has_next):
                for j in range(TPG):
                    qkv(g, j)
                    if j == 0:
                        logits(g)
                    if j < IC:
                        gate_up(g, j)
                    if j >= 1:
                        qk_transposes(g, j - 1, has_next)
                down(g, 0)
                if has_next:
                    transposes_x(g + 1, (0, 1))
                down(g, 1)
                down(g, 2)
                if has_next:
                    transposes_x(g + 1, (2, 3))
                down(g, 3)
                if has_next:
                    logitsT(g + 1)
                qk_transposes(g, 3, has_next)

            def first():
                transposes_x(0, range(C))
                logitsT(0)

            groups(pe, first, body)


def list_tokens(nc, dram, w):
    HALF_T, HALF_NT = T // 2, NT // 2
    with ExitStack() as ctx:
        sb = lambda name, shape, dt=F32: ctx.enter_context(nc.sbuf_tensor(name, shape, dt))
        sem = lambda name: ctx.enter_context(nc.semaphore(name))
        total, rtotal = sb("weight_total", [P, NT]), sb("weight_rtotal", [P, NT])
        wide = lambda t: t[:].unsqueeze(2).broadcast_to([P, NT, NE])
        down_i, down_f = sb("downcount_i", [P, HALF_T], I32), sb("downcount", [P, HALF_T])
        pairs = sb("mark_pairs", [P, HALF_NT, 2, NE])
        key = sb("key", [P, HALF_T])
        found = sb("found", [P, CAP])
        both = sb("found_both", [NE, 2 * CAP])
        first = sb("first", [NE, CAP])
        token = sb("token", [CAP, NE])
        empty = sb("empty", [CAP, NE])
        slot_i, slot = sb("slot_i", [CAP, 1], I32), sb("slot", [CAP, 1])
        zeros = sb("zero_rows", [CAP, E])
        banks = [ctx.enter_context(nc.psum_tensor(f"mask_bank{i}", [P, 512], F32)) for i in range(4)]
        lists = ctx.enter_context(nc.psum_tensor("lists", [P, 512], F32))

        marks_paired, counted, exp_done, weights_done, masks_turned = sem("marks_paired"), sem("counted"), sem("exp_done"), sem("weights_done"), sem("masks_turned")
        first_done, lists_turned, zeroed, stored, order = sem("first_done"), sem("lists_turned"), sem("zeroed"), sem("rows_stored"), sem("order")
        block = ctx.enter_context(nc.Block())

        @block.gpsimd
        def _(pool):
            nc.gpsimd.memset(zeros[:], 0.0).then_inc(zeroed, 1)
            for h in range(2):
                nc.gpsimd.iota(down_i[h * NE:(h + 1) * NE, :], pattern=[[-1, HALF_T]], base=T - h * HALF_T,
                               channel_multiplier=0)
            nc.gpsimd.iota(slot_i[:], pattern=[[1, 1]], base=0, channel_multiplier=1).then_inc(counted, 1)

        @block.tensor
        def _(pe):
            for q in range(4):
                for t in range(4):
                    if t == 0:
                        pe.wait_ge(marks_paired, q + 1)
                    last = nc.tensor.transpose(banks[q][:, t * P:(t + 1) * P], pairs[:, 4 * q + t].rearrange("p h n -> p (h n)"), w["ident"][:])
                last.then_inc(masks_turned, 1)
            pe.wait_ge(first_done, 1)
            nc.tensor.transpose(lists[0:CAP, 0:NE], first[:], w["ident"][0:NE, 0:NE]).then_inc(lists_turned, 1)

        @block.scalar
        def _(act):
            by_half = w["mask"][:].rearrange("p (h t) n -> p t h n", h=2)
            for q in range(4):
                part = slice(4 * q, 4 * q + 4)
                nc.scalar.activation(pairs[:, part], by_half[:, part], ACT.Copy).then_inc(marks_paired, 1)
            nc.scalar.activation(w["ldiff"][:], w["ldiff"][:], ACT.Exp).then_inc(exp_done, 1)

        @block.vector
        def _(dve):
            link = Links(dve, order, 0, None)
            dve.wait_ge(counted, 1)
            link(nc.vector.tensor_copy(down_f[:], down_i[:]))
            for q in range(4):
                dve.wait_ge(masks_turned, q + 1)
                last = nc.vector.tensor_tensor(key[:, q * 512:(q + 1) * 512], banks[q][:], down_f[:, q * 512:(q + 1) * 512], ALU.mult)
            link(last)
            dve.wait_ge(exp_done, 1)
            link(nc.vector.tensor_tensor(w["ldiff"][:], w["ldiff"][:], w["mask"][:], ALU.mult))
            link(nc.vector.tensor_reduce(total[:], w["ldiff"][:], AX.X, ALU.add))
            link(nc.vector.reciprocal(rtotal[:], total[:]))
            nc.vector.tensor_tensor(w["ldiff"][:], w["ldiff"][:], wide(rtotal), ALU.mult).then_inc(weights_done, 1)
            for r in range(CAP // 8):
                eight = found[:, 8 * r:8 * r + 8]
                link(nc.vector.max(eight, key[:]))
                link(nc.vector.match_replace(out=key[:], in_to_replace=eight, in_values=key[:], imm_value=0.0))
            nc.vector.tensor_copy(both[:, 0:CAP], found[0:NE, :])
            link(nc.vector.tensor_copy(both[:, CAP:], found[NE:, :]))
            for r in range(CAP // 8):
                eight = first[:, 8 * r:8 * r + 8]
                ins = nc.vector.max(eight, both[:])
                if r == CAP // 8 - 1:
                    ins.then_inc(first_done, 1)
                else:
                    link(ins)
                    link(nc.vector.match_replace(out=both[:], in_to_replace=eight, in_values=both[:], imm_value=0.0))
            dve.wait_ge(lists_turned, 1)
            link(nc.vector.tensor_scalar(token[:], lists[0:CAP, 0:NE], -1.0, float(T), ALU.mult, ALU.add))
            link(nc.vector.tensor_copy(slot[:], slot_i[:]))
            link(nc.vector.tensor_scalar(empty[:], token[:], float(T), slot[:, 0:1], ALU.is_equal, ALU.mult))
            nc.vector.tensor_tensor(w["scatter_to"][:], token[:], empty[:], ALU.add)
            two = token[:].rearrange("s (q h) -> s h q", h=2)
            for h in range(2):
                last = nc.vector.tensor_scalar(w["gather_from"][h * CAP:(h + 1) * CAP, 0:NE // 2], two[:, h], float(T - 1), None, ALU.min)
            link(last)
            nc.vector.tensor_copy(w["gather_from"][:, NE // 2:], w["gather_from"][:, 0:1])

        @block.sync
        def _(sp):
            sp.wait_ge(zeroed, 1)
            sp.dma_start(dram["ffn"][T:, :], zeros[:]).then_inc(stored, 16)
            sp.wait_ge(weights_done, 1)
            sp.dma_start(dram["xw"].rearrange("(t p) e -> p t e", p=P)[:, :, E:], w["ldiff"][:]).then_inc(stored, 16)
            sp.wait_ge(stored, 32)


def attend(nc, dram, w):
    K3 = 3 * D
    EP = NE // 2
    with ExitStack() as ctx:
        sb = lambda name, shape, dt=F32: ctx.enter_context(nc.sbuf_tensor(name, shape, dt))
        sems = []

        def sem(name):
            sems.append(ctx.enter_context(nc.semaphore(name)))
            return sems[-1]


        two = lambda f: [f(0), f(1)]
        qs = two(lambda u: sb(f"q_stack{u}", [K3, 2, N], F32R))
        ks = two(lambda u: sb(f"k_stack{u}", [K3, 2, N], F32R))
        vs = two(lambda u: sb(f"v_pair{u}", [P, N // P, 2 * VW]))
        wg = two(lambda u: sb(f"w_gate{u}", [P, 2, C, I]))
        wu = two(lambda u: sb(f"w_up{u}", [P, 2, C, I]))
        wd = sb("w_down", [P, 2, IC, E])
        a = two(lambda h: two(lambda r: sb(f"probs{h}{r}", [P, N])))
        o_raw = two(lambda u: sb(f"o_raw{u}", [P, N]))
        oT = sb("oT", [P, C, N])
        den, rden = sb("den", [2 * HEADS, N]), sb("rden", [2 * HEADS, N])
        rden_parts = sb("rden_parts", [4 * HEADS, N], F32R)
        on_hi, on_lo = sb("on_hi", [P, TPG, C, P], F32R), sb("on_lo", [P, TPG, C, P], F32R)
        wo_hi, wo_lo = sb("w_out_hi", [P, C, E], F32R), sb("w_out_lo", [P, C, E], F32R)
        sel_f, sel = sb("sel_f", [4 * HEADS, C, P]), sb("sel", [4 * HEADS, C, P], F32R)
        gi = two(lambda u: sb(f"gather_now{u}", [P, 1], U32))
        si = two(lambda u: sb(f"scatter_now{u}", [CAP, 2], U32))
        wt = two(lambda u: sb(f"weight_now{u}", [P, 1]))
        xg = two(lambda u: sb(f"x_rows{u}", [P, XW]))
        xgT = sb("x_rowsT", [P, C, P])
        esg, eh = sb("e_silu", [P, I]), sb("e_hidden", [P, I])
        ehT = sb("e_hiddenT", [P, IC, P])
        ey = two(lambda u: sb(f"e_out{u}", [P, E]))
        s_out = two(lambda u: sb(f"s_out{u}", [P, E]))

        S = two(lambda h: ctx.enter_context(nc.psum_tensor(f"scores{h}", [P, N], F32)))
        O = ctx.enter_context(nc.psum_tensor("o_acc", [P, N], F32))
        P1 = ctx.enter_context(nc.psum_tensor("e_bank1", [P, 512], F32))
        P2 = ctx.enter_context(nc.psum_tensor("e_bank2", [P, 512], F32))

        qkv_loaded = two(lambda u: sem(f"qkv_loaded{u}"))
        gu_loaded = two(lambda u: sem(f"gate_up_loaded{u}"))
        d_loaded, wo_loaded, wo_high, wo_low = sem("down_loaded"), sem("w_out_loaded"), sem("w_out_high"), sem("w_out_low")
        s_full, squared = two(lambda h: sem(f"scores_full{h}")), two(lambda h: sem(f"squared{h}"))
        masked, a_ready = two(lambda h: sem(f"masked{h}")), two(lambda h: sem(f"probs_ready{h}"))
        o_copied, den_loaded = sem("o_copied"), sem("den_loaded")
        index_ready, x_gathered = sem("index_ready"), two(lambda u: sem(f"x_gathered{u}"))
        xgT_full, xgT_copied = sem("x_rowsT_full"), sem("x_rowsT_copied")
        e_gate_full, e_silu_done, e_hidden_done = sem("e_gate_full"), sem("e_silu_done"), sem("e_hidden_done")
        ehT_full, ehT_copied, ey_full, ey_ready, scattered = sem("e_hT_full"), sem("e_hT_copied"), sem("e_out_full"), sem("e_out_ready"), sem("scattered")
        rden_high, rden_low, spread, normed, on_high, on_low_done = sem("rden_high"), sem("rden_low"), sem("rden_spread"), sem("o_normed"), sem("on_high"), sem("on_low_done")
        o_full_u, o_moved_u, e_up_u = two(lambda u: sem(f"o_full{u}")), two(lambda u: sem(f"o_moved{u}")), two(lambda u: sem(f"e_up_full{u}"))
        s_ready, s_copied, s_stored = sem("s_full"), sem("s_copied"), two(lambda u: sem(f"s_stored{u}"))
        passed, made, weight_ready, rden_done, sel_ready = sem("attend_passed"), sem("made"), sem("weight_ready"), sem("rden_done"), sem("sel_ready")
        start_at_one(nc, [s for s in sems if s not in (scattered, *x_gathered)])
        block = ctx.enter_context(nc.Block())

        NK = N // P
        RP = 4

        def pieces(j):
            return [(P * j, 512), (512, N)] if P * j < 512 else [(P * j, N)]

        def others(eng, b, pair):
            pair(b, 0, 1)
            with eng.Fori(1, PAIRS // 2) as i:
                for u in range(2):
                    pair(b, i, u)

        def loop(eng, pair, sequence):
            pair(0, 0, 0)
            with eng.Fori(0, B - 1) as b:
                others(eng, b, pair)
                pair(b + 1, 0, 0)
                sequence(b, False)
            others(eng, B - 1, pair)
            sequence(B - 1, True)

        def numbers(b, i, u):
            start = isinstance(i, int) and i == 0 and u == 0
            first = start and isinstance(b, int)
            return 8 * b + 2 * i + u, 4 * b + i, first, start and not first

        qk_src = [dram["qT"], dram["kT"]]
        wgate = dram["w_gate"].rearrange("(q e) (p c) n -> q p e (c n)", e=2, c=C)
        wup = dram["w_up"].rearrange("(q e) (p c) n -> q p e (c n)", e=2, c=C)
        wdown = dram["w_down"].rearrange("(q e) (p c) n -> q p e (c n)", e=2, c=IC)

        @block.sync
        def _(sp):
            sp.dma_start(oT[:, :, 0:E], dram["w_out"].rearrange("(c p) n -> p c n", p=P)).then_inc(wo_loaded, 16)

            def load(b, i, u):
                it, k, _, _ = numbers(b, i, u)
                sp.wait_ge(o_full_u[u], ONE + k)
                for h in range(2):
                    row = (2 * (2 * i + u) + h) * D
                    rows = lambda src, part: src[part, bass.ds(row, D), bass.ds(b * N, N)]
                    for g, part in enumerate((0, 0, 1)):
                        sp.dma_start(qs[u][g * D:(g + 1) * D, h].bitcast(F32), rows(qk_src[0], part)).then_inc(qkv_loaded[u], 16)
                    for g, part in enumerate((0, 1, 0)):
                        sp.dma_start(ks[u][g * D:(g + 1) * D, h].bitcast(F32), rows(qk_src[1], part)).then_inc(qkv_loaded[u], 16)
                for half in range(2):
                    sp.dma_start(vs[u][:, half * TPG:(half + 1) * TPG].rearrange("p j n -> p (j n)"),
                                 dram["v"][bass.ds(2 * b + half, 1), bass.ds(2 * i + u, 1)].rearrange("a q p n -> p (a q n)")).then_inc(qkv_loaded[u], 16)
                sp.wait_ge(e_up_u[u], ONE + k)
                for dst, src in ((wg[u], wgate), (wu[u], wup)):
                    sp.dma_start(dst[:].rearrange("p e c n -> p e (c n)"),
                                 src[bass.ds(it, 1)].rearrange("a p e n -> p (a e) n")).then_inc(gu_loaded[u], 16)
                sp.wait_ge(ey_full, ONE + it)
                sp.dma_start(wd[:].rearrange("p e c n -> p e (c n)"),
                             wdown[bass.ds(it, 1)].rearrange("a p e n -> p (a e) n")).then_inc(d_loaded, 16)

            def move(b, i, u):
                it, k, _, _ = numbers(b, i, u)
                sp.wait_ge(o_copied, ONE + 2 * (it + 1))
                for h in range(2):
                    r = 2 * u + h
                    sp.dma_start(oT[r * D:(r + 1) * D, bass.ds(i, 1)].rearrange("p a n -> p (a n)"),
                                 o_raw[u][64 * h:64 * h + D]).then_inc(o_moved_u[u], 16)
                    sp.dma_start(dram["den"][bass.ds(b, 1), bass.ds(4 * i + r, 1)].rearrange("a h n -> (a h) n"),
                                 o_raw[u][64 * h + D:64 * h + VW]).then_inc(o_moved_u[u], 16)

            def load_denominators(b):
                for u in range(2):
                    sp.wait_ge(o_moved_u[u], ONE + 64 * 4 * (b + 1))
                sp.wait_ge(rden_done, ONE + RP * b)
                sp.dma_start(den[0:HEADS], dram["den"][bass.ds(b, 1)].rearrange("a h n -> (a h) n")).then_inc(den_loaded, 16)

            def store_s(b):
                for t in range(NK):
                    sp.wait_ge(s_copied, ONE + NK * b + t + 1)
                    sp.dma_start(dram["s"][bass.ds(b * N + t * P, P), :], s_out[t % 2][:]).then_inc(s_stored[t % 2], 16)

            def rest(b):
                sp.wait_ge(on_low_done, ONE + 2 * C * b)
                move(b, 0, 0)
                with sp.Fori(1, PAIRS // 2) as i:
                    for u in range(2):
                        load(b, i, u)
                        move(b, i - 1 + u, 1 - u)

            load(0, 0, 0)
            load(0, 0, 1)
            sp.wait_ge(wo_low, ONE + 1)
            with sp.Fori(0, B - 1) as b:
                rest(b)
                load(b + 1, 0, 0)
                move(b, PAIRS // 2 - 1, 1)
                load_denominators(b)
                load(b + 1, 0, 1)
                store_s(b)
            rest(B - 1)
            move(B - 1, PAIRS // 2 - 1, 1)
            load_denominators(B - 1)
            store_s(B - 1)
            for u in range(2):
                sp.wait_ge(s_stored[u], ONE + 16 * NT // 2)
                sp.wait_ge(o_moved_u[u], ONE + 64 * EP // 2)

        @block.gpsimd
        def _(pool):
            nc.gpsimd.memset(sel_f[:], 0.0).then_inc(made, 1)
            nc.gpsimd.memset(ey[1][:], 0.0)
            nc.gpsimd.memset(den[:], 1.0).then_inc(made, 1)
            pool.wait_ge(made, ONE + 2)
            for h in range(2):
                part = sel_f[2 * HEADS * h:2 * HEADS * (h + 1)].rearrange("r c (g d) -> r c g d", d=D)
                nc.gpsimd.affine_select(out=part, in_=part, compare_op=ALU.not_equal, fill=1.0, base=0,
                                        pattern=[[-4, C], [-1, P // D], [0, D]], channel_multiplier=1).then_inc(sel_ready, 1)
                pool.wait_ge(sel_ready, ONE + h + 1)
            nc.gpsimd.iota(si[1][:].bitcast(I32), pattern=[[0, 2]], base=T, channel_multiplier=1).then_inc(made, 1)
            pool.wait_ge(made, ONE + 3)

            def gather(u, n):
                pool.wait_ge(index_ready, ONE + n)
                pool.sem_inc(passed, 1)
                nc.gpsimd.indirect_dma_start(out=xg[u][:], out_offset=None, in_=dram["xw"],
                                             in_offset=bass.IndirectOffsetOnAxis(ap=gi[u][:, 0:1], axis=0),
                                             bounds_check=T - 1).then_inc(x_gathered[u], 16)

            def scatter(u, e, n):
                if n is not None:
                    pool.wait_ge(scattered, 16 * n)
                    pool.sem_inc(passed, 1)
                nc.gpsimd.indirect_dma_start(out=dram["ffn"], out_offset=bass.IndirectOffsetOnAxis(ap=si[u][:, e:e + 1], axis=0),
                                             in_=ey[u][e * CAP:(e + 1) * CAP, :], in_offset=None,
                                             bounds_check=T + CAP - 1, compute_op=ALU.add).then_inc(scattered, 16)

            gather(0, 1)
            scatter(1, 0, None)

            def pair(b, i, u):
                it, k, _, _ = numbers(b, i, u)
                for j in range(NK):
                    for h in range(2):
                        pool.wait_ge(squared[h], ONE + NK * it + j + 1)
                        pool.sem_inc(passed, 1)
                        d = a[h][j % 2][:, j * P:(j + 1) * P]
                        nc.gpsimd.affine_select(out=d, in_=d, compare_op=ALU.is_ge, fill=0.0, base=0,
                                                pattern=[[1, P]], channel_multiplier=-1).then_inc(masked[h], 1)
                    if j == 1:
                        pool.wait_ge(ey_ready, ONE + it)
                        scatter(1 - u, 0, 2 * it + 1)
                    if j == 4:
                        scatter(1 - u, 1, 2 * it + 2)
                    if j == 3:
                        gather(1 - u, it + 2)

            loop(pool, pair, lambda b, last: None)
            pool.wait_ge(ey_ready, ONE + EP)
            scatter(1, 0, 2 * EP + 1)
            scatter(1, 1, 2 * EP + 2)
            pool.wait_ge(scattered, 16 * (2 * EP + 3))
            for u in range(2):
                pool.wait_ge(x_gathered[u], 16 * (EP // 2 + 1 - u))

        @block.scalar
        def _(act):
            act.wait_ge(wo_loaded, ONE + 16)
            nc.scalar.activation(wo_hi[:], oT[:, :, 0:E], ACT.Copy).then_inc(wo_high, 1)

            def copy_o(it, u, k):
                act.wait_ge(o_full_u[u], ONE + k + 1)
                act.wait_ge(o_moved_u[u], ONE + 64 * k)
                for h in range(2):
                    nc.scalar.activation(o_raw[u][64 * h:64 * h + VW], O[64 * h:64 * h + VW], ACT.Copy).then_inc(o_copied, 1)

            def rden_hi(b, half):
                act.wait_ge(rden_done, ONE + RP * b + (half + 1) * RP // 2)
                part = slice(512 * half, 512 * (half + 1))
                nc.scalar.activation(rden_parts[0:2 * HEADS, part], rden[:, part], ACT.Copy).then_inc(rden_high, 1)

            def pair(b, i, u):
                it, k, first, start = numbers(b, i, u)
                for j in range(NK):
                    for h in range(2):
                        act.wait_ge(s_full[h], ONE + NK * it + j + 1)
                        nc.scalar.activation(a[h][j % 2][:, P * j:], S[h][:, P * j:], ACT.Square).then_inc(squared[h], 1)
                    if j == 0:
                        act.wait_ge(xgT_full, ONE + it + 1)
                        nc.scalar.activation(xgT[:], P1[:].rearrange("p (c t) -> p c t", c=C), ACT.Copy).then_inc(xgT_copied, 1)
                        if not first:
                            copy_o(it - 1, 1 - u, k - 1 + u)
                    if j == 4:
                        act.wait_ge(e_gate_full, ONE + it + 1)
                        nc.scalar.activation(esg[:], P1[:, 0:I], ACT.Silu).then_inc(e_silu_done, 1)
                    if j == 5:
                        act.wait_ge(ehT_full, ONE + it + 1)
                        nc.scalar.activation(ehT[:], P1[:, 0:IC * P].rearrange("p (c t) -> p c t", c=IC), ACT.Copy).then_inc(ehT_copied, 1)
                    if start and j in (5, 7):
                        rden_hi(b - 1, (j - 5) // 2)

            def sequence(b, last):
                if last:
                    copy_o(EP - 1, 1, EP // 2 - 1)
                    rden_hi(b, 0)
                    rden_hi(b, 1)

                def cut(m):
                    act.wait_ge(normed, ONE + 2 * C * b + C * (m // TPG + 1))
                    if m >= TPG:
                        act.wait_ge(s_ready, ONE + NK * b + m - TPG + 1)
                    nc.scalar.activation(on_hi[:, m % TPG], oT[:, :, m * P:(m + 1) * P], ACT.Copy).then_inc(on_high, 1)

                for m in range(TPG):
                    cut(m)
                for m in range(NK):
                    act.wait_ge(s_ready, ONE + NK * b + m + 1)
                    act.wait_ge(s_stored[m % 2], ONE + 16 * (TPG * b + m // 2))
                    nc.scalar.activation(s_out[m % 2][:], S[1][:, 512 * (m % 2):512 * (m % 2) + 512], ACT.Copy).then_inc(s_copied, 1)
                    if m < TPG:
                        cut(m + TPG)

            loop(act, pair, sequence)

        @block.vector
        def _(dve):
            dve.wait_ge(wo_high, ONE + 1)
            nc.vector.tensor_tensor(wo_lo[:], oT[:, :, 0:E], wo_hi[:].bitcast(F32), ALU.subtract).then_inc(wo_low, 1)
            dve.wait_ge(sel_ready, ONE + 2)
            nc.vector.tensor_copy(sel[:], sel_f[:])
            nc.vector.tensor_copy(gi[0][:], w["gather_from"][:, 0:1]).then_inc(index_ready, 1)

            def reciprocals(b, q):
                if q == 0:
                    dve.wait_ge(den_loaded, ONE + 16 * (b + 1))
                    dve.wait_ge(rden_high, ONE + 2 * b)
                part = slice(q * N // RP, (q + 1) * N // RP)
                nc.vector.reciprocal(rden[:, part], den[:, part]).then_inc(rden_done, 1)

            def rden_lo(b, half):
                dve.wait_ge(rden_high, ONE + 2 * b + half + 1)
                part = slice(512 * half, 512 * (half + 1))
                nc.vector.tensor_tensor(rden_parts[2 * HEADS:, part], rden[:, part], rden_parts[0:2 * HEADS, part].bitcast(F32),
                                        ALU.subtract).then_inc(rden_low, 1)

            def pair(b, i, u):
                it, k, first, start = numbers(b, i, u)
                for j in range(NK):
                    for h in range(2):
                        dve.wait_ge(masked[h], ONE + NK * it + j + 1)
                        part = a[h][j % 2][:, P * j:]
                        nc.vector.tensor_tensor(part, part, part, ALU.mult).then_inc(a_ready[h], 1)
                    if j == 2:
                        dve.wait_ge(x_gathered[u], 16 * (k + 1))
                        dve.wait_ge(scattered, 16 * (2 * it + 1))
                        nc.vector.tensor_copy(si[u][:], w["scatter_to"][:, bass.ds(2 * it, 2)])
                        for h in range(2):
                            part = slice(h * CAP, (h + 1) * CAP)
                            last = nc.vector.tensor_copy(wt[u][part, :], xg[u][part, bass.ds(2 * it + E + h, 1)])
                        last.then_inc(weight_ready, 1)
                        nc.vector.tensor_copy(gi[1 - u][:], w["gather_from"][:, bass.ds(it + 1, 1)]).then_inc(index_ready, 1)
                    if j == 4:
                        dve.wait_ge(e_silu_done, ONE + it + 1)
                        dve.wait_ge(e_up_u[u], ONE + k + 1)
                        dve.wait_ge(ehT_full, ONE + it)
                        nc.vector.tensor_tensor(eh[:], esg[:], P2[:, 0:I], ALU.mult).then_inc(e_hidden_done, 1)
                    if start and 2 <= j < 2 + RP:
                        reciprocals(b - 1, j - 2)
                    if start and j >= 6:
                        rden_lo(b - 1, j - 6)
                dve.wait_ge(ey_full, ONE + it + 1)
                dve.wait_ge(scattered, 16 * (2 * it + 1))
                dve.wait_ge(weight_ready, ONE + it + 1)
                nc.vector.tensor_scalar(ey[u][:], P2[:], wt[u][:, 0:1], None, ALU.mult).then_inc(ey_ready, 1)

            def sequence(b, last):
                if last:
                    for q in range(RP):
                        reciprocals(b, q)
                        if q >= 2:
                            rden_lo(b, q - 2)

                def normalise(n):
                    half, c = n // C, n % C
                    dve.wait_ge(spread, ONE + 2 * C * b + n + 1)
                    part = oT[:, c, 512 * half:512 * (half + 1)]
                    nc.vector.tensor_tensor(part, part, S[0][:, 512 * (c % 2):512 * (c % 2) + 512], ALU.mult).then_inc(normed, 1)

                def rest(m):
                    dve.wait_ge(on_high, ONE + 2 * C * b + m + 1)
                    nc.vector.tensor_tensor(on_lo[:, m % TPG], oT[:, :, m * P:(m + 1) * P], on_hi[:, m % TPG].bitcast(F32),
                                            ALU.subtract).then_inc(on_low_done, 1)

                for n in range(C):
                    normalise(n)
                for m in range(TPG):
                    rest(m)
                    normalise(C + m)
                for m in range(TPG, NK):
                    rest(m)

            loop(dve, pair, sequence)

        @block.tensor
        def _(pe):
            pe.wait_ge(wo_low, ONE + 1)

            def scores(u, it, j, b, i, k):
                for h in range(2):
                    pe.wait_ge(squared[h], ONE + NK * it + j)
                    if j == 0 and isinstance(i, int) and i == 0 and u == 1:
                        pe.wait_ge(s_copied, ONE + NK * b)
                        pe.wait_ge(on_low_done, ONE + 2 * C * b)
                    for n0, n1 in pieces(j):
                        last = nc.tensor.matmul(S[h][:, n0:n1], ks[u][:, h, P * j:P * (j + 1)], qs[u][:, h, n0:n1], start=True, stop=True)
                    last.then_inc(s_full[h], 1)

            def values(u, it, j, k):
                for h in range(2):
                    pe.wait_ge(a_ready[h], ONE + NK * it + j + 1)
                if j == 0:
                    pe.wait_ge(o_copied, ONE + 2 * it)
                for n0, n1 in pieces(j):
                    for h in range(2):
                        last = nc.tensor.matmul(O[64 * h:64 * h + VW, n0:n1], vs[u][:, j, VW * h:VW * (h + 1)],
                                                a[h][j % 2][:, n0:n1], start=(j == 0), stop=(j == (3 if n0 < 512 else 7)))
                if j == NK - 1:
                    last.then_inc(o_full_u[u], 1)

            def expert(u, it, j, k):
                if j == 0:
                    pe.wait_ge(x_gathered[u], 16 * (k + 1))
                    pe.wait_ge(ehT_copied, ONE + it)
                    for c in range(C):
                        last = nc.tensor.transpose(P1[:, c * P:(c + 1) * P], xg[u][:, c:E:C], w["ident"][:])
                    last.then_inc(xgT_full, 1)
                elif j <= C:
                    c = j - 1
                    if c == 0:
                        pe.wait_ge(gu_loaded[u], ONE + 32 * (k + 1))
                        pe.wait_ge(xgT_copied, ONE + it + 1)
                        pe.wait_ge(ey_ready, ONE + it)
                    for out, wts, full in ((P1, wg[u], e_gate_full), (P2, wu[u], e_up_u[u])):
                        for h in range(2):
                            t = slice(h * CAP, (h + 1) * CAP)
                            last = nc.tensor.matmul(out[t, 0:I], xgT[:, c, t], wts[:, h, c], start=(c == 0), stop=(c == C - 1))
                        if c == C - 1:
                            last.then_inc(full, 1)
                elif j == 5:
                    pe.wait_ge(e_hidden_done, ONE + it + 1)
                    for c in range(IC):
                        last = nc.tensor.transpose(P1[:, c * P:(c + 1) * P], eh[:, c:I:IC], w["ident"][:])
                    last.then_inc(ehT_full, 1)
                else:
                    if j == 6:
                        pe.wait_ge(ehT_copied, ONE + it + 1)
                        pe.wait_ge(d_loaded, ONE + 16 * (it + 1))
                    for c in (0, 1) if j == 6 else (2,):
                        for h in range(2):
                            t = slice(h * CAP, (h + 1) * CAP)
                            last = nc.tensor.matmul(P2[t, :], ehT[:, c, t], wd[:, h, c], start=(c == 0), stop=(c == IC - 1))
                    if j == 7:
                        last.then_inc(ey_full, 1)

            def pair(b, i, u):
                it, k, first, _ = numbers(b, i, u)
                pe.wait_ge(qkv_loaded[u], ONE + 14 * 16 * (k + 1))
                for j in range(NK):
                    scores(u, it, j, b, i, k)
                    expert(u, it, j, k)
                    if j:
                        values(u, it, j - 1, k)
                    elif not first:
                        values(1 - u, it - 1, NK - 1, k - 1 + u)

            def sequence(b, last):
                if last:
                    values(1, EP - 1, NK - 1, EP // 2 - 1)
                for h in range(2):
                    pe.wait_ge(squared[h], ONE + NK * (PAIRS * (b + 1) + (not last)))

                def spread_out(n):
                    half, c = n // C, n % C
                    if c == 0:
                        pe.wait_ge(rden_low, ONE + 2 * b + half + 1)
                    if n >= 2:
                        pe.wait_ge(normed, ONE + 2 * C * b + n - 1)
                    nc.tensor.matmul(S[0][:, 512 * (c % 2):512 * (c % 2) + 512], sel[:, c], rden_parts[:, 512 * half:512 * (half + 1)],
                                     start=True, stop=True).then_inc(spread, 1)

                for n in range(C + 2):
                    spread_out(n)
                for m in range(NK):
                    pe.wait_ge(on_low_done, ONE + 2 * C * b + m + 1)
                    if m >= 2:
                        pe.wait_ge(s_copied, ONE + NK * b + m - 1)
                    out = S[1][:, 512 * (m % 2):512 * (m % 2) + 512]
                    hi, lo = on_hi[:, m % TPG], on_lo[:, m % TPG]
                    for c in range(C):
                        nc.tensor.matmul(out, hi[:, c], wo_hi[:, c], start=(c == 0), stop=False)
                        nc.tensor.matmul(out, hi[:, c], wo_lo[:, c], start=False, stop=False)
                        last_one = nc.tensor.matmul(out, lo[:, c], wo_hi[:, c], start=False, stop=(c == C - 1))
                    last_one.then_inc(s_ready, 1)
                    if m < C - 2:
                        spread_out(C + 2 + m)

            loop(pe, pair, sequence)


def combine(nc, dram, w):
    W2 = 2
    with ExitStack() as ctx:
        sb = lambda name, shape, dt=F32: ctx.enter_context(nc.sbuf_tensor(name, shape, dt))
        sems = []

        def sem(name):
            sems.append(ctx.enter_context(nc.semaphore(name)))
            return sems[-1]


        two = lambda f: [f(0), f(1)]
        xt, st, ft, yt = (two(lambda u: sb(f"c_{n}{u}", [P, W2, E])) for n in ("x", "s", "ffn", "out"))
        loaded, stored = two(lambda u: sem(f"c_loaded{u}")), two(lambda u: sem(f"c_stored{u}"))
        gated, product, done_u = sem("c_gated"), sem("c_product"), two(lambda u: sem(f"c_done{u}"))
        start_at_one(nc, sems)
        block = ctx.enter_context(nc.Block())
        view = lambda name: dram[name][0:T, :].rearrange("(q p w) e -> q p w e", p=P, w=W2)
        STEPS = NT // W2

        def steps(eng, body):
            with eng.Fori(0, STEPS // 2) as i:
                for u in range(2):
                    body(i, u, 2 * i + u)

        @block.sync
        def _(sp):
            def body(i, u, n):
                sp.wait_ge(done_u[u], ONE + i)
                for dst, name in ((ft, "ffn"), (st, "s"), (xt, "x")):
                    sp.dma_start(dst[u][:], view(name)[bass.ds(n, 1)].rearrange("a p w e -> p (a w) e")).then_inc(loaded[u], 16)
            steps(sp, body)

        @block.scalar
        def _(act):
            def body(i, u, n):
                act.wait_ge(loaded[u], ONE + 48 * (i + 1))
                nc.scalar.activation(ft[u][:], ft[u][:], ACT.Silu).then_inc(gated, 1)
                act.wait_ge(done_u[u], ONE + i + 1)
                act.dma_start(view("out")[bass.ds(n, 1)].rearrange("a p w e -> p (a w) e"), yt[u][:]).then_inc(stored[u], 16)
            steps(act, body)
            for u in range(2):
                act.wait_ge(stored[u], ONE + 16 * STEPS // 2)

        @block.vector
        def _(dve):
            def body(i, u, n):
                dve.wait_ge(gated, ONE + n + 1)
                nc.vector.tensor_tensor(st[u][:], st[u][:], ft[u][:], ALU.mult).then_inc(product, 1)
                dve.wait_ge(product, ONE + n + 1)
                dve.wait_ge(stored[u], ONE + 16 * i)
                nc.vector.tensor_tensor(yt[u][:], st[u][:], xt[u][:], ALU.add).then_inc(done_u[u], 1)
            steps(dve, body)


def build(nc, x, w_qkv, w_out, ln_scale, ln_bias, w_router, w_gate, w_up, w_down, w_sh_gate, w_sh_up, w_sh_down, out, upto=9):
    cos, sin = rope_tables()
    scratch = lambda name, shape: nc.dram_tensor(name, shape, F32, kind="Internal").ap()
    dram = {
        "x": x.rearrange("b n e -> (b n) e"), "out": out.rearrange("b n e -> (b n) e"),
        "w_qkv": w_qkv, "w_out": w_out, "ln_scale": ln_scale, "ln_bias": ln_bias,
        "router": w_router, "w_gate": w_gate, "w_up": w_up, "w_down": w_down,
        "w_sh_gate": w_sh_gate, "w_sh_up": w_sh_up, "w_sh_down": w_sh_down,
        "cos": nc.inline_tensor(cos, "rope_cos").ap(), "sin": nc.inline_tensor(sin, "rope_sin").ap(),
        "xw": scratch("xw_rows", [T, XW]),
        "ffn": scratch("ffn_rows", [T + CAP, E]),
        "qT": scratch("qT_parts", [2, E, T]), "kT": scratch("kT_parts", [2, E, T]),
        "v": scratch("v_parts", [G, PAIRS, P, TPG * 2 * VW]),
        "den": scratch("denominators", [B, HEADS, N]), "s": scratch("attention_out", [T, E]),
    }
    with ExitStack() as keep:
        sb = lambda stack, name, shape, dt=F32: stack.enter_context(nc.sbuf_tensor(name, shape, dt))
        w = {"ident": sb(keep, "ident", [P, P]), "gather_from": sb(keep, "gather_from", [P, NE // 2 + 1], U32),
             "scatter_to": sb(keep, "scatter_to", [CAP, NE], U32)}
        with ExitStack() as marks:
            w |= {"mask": sb(marks, "mask", [P, NT, NE]), "ldiff": sb(marks, "ldiff", [P, NT, NE])}
            with ExitStack() as ctx:
                for k, n in (("qkv", C * 3 * E), ("gu", C * 2 * I), ("down", IC * E), ("router", C * NE)):
                    w[k + "_hi"], w[k + "_lo"] = sb(ctx, k + "_hi", [P, n], F32R), sb(ctx, k + "_lo", [P, n], F32R)
                w |= {"cos": sb(ctx, "cos", [P, N // P, D]), "sin": sb(ctx, "sin", [P, N // P, D]),
                      "ln_scale": sb(ctx, "ln_scale_col", [P, 1]), "ln_bias": sb(ctx, "ln_bias_col", [P, 1]),
                          "minus_half": sb(ctx, "minus_half", [P, 2 * HEADS])}
                split_weights(nc, dram, w)
                project(nc, dram, w)
            if upto > 1:
                list_tokens(nc, dram, w)
        if upto > 2:
            attend(nc, dram, w)
        if upto > 3:
            combine(nc, dram, w)


_INS = ["L0_attn_x", "L0_attn_w_qkv", "L0_attn_w_out", "L0_attn_ln_scale", "L0_attn_ln_bias", "L0_ffn_w_router",
        "L0_ffn_w_gate", "L0_ffn_w_up", "L0_ffn_w_down", "L0_ffn_w_sh_gate", "L0_ffn_w_sh_up", "L0_ffn_w_sh_down"]


def kernel(**inputs):
    import numpy as _np
    import concourse.bacc as _bacc
    from concourse.bass_utils import run_bass_kernel_spmd as _run

    nc = _bacc.Bacc("TRN2", target_bir_lowering=False, num_devices=1)
    arrays, args = {}, []
    for name in _INS:
        a = _np.ascontiguousarray(inputs[name].T if name == "L0_ffn_w_router" else inputs[name])
        arrays[f"in_{name}"] = a
        args.append(nc.dram_tensor(f"in_{name}", a.shape, mybir.dt.from_np(a.dtype), kind="ExternalInput").ap())
    args.append(nc.dram_tensor("out_0", (B, N, E), F32, kind="ExternalOutput").ap())
    build(nc, *args)
    r = _run(nc, [arrays], core_ids=[0])
    return r.results[0]["out_0"]
```

```python
import numpy as np
import concourse.bass as bass
from concourse import mybir
from contextlib import ExitStack

F32 = mybir.dt.float32
F32R = mybir.dt.float32r
U32 = mybir.dt.uint32
I32 = mybir.dt.int32
ALU = mybir.AluOpType
ACT = mybir.ActivationFunctionType
AX = mybir.AxisListType

P = 128
B, N, E = 4, 1024, 512
T = B * N
HEADS = 16
D = E // HEADS
C = E // P
GT = 512
TPG = GT // P
G = T // GT
NT = T // P
PAIRS = HEADS // 2
VW = D + 1
NE, TOPK, CAP = 64, 4, 64
I = 384
IC = I // P
XW = E + NE
EPS = 1e-5
NEVER = 3e38
ONE = 1


class Links:

    def __init__(self, eng, sem, base, passed):
        self.eng, self.sem, self.base, self.passed, self.n = eng, sem, base, passed, 0

    def __call__(self, ins, apart=False):
        self.n += 1
        ins.then_inc(self.sem, 1)
        self.eng.wait_ge(self.sem, self.base + self.n)
        if apart:
            self.eng.sem_inc(self.passed, 1)


def start_at_one(nc, sems):
    with nc.Block() as block:
        @block.sync
        def _(sp):
            for s in sems:
                sp.sem_inc(s, ONE)


def rope_tables():
    inv = (np.float32(1.0) / np.float32(10000.0) ** (np.arange(0, D, 2, dtype=np.float32) / np.float32(D))).astype(np.float32)
    t = (np.arange(N, dtype=np.float32)[:, None] * inv[None, :]).astype(np.float32)
    c, s = np.cos(t.astype(np.float64)), np.sin(t.astype(np.float64))
    cc = np.concatenate([c, c], 1).astype(np.float32)
    ss = np.concatenate([-s, s], 1).astype(np.float32)

    def lay(a):
        return np.ascontiguousarray(a.reshape(N // P, P, D).transpose(1, 0, 2))

    return lay(cc), lay(ss)


def prepare(nc, dram, w):
    parts = [("qkv", C, 3 * E), ("router", 1, C * NE), ("gu", C, 2 * I), ("down", IC, E)]
    with ExitStack() as ctx:
        down = ctx.enter_context(nc.sbuf_tensor("downcount_i", [P, 512], I32))
        full = {k: ctx.enter_context(nc.sbuf_tensor(f"full_{k}", [P, n * m], F32)) for k, n, m in parts}
        loaded = {k: [ctx.enter_context(nc.semaphore(f"w_loaded_{k}{c}")) for c in range(n)] for k, n, _ in parts}
        sem = lambda name: ctx.enter_context(nc.semaphore(name))
        counted = sem("down_counted")
        high_done, tables, made, x_loaded = sem("w_high_done"), sem("tables_loaded"), sem("constants_made"), sem("x0_loaded")
        order, var_ready, rstd_ready, bias_ready = sem("x0_order"), sem("x0_var_ready"), sem("x0_rstd_ready"), sem("x0_bias_ready")
        block = ctx.enter_context(nc.Block())

        def pieces():
            for k, n, m in parts:
                for c in range(n):
                    yield k, c, slice(c * m, (c + 1) * m)

        @block.sync
        def _(sp):
            sp.dma_start(w["x"][:], dram["x"].rearrange("(g j p) e -> g p j e", p=P, j=TPG)[0]).then_inc(x_loaded, 16)
            for k, c, cols in pieces():
                if k == "gu":
                    for two, name in enumerate(("w_sh_gate", "w_sh_up")):
                        sp.dma_start(full[k][:, cols][:, two * I:(two + 1) * I], dram[name][c * P:(c + 1) * P, :]).then_inc(loaded[k][c], 16)
                elif k == "router":
                    sp.dma_start(full[k][:].rearrange("p (c n) -> p c n", c=C), dram["router"].rearrange("(c p) n -> p c n", p=P)).then_inc(loaded[k][c], 16)
                else:
                    name = "w_qkv" if k == "qkv" else "w_sh_down"
                    sp.dma_start(full[k][:, cols], dram[name][c * P:(c + 1) * P, :]).then_inc(loaded[k][c], 16)
            sp.dma_start(w["cos"][:], dram["cos"]).then_inc(tables, 16)
            sp.dma_start(w["sin"][:], dram["sin"]).then_inc(tables, 16)
            for r in range(P // D):
                sp.dma_start(w["ln_scale"][r * D:(r + 1) * D, :], dram["ln_scale"].rearrange("(d a) -> d a", a=1)).then_inc(tables, 16)
                sp.dma_start(w["ln_bias"][r * D:(r + 1) * D, :], dram["ln_bias"].rearrange("(d a) -> d a", a=1)).then_inc(tables, 16)
            sp.wait_ge(tables, 16 * (2 + 2 * P // D))

        @block.scalar
        def _(act):
            for i, (k, c, cols) in enumerate(pieces()):
                if i == C - 1:
                    act.wait_ge(bias_ready, 1)
                    for j in range(TPG):
                        nc.scalar.activation(w["x"][:, j], w["x"][:, j], ACT.Identity, scale=w["xrstd"][:, j:j + 1], bias=w["xbias"][:, j:j + 1])
                act.wait_ge(loaded[k][c], 32 if k == "gu" else 16)
                nc.scalar.activation(w[k + "_hi"][:, cols], full[k][:, cols], ACT.Copy).then_inc(high_done, 1)

        @block.vector
        def _(dve):
            link = Links(dve, order, 0, None)
            dve.wait_ge(x_loaded, 16)
            for j in range(TPG):
                link(nc.vector.bn_stats(w["stats"][:, j], w["x"][:, j]))
                link(nc.vector.bn_aggr(w["mv"][:, j], w["stats"][:, j]))
            nc.vector.tensor_scalar(w["xneg"][:], w["mv"][:, :, 0], -1.0, None, ALU.mult)
            nc.vector.tensor_scalar(w["xvar"][:], w["mv"][:, :, 1], EPS, None, ALU.add).then_inc(var_ready, 1)
            for i, (k, c, cols) in enumerate(pieces()):
                dve.wait_ge(high_done, i + 1)
                nc.vector.tensor_tensor(w[k + "_lo"][:, cols], full[k][:, cols], w[k + "_hi"][:, cols].bitcast(F32), ALU.subtract)

        @block.gpsimd
        def _(pool):
            nc.gpsimd.memset(w["minus_half"][:], -0.5).then_inc(made, 1)
            nc.gpsimd.memset(w["ident"][:], 0.0).then_inc(made, 1)
            pool.wait_ge(made, 2)
            nc.gpsimd.affine_select(out=w["ident"][:], in_=w["ident"][:], compare_op=ALU.not_equal, fill=1.0,
                                    base=0, pattern=[[-1, P]], channel_multiplier=1)
            for h in range(2):
                nc.gpsimd.iota(down[h * NE:(h + 1) * NE, :], pattern=[[-1, 512]], base=T - h * T // 2,
                               channel_multiplier=0).then_inc(counted, 1)
                pool.wait_ge(counted, h + 1)
            nc.gpsimd.tensor_copy(w["down"][:], down[:])
            pool.wait_ge(var_ready, 1)
            nc.gpsimd.tensor_tensor(w["xrstd"][:], w["xvar"][:], w["minus_half"][:, 0:TPG], ALU.pow).then_inc(rstd_ready, 1)
            pool.wait_ge(rstd_ready, 1)
            nc.gpsimd.tensor_tensor(w["xbias"][:], w["xneg"][:], w["xrstd"][:], ALU.mult).then_inc(bias_ready, 1)


EIGHTS_BEFORE = 4


def find_eight(nc, w, r, link):
    key = w["mask"].rearrange("p t n -> p (t n)")
    eight = w["found"][:, 8 * r:8 * r + 8]
    link(nc.vector.max(eight, key))
    link(nc.vector.match_replace(out=key, in_to_replace=eight, in_values=key, imm_value=0.0))


def project(nc, dram, w):
    with ExitStack() as ctx:
        sb = lambda name, shape, dt=F32: ctx.enter_context(nc.sbuf_tensor(name, shape, dt))
        sems = []

        def sem(name):
            sems.append(ctx.enter_context(nc.semaphore(name)))
            return sems[-1]

        bank = lambda name: ctx.enter_context(nc.psum_tensor(name, [P, 512], F32))

        x, stats, mv, xvar, xneg, xrstd, xbias = (w[n] for n in ("x", "stats", "mv", "xvar", "xneg", "xrstd", "xbias"))
        xT_hi = sb("xT_hi", [P, C, GT], F32R)
        xT_lo = sb("xT_lo", [P, C, GT], F32R)
        rope = sb("rope_a", [P, 2 * E])
        rope_b = sb("rope_b", [P, 2 * E])
        cen = sb("centred", [P, 2 * E])
        y = sb("qk_normed", [P, 2 * E])
        hsum = sb("head_sum", [P, 2 * HEADS])
        hmean = sb("head_mean", [P, 2 * HEADS])
        hvar = sb("head_var", [P, 2 * HEADS])
        hrstd = sb("head_rstd", [P, 2 * HEADS])
        qkT = sb("qkT_full", [P, 2, C, P])
        qkT_hi = [sb(f"qkT_hi{u}", [P, 2, C, P], F32R) for u in range(2)]
        qkT_lo = [sb(f"qkT_lo{u}", [P, 2, C, P], F32R) for u in range(2)]
        v = sb("v_group", [P, PAIRS, TPG, 2, VW])
        sg = sb("sh_silu", [P, GT])
        hf = sb("sh_hidden", [P, GT])
        hT_hi = sb("sh_hT_hi", [P, IC, GT], F32R)
        hT_lo = sb("sh_hT_lo", [P, IC, GT], F32R)
        ffn = sb("sh_out", [P, TPG, E])
        lgT = sb("logitsT", [NE, GT])
        lg = sb("logits", [P, TPG, NE])
        top = sb("top8", [P, TPG, 8])
        unmarked = sb("logits_unmarked", [P, TPG, NE])

        TR = [bank("tr0"), bank("tr1")]
        QK = ctx.enter_context(nc.psum_tensor("qk", [P, 2 * E], F32))
        V = bank("v")
        GATE, UP, DN = bank("gate"), bank("up"), bank("down")
        DOWN = [DN, GATE, UP, DN]

        x_loaded, x_stored, x_transposed = sem("x_loaded"), sem("x_stored"), sem("x_transposed")
        var_ready, rstd_ready, bias_ready, xn_ready = sem("x_var_ready"), sem("x_rstd_ready"), sem("x_bias_ready"), sem("xn_ready")
        xT_high, xT_low = sem("xT_high"), sem("xT_low")
        qk_full, v_full, v_copied, v_stored, v_ones = sem("qk_full"), sem("v_full"), sem("v_copied"), sem("v_stored"), sem("v_ones")
        rope_parts, roped, centred, squared = sem("rope_parts"), sem("roped"), sem("centred"), sem("squared")
        hvar_ready, hrstd_ready, y_ready = sem("hvar_ready"), sem("hrstd_ready"), sem("y_ready")
        q_transposed, k_transposed = sem("q_transposed"), sem("k_transposed")
        q_copied, k_copied = sem("q_copied"), sem("k_copied")
        qkT_high, qkT_low, qkT_stored = sem("qkT_high"), sem("qkT_low"), [sem("qkT_stored0"), sem("qkT_stored1")]
        gate_full, up_full = sem("gate_full"), sem("up_full")
        silu_done, hidden_done, hidden_high, hidden_low = sem("silu_done"), sem("hidden_done"), sem("hidden_high"), sem("hidden_low")
        down_full, ffn_copied = sem("down_full"), sem("ffn_copied")
        ffn_stored = sem("ffn_stored")
        logitsT_full, logitsT_copied = sem("logitsT_full"), sem("logitsT_copied")
        logits_full, logits_copied = sem("logits_full"), sem("logits_copied")
        dve_order, passed = sem("dve_order"), sem("passed")
        marked, marks_paired, marks_turned, keyed = sem("marked"), sem("marks_paired"), sem("marks_turned"), sem("keyed")
        exp_done, marked_exp = sem("exp_done"), sem("marked_exp")
        pairs = ffn[:].rearrange("p j (a h n) -> p (j a) h n", h=2, n=NE)
        key = w["mask"].rearrange("p t n -> p (t n)")

        x_dram = dram["x"].rearrange("(g j p) e -> g p j e", p=P, j=TPG)
        xw_dram = dram["xw"].rearrange("(g j p) e -> g p j e", p=P, j=TPG)
        ffn_dram = dram["ffn"][0:T, :].rearrange("(g j p) e -> g p j e", p=P, j=TPG)
        qk_dram = [[dram[s][h].rearrange("(c p) n -> p c n", p=P) for h in range(2)] for s in ("qT", "kT")]

        start_at_one(nc, sems)
        block = ctx.enter_context(nc.Block())

        def groups(eng, first, body):
            first()
            with eng.Fori(0, G - 1) as g:
                body(g, True)
            body(G - 1, False)

        @block.sync
        def _(sp):
            def load_x(g):
                sp.dma_start(x[:], x_dram[bass.ds(g, 1)].rearrange("a p j e -> p (a j) e")).then_inc(x_loaded, 16)

            def store_xn(g):
                sp.wait_ge(xn_ready, ONE + g + 1)
                sp.dma_start(xw_dram[bass.ds(g, 1)].rearrange("a p j e -> p (a j) e")[:, :, 0:E], x[:]).then_inc(x_stored, 16)

            def store_qk(g, j):
                n = TPG * g + j
                sp.wait_ge(qkT_high, ONE + n + 1)
                sp.wait_ge(qkT_low, ONE + n + 1)
                for s in range(2):
                    for h, src in enumerate((qkT_hi, qkT_lo)):
                        sp.dma_start(qk_dram[s][h][:, :, bass.ds(n * P, P)], src[j % 2][:, s].bitcast(F32)).then_inc(qkT_stored[j % 2], 16)

            def body(g, has_next):
                if has_next:
                    sp.wait_ge(x_transposed, ONE + C * (g + 1))
                    sp.sem_inc(passed, 1)
                    sp.wait_ge(x_stored, ONE + 16 * (g + 1))
                    sp.sem_inc(passed, 1)
                    load_x(g + 1)
                store_qk(g, 0)
                store_qk(g, 1)
                if has_next:
                    store_xn(g + 1)
                sp.wait_ge(v_copied, ONE + TPG * (g + 1))
                sp.dma_start(dram["v"][bass.ds(g, 1)].rearrange("a q p n -> p (a q) n"),
                             v[:].rearrange("p q j h d -> p q (j h d)")).then_inc(v_stored, 16)
                store_qk(g, 2)
                sp.wait_ge(ffn_copied, ONE + TPG * (g + 1))
                sp.dma_start(ffn_dram[bass.ds(g, 1)].rearrange("a p j e -> p (a j) e"), ffn[:]).then_inc(ffn_stored, 16)
                store_qk(g, 3)

            def first():
                sp.sem_inc(x_loaded, 16)
                store_xn(0)

            groups(sp, first, body)
            sp.wait_ge(x_stored, ONE + 16 * G)
            for stored in qkT_stored:
                sp.wait_ge(stored, ONE + 16 * 4 * NT // 2)
            sp.wait_ge(v_stored, ONE + 16 * G)
            sp.wait_ge(ffn_stored, ONE + 16 * G)

        @block.gpsimd
        def _(pool):
            nc.gpsimd.memset(v[:], 1.0).then_inc(v_ones, 1)

            def x_rstd(g):
                pool.wait_ge(var_ready, ONE + g + 1)
                nc.gpsimd.tensor_tensor(xrstd[:], xvar[:], w["minus_half"][:, 0:TPG], ALU.pow).then_inc(rstd_ready, 1)
                pool.wait_ge(rstd_ready, ONE + g + 1)
                nc.gpsimd.tensor_tensor(xbias[:], xneg[:], xrstd[:], ALU.mult).then_inc(bias_ready, 1)

            def hidden_rest(g, j):
                pool.wait_ge(hidden_high, ONE + IC * g + j + 1)
                nc.gpsimd.tensor_tensor(hT_lo[:, j], hf[:], hT_hi[:, j].bitcast(F32), ALU.subtract).then_inc(hidden_low, 1)

            def body(g, has_next):
                for j in range(TPG):
                    n = TPG * g + j
                    pool.wait_ge(rope_parts, ONE + n + 1)
                    nc.gpsimd.tensor_tensor(rope[:], rope[:], rope_b[:], ALU.add).then_inc(roped, 1)
                    if 1 <= j < IC:
                        hidden_rest(g, j - 1)
                    pool.wait_ge(hvar_ready, ONE + n + 1)
                    nc.gpsimd.tensor_tensor(hrstd[:], hvar[:], w["minus_half"][:], ALU.pow).then_inc(hrstd_ready, 1)
                    if j == 0 and not has_next:
                        pool.wait_ge(exp_done, ONE + 1)
                        ex = w["ldiff"].rearrange("p (h t) n -> p t h n", h=2)
                        nc.gpsimd.tensor_tensor(ex, ex, pairs, ALU.mult).then_inc(marked_exp, 1)
                    if j == 2 and has_next:
                        x_rstd(g + 1)

            def first():
                pool.sem_inc(rstd_ready, 1)
                pool.sem_inc(bias_ready, 1)

            groups(pool, first, body)

        @block.scalar
        def _(act):
            def x_norm(g):
                act.wait_ge(bias_ready, ONE + g + 1)
                for j in range(TPG):
                    last = nc.scalar.activation(x[:, j], x[:, j], ACT.Identity, scale=xrstd[:, j:j + 1], bias=xbias[:, j:j + 1])
                last.then_inc(xn_ready, 1)

            def x_high(g, chunks):
                act.wait_ge(v_full, ONE + TPG * g)
                for c in chunks:
                    act.wait_ge(x_transposed, ONE + C * g + c + 1)
                    nc.scalar.activation(xT_hi[:, c], TR[c % 2][:], ACT.Copy).then_inc(xT_high, 1)

            def copy_logitsT(g):
                act.wait_ge(logitsT_full, ONE + g + 1)
                act.wait_ge(logits_full, ONE + g)
                nc.scalar.activation(lgT[:], TR[0][0:NE, :], ACT.Copy).then_inc(logitsT_copied, 1)

            def qk_out(g, j):
                n = TPG * g + j
                act.wait_ge(qkT_low, ONE + n)
                for s, full, copied in ((1, k_transposed, k_copied), (0, q_transposed, q_copied)):
                    act.wait_ge(full, ONE + n + 1)
                    nc.scalar.activation(qkT[:, s], TR[s][:].rearrange("p (c t) -> p c t", c=C), ACT.Identity,
                                         scale=w["ln_scale"][:, 0:1], bias=w["ln_bias"][:, 0:1]).then_inc(copied, 1)
                act.wait_ge(q_copied, ONE + n + 1)
                act.wait_ge(k_copied, ONE + n + 1)
                act.wait_ge(qkT_stored[j % 2], ONE + 16 * 4 * (2 * g + j // 2))
                nc.scalar.activation(qkT_hi[j % 2][:], qkT[:], ACT.Copy).then_inc(qkT_high, 1)

            def copy_out(g, j):
                act.wait_ge(down_full, ONE + TPG * g + j + 1)
                if j == 0:
                    act.wait_ge(ffn_stored, ONE + 16 * g)
                    if isinstance(g, int):
                        act.wait_ge(marked_exp, ONE + 1)
                nc.scalar.activation(ffn[:, j], DOWN[j][:], ACT.Copy).then_inc(ffn_copied, 1)

            def body(g, has_next):
                for j in range(TPG):
                    n, m = TPG * g + j, IC * g + j
                    if j == 0 and not has_next:
                        act.wait_ge(marked, ONE + 1)
                        act.wait_ge(ffn_stored, ONE + 16 * g)
                        by_half = w["mask"].rearrange("p (h t) n -> p t h n", h=2)
                        for q in range(4):
                            part = slice(4 * q, 4 * q + 4)
                            nc.scalar.activation(pairs[:, part], by_half[:, part], ACT.Copy).then_inc(marks_paired, 1)
                        nc.scalar.activation(w["ldiff"], w["ldiff"], ACT.Exp).then_inc(exp_done, 1)
                    act.wait_ge(v_full, ONE + n + 1)
                    if j == 0:
                        act.wait_ge(v_ones, ONE + 1)
                        act.wait_ge(v_stored, ONE + 16 * g)
                    nc.scalar.activation(v[:, :, j, :, 0:D], V[:].rearrange("p (q h d) -> p q h d", q=PAIRS, h=2),
                                         ACT.Copy).then_inc(v_copied, 1)
                    if j < IC:
                        act.wait_ge(gate_full, ONE + m + 1)
                        act.wait_ge(hidden_done, ONE + m)
                        nc.scalar.activation(sg[:], GATE[:], ACT.Silu).then_inc(silu_done, 1)
                    else:
                        if has_next:
                            x_norm(g + 1)
                        qk_out(g, 2)
                    act.wait_ge(centred, ONE + n + 1)
                    nc.scalar.activation(rope_b[:], cen[:], ACT.Square).then_inc(squared, 1)
                    if j < IC:
                        act.wait_ge(hidden_done, ONE + m + 1)
                        act.wait_ge(down_full, ONE + TPG * g)
                        nc.scalar.activation(hT_hi[:, j], hf[:], ACT.Copy).then_inc(hidden_high, 1)
                        if j >= 1:
                            qk_out(g, j - 1)
                copy_out(g, 0)
                if has_next:
                    x_high(g + 1, (0, 1))
                copy_out(g, 1)
                copy_out(g, 2)
                if has_next:
                    x_high(g + 1, (2, 3))
                copy_out(g, 3)
                if has_next:
                    copy_logitsT(g + 1)
                qk_out(g, 3)

            def first():
                act.sem_inc(xn_ready, 1)
                x_high(0, range(C))
                copy_logitsT(0)

            groups(act, first, body)

        @block.vector
        def _(dve):
            def x_stats(g, tiles, link):
                for j in tiles:
                    if j == 0:
                        dve.wait_ge(x_loaded, ONE + 16 * (g + 1))
                    link(nc.vector.bn_stats(stats[:, j], x[:, j]), apart=True)
                    link(nc.vector.bn_aggr(mv[:, j], stats[:, j]))
                if 3 in tiles:
                    nc.vector.tensor_scalar(xneg[:], mv[:, :, 0], -1.0, None, ALU.mult)
                    nc.vector.tensor_scalar(xvar[:], mv[:, :, 1], EPS, None, ALU.add).then_inc(var_ready, 1)

            def x_low(g, chunks):
                for c in chunks:
                    dve.wait_ge(xT_high, ONE + C * g + c + 1)
                    nc.vector.tensor_tensor(xT_lo[:, c], TR[c % 2][:], xT_hi[:, c].bitcast(F32),
                                            ALU.subtract).then_inc(xT_low, 1)

            def route(g, link):
                dve.wait_ge(logits_full, ONE + g + 1)
                nc.vector.tensor_copy(lg[:], TR[1][:, 0:TPG * NE].rearrange("p (j n) -> p j n", j=TPG)).then_inc(logits_copied, 1)
                dve.wait_ge(logits_copied, ONE + g + 1)
                dve.sem_inc(passed, 1)
                for j in range(TPG):
                    last = nc.vector.max(top[:, j], lg[:, j])
                link(last)
                link(nc.vector.memset(top[:, :, TOPK:], NEVER), apart=True)
                for j in range(TPG):
                    last = nc.vector.match_replace(out=unmarked[:, j], in_to_replace=top[:, j], in_values=lg[:, j], imm_value=-NEVER)
                link(last)
                nc.vector.tensor_tensor(w["mask"][:, bass.ds(TPG * g, TPG), :], unmarked[:], lg[:], ALU.not_equal)
                last = nc.vector.tensor_tensor(w["ldiff"][:, bass.ds(TPG * g, TPG), :], lg[:],
                                               top[:, :, 0:1].broadcast_to([P, TPG, NE]), ALU.subtract)
                if isinstance(g, int):
                    last.then_inc(marked, 1)

            def keys(q):
                dve.wait_ge(marks_turned, ONE + q + 1)
                if q == 0:
                    dve.wait_ge(marks_paired, ONE + 4)
                part = key[:, q * 512:(q + 1) * 512]
                nc.vector.scalar_tensor_tensor(out=part, in0=w["down"][:], scalar=-512.0 * q, in1=DN[:],
                                               op0=ALU.add, op1=ALU.mult).then_inc(keyed, 1)
                if q == 3:
                    dve.wait_ge(keyed, ONE + 4)


            heads = lambda t: t[:].rearrange("p (h d) -> p h d", d=D)
            wide = lambda t: t[:].unsqueeze(2).broadcast_to([P, 2 * HEADS, D])
            half = D // 2

            def rotate(g, j):
                n = TPG * g + j
                dve.wait_ge(qk_full, ONE + n + 1)
                place = bass.ds(n % (N // P), 1)
                cos = w["cos"][:, place, :].broadcast_to([P, 2 * HEADS, D])
                sin = w["sin"][:, place, :].broadcast_to([P, 2 * HEADS, D])
                q = heads(QK)
                nc.vector.tensor_tensor(heads(rope), q, cos, ALU.mult)
                nc.vector.tensor_tensor(heads(rope_b)[:, :, 0:half], q[:, :, half:D], sin[:, :, 0:half], ALU.mult)
                nc.vector.tensor_tensor(heads(rope_b)[:, :, half:D], q[:, :, 0:half], sin[:, :, half:D],
                                        ALU.mult).then_inc(rope_parts, 1)

            def centre(g, j, link):
                dve.wait_ge(roped, ONE + TPG * g + j + 1)
                link(nc.vector.tensor_reduce(hsum[:], heads(rope), AX.X, ALU.add))
                link(nc.vector.tensor_scalar(hmean[:], hsum[:], 1.0 / D, None, ALU.mult))
                nc.vector.tensor_tensor(heads(cen), heads(rope), wide(hmean), ALU.subtract).then_inc(centred, 1)

            def variance(g, j, link):
                dve.wait_ge(squared, ONE + TPG * g + j + 1)
                link(nc.vector.tensor_reduce(hsum[:], heads(rope_b), AX.X, ALU.add))
                nc.vector.tensor_scalar(hvar[:], hsum[:], 1.0 / D, EPS, ALU.mult, ALU.add).then_inc(hvar_ready, 1)

            def norm(g, j):
                n = TPG * g + j
                dve.wait_ge(hrstd_ready, ONE + n + 1)
                dve.wait_ge(q_transposed, ONE + n)
                nc.vector.tensor_tensor(heads(y), heads(cen), wide(hrstd), ALU.mult).then_inc(y_ready, 1)

            def qk_low(g, j):
                n = TPG * g + j
                dve.wait_ge(qkT_high, ONE + n + 1)
                dve.wait_ge(qkT_stored[j % 2], ONE + 16 * 4 * (2 * g + j // 2))
                nc.vector.tensor_tensor(qkT_lo[j % 2][:], qkT[:], qkT_hi[j % 2][:].bitcast(F32), ALU.subtract).then_inc(qkT_low, 1)

            def hidden(g, j):
                m = IC * g + j
                dve.wait_ge(silu_done, ONE + m + 1)
                dve.wait_ge(up_full, ONE + m + 1)
                dve.wait_ge(hidden_low, ONE + m)
                nc.vector.tensor_tensor(hf[:], sg[:], UP[:], ALU.mult).then_inc(hidden_done, 1)

            ROUTE_LINKS = 3
            GROUP_LINKS = 2 * TPG + ROUTE_LINKS + 3 * TPG

            def body(g, has_next):
                link = Links(dve, dve_order, ONE + GROUP_LINKS * g, passed)
                for j in range(TPG):
                    if j == 0 and not has_next:
                        route(g, link)
                    rotate(g, j)
                    if j >= 1:
                        norm(g, j - 1)
                    if j >= 2:
                        qk_low(g, j - 2)
                    if not has_next and j in (1, 2):
                        keys(2 * (j - 1))
                    centre(g, j, link)
                    variance(g, j, link)
                    if j < IC:
                        hidden(g, j)
                    if j == 0 and has_next:
                        route(g, link)
                    if j == 1 and has_next:
                        x_stats(g + 1, (0, 1), link)
                    if j == 1 and not has_next:
                        keys(1)
                    if j == 2:
                        if has_next:
                            x_stats(g + 1, (2, 3), link)
                        dve.wait_ge(hidden_high, ONE + IC * (g + 1))
                        nc.vector.tensor_tensor(hT_lo[:, j], hf[:], hT_hi[:, j].bitcast(F32), ALU.subtract).then_inc(hidden_low, 1)
                        if not has_next:
                            keys(3)
                            find_eight(nc, w, 0, link)
                qk_low(g, 2)
                if has_next:
                    x_low(g + 1, (0, 1))
                    x_low(g + 1, (2, 3))
                else:
                    find_eight(nc, w, 1, link)
                norm(g, 3)
                qk_low(g, 3)
                if not has_next:
                    for r in range(2, EIGHTS_BEFORE):
                        find_eight(nc, w, r, link)
                if has_next:
                    assert link.n == GROUP_LINKS, link.n

            def first():
                dve.sem_inc(var_ready, 1)
                x_low(0, range(C))

            groups(dve, first, body)

        @block.tensor
        def _(pe):
            def three(out, hi, lo, w_hi, w_lo, start, stop):
                nc.tensor.matmul(out, hi, w_hi, start=start, stop=False)
                nc.tensor.matmul(out, hi, w_lo, start=False, stop=False)
                return nc.tensor.matmul(out, lo, w_hi, start=False, stop=stop)

            def transposes_x(g, chunks):
                pe.wait_ge(xn_ready, ONE + g + 1)
                for c in chunks:
                    if c < 2:
                        if not (isinstance(g, int) and g == 0):
                            pe.wait_ge((q_copied, k_copied)[c], ONE + TPG * g - 1)
                    else:
                        pe.wait_ge(xT_low, ONE + C * g + c - 1)
                    for j in range(TPG):
                        last = nc.tensor.transpose(TR[c % 2][:, j * P:(j + 1) * P], x[:, j, c * P:(c + 1) * P], w["ident"][:])
                    last.then_inc(x_transposed, 1)

            wr = [w["router_" + s][:].rearrange("p (c n) -> p c n", c=C) for s in ("hi", "lo")]
            wq = [w["qkv_" + s][:].rearrange("p (c k n) -> p c k n", c=C, k=3) for s in ("hi", "lo")]
            wg = [w["gu_" + s][:].rearrange("p (c two n) -> p c two n", c=C, two=2) for s in ("hi", "lo")]
            wd = [w["down_" + s][:].rearrange("p (c n) -> p c n", c=IC) for s in ("hi", "lo")]

            def logitsT(g):
                pe.wait_ge(xT_low, ONE + C * (g + 1))
                for c in range(C):
                    last = three(TR[0][0:NE, :], wr[0][:, c], wr[1][:, c], xT_hi[:, c], xT_lo[:, c], c == 0, c == C - 1)
                last.then_inc(logitsT_full, 1)

            def logits(g):
                pe.wait_ge(k_copied, ONE + TPG * g)
                pe.wait_ge(logitsT_copied, ONE + g + 1)
                pe.sem_inc(passed, 1)
                for j in range(TPG):
                    last = nc.tensor.transpose(TR[1][:, j * NE:(j + 1) * NE], lgT[:, j * P:(j + 1) * P], w["ident"][0:NE, 0:NE])
                last.then_inc(logits_full, 1)

            def qkv(g, j):
                n = TPG * g + j
                pe.wait_ge(xT_low, ONE + C * (g + 1))
                pe.wait_ge(rope_parts, ONE + n)
                for k in range(3):
                    if k == 2:
                        pe.wait_ge(v_copied, ONE + n)
                    out = QK[:, k * E:(k + 1) * E] if k < 2 else V[:]
                    for c in range(C):
                        t = slice(j * P, (j + 1) * P)
                        last = three(out, xT_hi[:, c, t], xT_lo[:, c, t], wq[0][:, c, k], wq[1][:, c, k], c == 0, c == C - 1)
                    if k > 0:
                        last.then_inc((qk_full, v_full)[k - 1], 1)

            def gate_up(g, m):
                t = slice(m * P, (m + 1) * P)
                if m == 0:
                    pe.wait_ge(ffn_copied, ONE + TPG * g)
                for k, (out, full, free) in enumerate(((GATE, gate_full, silu_done), (UP, up_full, hidden_done))):
                    pe.wait_ge(free, ONE + IC * g + m)
                    for c in range(C):
                        nc.tensor.matmul(out[:], wg[0][:, c, k, t], xT_hi[:, c], start=(c == 0), stop=False)
                        nc.tensor.matmul(out[:], wg[0][:, c, k, t], xT_lo[:, c], start=False, stop=False)
                        last = nc.tensor.matmul(out[:], wg[1][:, c, k, t], xT_hi[:, c], start=False, stop=(c == C - 1))
                    last.then_inc(full, 1)

            def qk_transposes(g, j, has_next):
                n = TPG * g + j
                pe.wait_ge(y_ready, ONE + n + 1)
                pe.wait_ge(k_copied, ONE + n)
                if j == 0:
                    pe.wait_ge(logits_copied, ONE + g + 1)
                if j == 3 and has_next:
                    pe.wait_ge(xT_low, ONE + C * (g + 2))
                for c in range(C):
                    last = nc.tensor.transpose(TR[1][:, c * P:(c + 1) * P], y[:, E + c * P:E + (c + 1) * P], w["ident"][:])
                last.then_inc(k_transposed, 1)
                pe.wait_ge(q_copied, ONE + n)
                if j == 0:
                    pe.wait_ge(logitsT_copied, ONE + g + 1)
                if j == 3 and has_next:
                    pe.wait_ge(logitsT_copied, ONE + g + 2)
                for c in range(C):
                    last = nc.tensor.transpose(TR[0][:, c * P:(c + 1) * P], y[:, c * P:(c + 1) * P], w["ident"][:])
                last.then_inc(q_transposed, 1)

            def down(g, j):
                if j == 0:
                    pe.wait_ge(hidden_low, ONE + IC * (g + 1))
                    if isinstance(g, int):
                        pe.wait_ge(keyed, ONE + 4)
                    pe.wait_ge(ffn_copied, ONE + TPG * g)
                elif j == 1:
                    pe.wait_ge(silu_done, ONE + IC * (g + 1))
                elif j == 2:
                    pe.wait_ge(hidden_done, ONE + IC * (g + 1))
                else:
                    pe.wait_ge(ffn_copied, ONE + TPG * g + 1)
                t = slice(j * P, (j + 1) * P)
                for c in range(IC):
                    last = three(DOWN[j][:], hT_hi[:, c, t], hT_lo[:, c, t], wd[0][:, c], wd[1][:, c], c == 0, c == IC - 1)
                last.then_inc(down_full, 1)

            def turn_marks(q):
                pe.wait_ge(marks_paired, ONE + q + 1)
                if q == 0:
                    pe.wait_ge(ffn_copied, ONE + TPG * (G - 1))
                else:
                    pe.wait_ge(keyed, ONE + q)
                for t in range(4):
                    last = nc.tensor.transpose(DN[:, t * P:(t + 1) * P], pairs[:, 4 * q + t].rearrange("p h n -> p (h n)"), w["ident"][:])
                last.then_inc(marks_turned, 1)

            def body(g, has_next):
                for j in range(TPG):
                    if j == 0 and not has_next:
                        logits(g)
                    qkv(g, j)
                    if j == 0 and has_next:
                        logits(g)
                    if j == 2 and not has_next:
                        turn_marks(2)
                    if j < IC:
                        gate_up(g, j)
                        if not has_next:
                            turn_marks((0, 1, 3)[j])
                    else:
                        down(g, 0)
                    if j >= 1:
                        qk_transposes(g, j - 1, has_next)
                if has_next:
                    transposes_x(g + 1, (0, 1))
                down(g, 1)
                down(g, 2)
                if has_next:
                    transposes_x(g + 1, (2, 3))
                down(g, 3)
                if has_next:
                    logitsT(g + 1)
                qk_transposes(g, 3, has_next)

            def first():
                transposes_x(0, range(C))
                logitsT(0)

            groups(pe, first, body)


def list_tokens(nc, dram, w):
    with ExitStack() as ctx:
        sb = lambda name, shape, dt=F32: ctx.enter_context(nc.sbuf_tensor(name, shape, dt))
        sem = lambda name: ctx.enter_context(nc.semaphore(name))
        total, rtotal = sb("weight_total", [P, NT]), sb("weight_rtotal", [P, NT])
        wide = lambda t: t[:].unsqueeze(2).broadcast_to([P, NT, NE])
        found = w["found"]
        both = sb("found_both", [NE, 2 * CAP])
        first = sb("first", [NE, CAP])
        token = sb("token", [CAP, NE])
        empty = sb("empty", [CAP, NE])
        slot_i, slot = sb("slot_i", [CAP, 1], I32), sb("slot", [CAP, 1])
        zeros = sb("zero_rows", [CAP, E])
        wo, sel = sb("w_out_full", [P, C, E]), sb("sel_full", [4 * HEADS, C, P])
        lists = ctx.enter_context(nc.psum_tensor("lists", [P, 512], F32))

        counted, weights_done = sem("counted"), sem("weights_done")
        first_done, lists_turned, zeroed, stored, order = sem("first_done"), sem("lists_turned"), sem("zeroed"), sem("rows_stored"), sem("order")
        wo_loaded, wo_high = sem("w_out_loaded"), sem("w_out_high")
        totalled, divided = sem("totalled"), sem("divided")
        start_at_one(nc, [*w["qkv_loaded"], *w["gu_loaded"], w["d_loaded"]])
        block = ctx.enter_context(nc.Block())

        @block.gpsimd
        def _(pool):
            nc.gpsimd.memset(zeros[:], 0.0).then_inc(zeroed, 1)
            nc.gpsimd.iota(slot_i[:], pattern=[[1, 1]], base=0, channel_multiplier=1).then_inc(counted, 1)
            nc.gpsimd.memset(sel[:], 0.0).then_inc(counted, 1)
            pool.wait_ge(counted, 2)
            for h in range(2):
                part = sel[2 * HEADS * h:2 * HEADS * (h + 1)].rearrange("r c (g d) -> r c g d", d=D)
                nc.gpsimd.affine_select(out=part, in_=part, compare_op=ALU.not_equal, fill=1.0, base=0,
                                        pattern=[[-4, C], [-1, P // D], [0, D]], channel_multiplier=1).then_inc(counted, 1)
                pool.wait_ge(counted, 3 + h)
            nc.gpsimd.tensor_copy(w["sel"][:], sel[:])
            pool.wait_ge(divided, 1)
            nc.gpsimd.tensor_tensor(w["ldiff"], w["ldiff"], wide(rtotal), ALU.mult).then_inc(weights_done, 1)
            pool.wait_ge(wo_high, 1)
            nc.gpsimd.tensor_tensor(w["wo_lo"][:], wo[:], w["wo_hi"][:].bitcast(F32), ALU.subtract)

        @block.tensor
        def _(pe):
            pe.wait_ge(first_done, 1)
            nc.tensor.transpose(lists[0:CAP, 0:NE], first[:], w["ident"][0:NE, 0:NE]).then_inc(lists_turned, 1)

        @block.scalar
        def _(act):
            act.wait_ge(wo_loaded, 16)
            nc.scalar.activation(w["wo_hi"][:], wo[:], ACT.Copy).then_inc(wo_high, 1)

        @block.vector
        def _(dve):
            link = Links(dve, order, 0, None)
            nc.vector.tensor_reduce(total[:], w["ldiff"], AX.X, ALU.add).then_inc(totalled, 1)
            dve.wait_ge(totalled, 1)
            nc.vector.reciprocal(rtotal[:], total[:]).then_inc(divided, 1)
            for r in range(EIGHTS_BEFORE, CAP // 8):
                find_eight(nc, w, r, link)
            nc.vector.tensor_copy(both[:, 0:CAP], found[0:NE, :])
            link(nc.vector.tensor_copy(both[:, CAP:], found[NE:, :]))
            for r in range(CAP // 8):
                eight = first[:, 8 * r:8 * r + 8]
                ins = nc.vector.max(eight, both[:])
                if r == CAP // 8 - 1:
                    ins.then_inc(first_done, 1)
                else:
                    link(ins)
                    link(nc.vector.match_replace(out=both[:], in_to_replace=eight, in_values=both[:], imm_value=0.0))
            dve.wait_ge(lists_turned, 1)
            link(nc.vector.tensor_scalar(token[:], lists[0:CAP, 0:NE], -1.0, float(T), ALU.mult, ALU.add))
            dve.wait_ge(counted, 1)
            link(nc.vector.tensor_copy(slot[:], slot_i[:]))
            link(nc.vector.tensor_scalar(empty[:], token[:], float(T), slot[:, 0:1], ALU.is_equal, ALU.mult))
            nc.vector.tensor_tensor(w["scatter_to"][:], token[:], empty[:], ALU.add)
            two = token[:].rearrange("s (q h) -> s h q", h=2)
            for h in range(2):
                last = nc.vector.tensor_scalar(w["gather_from"][h * CAP:(h + 1) * CAP, 0:NE // 2], two[:, h], float(T - 1), None, ALU.min)
            link(last)
            nc.vector.tensor_copy(w["gather_from"][:, NE // 2:], w["gather_from"][:, 0:1])

        @block.sync
        def _(sp):
            sp.dma_start(wo[:], dram["w_out"].rearrange("(c p) n -> p c n", p=P)).then_inc(wo_loaded, 16)
            load_qkv(sp, dram, w, 0, 0, 0)
            load_experts(sp, dram, w["wg"][0], "w_gate", C, 0, w["gu_loaded"][0])
            sp.wait_ge(zeroed, 1)
            sp.dma_start(dram["ffn"][T:, :], zeros[:]).then_inc(stored, 16)
            sp.wait_ge(weights_done, 1)
            sp.dma_start(dram["xw"].rearrange("(t p) e -> p t e", p=P)[:, :, E:], w["ldiff"]).then_inc(stored, 16)
            load_experts(sp, dram, w["wu"][0], "w_up", C, 0, w["gu_loaded"][0])
            load_experts(sp, dram, w["wd"], "w_down", IC, 0, w["d_loaded"])
            sp.wait_ge(stored, 32)


def attend_buffers(nc, ctx):
    sb = lambda name, shape, dt=F32: ctx.enter_context(nc.sbuf_tensor(name, shape, dt))
    sem = lambda name: ctx.enter_context(nc.semaphore(name))
    two = lambda f: [f(0), f(1)]
    return {
        "qs": two(lambda u: sb(f"q_stack{u}", [3 * D, 2, N], F32R)),
        "ks": two(lambda u: sb(f"k_stack{u}", [3 * D, 2, N], F32R)),
        "vs": two(lambda u: sb(f"v_pair{u}", [P, N // P, 2 * VW])),
        "wg": two(lambda u: sb(f"w_gate{u}", [P, 2, C, I])),
        "wu": two(lambda u: sb(f"w_up{u}", [P, 2, C, I])),
        "wd": sb("w_down", [P, 2, IC, E]),
        "sel": sb("sel", [4 * HEADS, C, P], F32R),
        "wo_hi": sb("w_out_hi", [P, C, E], F32R), "wo_lo": sb("w_out_lo", [P, C, E], F32R),
        "qkv_loaded": two(lambda u: sem(f"qkv_loaded{u}")),
        "gu_loaded": two(lambda u: sem(f"gate_up_loaded{u}")), "d_loaded": sem("down_loaded"),
    }


def load_qkv(sp, dram, w, b, i, u):
    for h in range(2):
        row = (2 * (2 * i + u) + h) * D
        for name, dst, parts in (("qT", w["qs"], (0, 0, 1)), ("kT", w["ks"], (0, 1, 0))):
            for g, part in enumerate(parts):
                sp.dma_start(dst[u][g * D:(g + 1) * D, h].bitcast(F32),
                             dram[name][part, bass.ds(row, D), bass.ds(b * N, N)]).then_inc(w["qkv_loaded"][u], 16)
    for half in range(2):
        sp.dma_start(w["vs"][u][:, half * TPG:(half + 1) * TPG].rearrange("p j n -> p (j n)"),
                     dram["v"][bass.ds(2 * b + half, 1), bass.ds(2 * i + u, 1)].rearrange("a q p n -> p (a q n)")).then_inc(w["qkv_loaded"][u], 16)


def load_experts(sp, dram, dst, name, chunks, it, loaded):
    sp.dma_start(dst[:].rearrange("p e c n -> p e (c n)"),
                 dram[name].rearrange("(q e) (p c) n -> q p e (c n)", e=2, c=chunks)[bass.ds(it, 1)].rearrange("a p e n -> p (a e) n")).then_inc(loaded, 16)


def attend(nc, dram, w):
    EP = NE // 2
    with ExitStack() as ctx:
        sb = lambda name, shape, dt=F32: ctx.enter_context(nc.sbuf_tensor(name, shape, dt))
        sems = []

        def sem(name):
            sems.append(ctx.enter_context(nc.semaphore(name)))
            return sems[-1]

        two = lambda f: [f(0), f(1)]
        qs, ks, vs, wg, wu, wd = (w[x] for x in ("qs", "ks", "vs", "wg", "wu", "wd"))
        wo_hi, wo_lo, sel, oT = w["wo_hi"], w["wo_lo"], w["sel"], w["oT"]
        qkv_loaded, gu_loaded, d_loaded = w["qkv_loaded"], w["gu_loaded"], w["d_loaded"]
        a = two(lambda h: two(lambda r: sb(f"probs{h}{r}", [P, N])))
        o_raw = two(lambda u: sb(f"o_raw{u}", [P, N]))
        den, rden = sb("den", [2 * HEADS, N]), sb("rden", [2 * HEADS, N])
        rden_parts = sb("rden_parts", [4 * HEADS, N], F32R)
        on_hi, on_lo = sb("on_hi", [P, TPG, C, P], F32R), sb("on_lo", [P, TPG, C, P], F32R)
        gi = two(lambda u: sb(f"gather_now{u}", [P, 1], U32))
        si = two(lambda u: sb(f"scatter_now{u}", [CAP, 2], U32))
        wt = two(lambda u: sb(f"weight_now{u}", [P, 1]))
        xg = two(lambda u: sb(f"x_rows{u}", [P, XW]))
        xgT = sb("x_rowsT", [P, C, P])
        esg, eh = sb("e_silu", [P, I]), sb("e_hidden", [P, I])
        ehT = sb("e_hiddenT", [P, IC, P])
        ey = two(lambda u: sb(f"e_out{u}", [P, E]))
        s_out = two(lambda u: sb(f"s_out{u}", [P, E]))

        S = two(lambda h: ctx.enter_context(nc.psum_tensor(f"scores{h}", [P, N], F32)))
        O = ctx.enter_context(nc.psum_tensor("o_acc", [P, N], F32))
        P1 = ctx.enter_context(nc.psum_tensor("e_bank1", [P, 512], F32))
        P2 = ctx.enter_context(nc.psum_tensor("e_bank2", [P, 512], F32))

        s_full, squared = two(lambda h: sem(f"scores_full{h}")), two(lambda h: sem(f"squared{h}"))
        masked, a_ready = two(lambda h: sem(f"masked{h}")), two(lambda h: sem(f"probs_ready{h}"))
        o_copied, den_loaded = sem("o_copied"), sem("den_loaded")
        index_ready, x_gathered = sem("index_ready"), two(lambda u: sem(f"x_gathered{u}"))
        xgT_full, xgT_copied = sem("x_rowsT_full"), sem("x_rowsT_copied")
        e_gate_full, e_silu_done, e_hidden_done = sem("e_gate_full"), sem("e_silu_done"), sem("e_hidden_done")
        ehT_full, ehT_copied, ey_full, ey_ready, scattered = sem("e_hT_full"), sem("e_hT_copied"), sem("e_out_full"), sem("e_out_ready"), sem("scattered")
        rden_high, rden_low, spread, normed, on_high, on_low_done = sem("rden_high"), sem("rden_low"), sem("rden_spread"), sem("o_normed"), sem("on_high"), sem("on_low_done")
        o_full_u, o_moved_u, e_up_u = two(lambda u: sem(f"o_full{u}")), two(lambda u: sem(f"o_moved{u}")), two(lambda u: sem(f"e_up_full{u}"))
        s_ready, s_copied, s_stored = sem("s_full"), sem("s_copied"), two(lambda u: sem(f"s_stored{u}"))
        set_loaded, set_stored = [sem(f"set_loaded{q}") for q in range(5)], [sem(f"set_stored{q}") for q in range(5)]
        gated, pool_product, pool_done, dve_product, dve_done = (sem(x) for x in ("gated", "pool_product", "pool_done", "dve_product", "dve_done"))
        passed, made, weight_ready, rden_done = sem("attend_passed"), sem("made"), sem("weight_ready"), sem("rden_done")
        start_at_one(nc, [s for s in sems if s not in (scattered, *x_gathered)])
        block = ctx.enter_context(nc.Block())

        NK = N // P
        RP = 4

        def pieces(j):
            return [(P * j, 512), (512, N)] if P * j < 512 else [(P * j, N)]

        STEPS, OWN = NT // 2, (NT - NK) // 2
        POOLS = 8
        sets = [t[:].rearrange("p e c n -> p (e c n)") for t in (wg[0], wu[0], wg[1], wu[1], wd)]
        SETS = len(sets)
        last_s = [a[0][0], a[0][1], a[1][0], a[1][1]]

        def operands(n):
            x, s_, f = (sets[n % SETS][:, 2 * E * i:2 * E * (i + 1)] for i in range(3))
            return x, (last_s[n - OWN][:] if n >= OWN else s_), f

        def step_rows(name, n, tile):
            rows = dram[name][2 * P * n:2 * P * (n + 1), :]
            if n < OWN:
                return rows.rearrange("(p w) e -> p (w e)", w=2), tile
            return rows.rearrange("(w p) e -> p w e", w=2), tile.rearrange("p (w e) -> p w e", w=2)

        def loads_of(n):
            return sum(2 if m >= OWN else 3 for m in range(n % SETS, n + 1, SETS))

        def combine(eng, engine, n, product, done):
            k = n if n < POOLS else n - POOLS
            x, s_, f = operands(n)
            eng.wait_ge(gated, ONE + n + 1)
            if n >= OWN:
                eng.wait_ge(s_copied, ONE + NT - NK + 2 * (n - OWN) + 2)
            engine.tensor_tensor(s_, s_, f, ALU.mult).then_inc(product, 1)
            eng.wait_ge(product, ONE + k + 1)
            engine.tensor_tensor(s_, s_, x, ALU.add).then_inc(done, 1)

        def others(eng, b, pair):
            pair(b, 0, 1)
            with eng.Fori(1, PAIRS // 2) as i:
                for u in range(2):
                    pair(b, i, u)

        def loop(eng, pair, sequence):
            pair(0, 0, 0)
            with eng.Fori(0, B - 1) as b:
                others(eng, b, pair)
                pair(b + 1, 0, 0)
                sequence(b, False)
            others(eng, B - 1, pair)
            sequence(B - 1, True)

        def numbers(b, i, u):
            start = isinstance(i, int) and i == 0 and u == 0
            first = start and isinstance(b, int)
            return 8 * b + 2 * i + u, 4 * b + i, first, start and not first

        @block.sync
        def _(sp):
            def load_down(it):
                sp.wait_ge(ey_full, ONE + it)
                load_experts(sp, dram, wd, "w_down", IC, it, d_loaded)

            def load(b, i, u):
                it, k, _, _ = numbers(b, i, u)
                sp.wait_ge(o_full_u[u], ONE + k)
                load_qkv(sp, dram, w, b, i, u)
                sp.wait_ge(e_up_u[u], ONE + k)
                load_experts(sp, dram, wg[u], "w_gate", C, it, gu_loaded[u])
                load_experts(sp, dram, wu[u], "w_up", C, it, gu_loaded[u])
                load_down(it)

            def move(b, i, u):
                it, k, _, _ = numbers(b, i, u)
                sp.wait_ge(o_copied, ONE + 2 * (it + 1))
                for h in range(2):
                    r = 2 * u + h
                    sp.dma_start(oT[r * D:(r + 1) * D, bass.ds(i, 1)].rearrange("p a n -> p (a n)"),
                                 o_raw[u][64 * h:64 * h + D]).then_inc(o_moved_u[u], 16)
                    sp.dma_start(dram["den"][bass.ds(b, 1), bass.ds(4 * i + r, 1)].rearrange("a h n -> (a h) n"),
                                 o_raw[u][64 * h + D:64 * h + VW]).then_inc(o_moved_u[u], 16)

            def load_denominators(b):
                for u in range(2):
                    sp.wait_ge(o_moved_u[u], ONE + 64 * 4 * (b + 1))
                sp.wait_ge(rden_done, ONE + RP * b)
                sp.dma_start(den[0:HEADS], dram["den"][bass.ds(b, 1)].rearrange("a h n -> (a h) n")).then_inc(den_loaded, 16)

            def store_s(b):
                for t in range(NK):
                    sp.wait_ge(s_copied, ONE + NK * b + t + 1)
                    sp.dma_start(dram["s"][bass.ds(b * N + t * P, P), :], s_out[t % 2][:]).then_inc(s_stored[t % 2], 16)

            def rest(b):
                sp.wait_ge(on_low_done, ONE + 2 * C * b)
                move(b, 0, 0)
                with sp.Fori(1, PAIRS // 2) as i:
                    for u in range(2):
                        load(b, i, u)
                        move(b, i - 1 + u, 1 - u)

            sp.wait_ge(x_gathered[0], 16)
            load_qkv(sp, dram, w, 0, 0, 1)
            load_experts(sp, dram, wg[1], "w_gate", C, 1, gu_loaded[1])
            load_experts(sp, dram, wu[1], "w_up", C, 1, gu_loaded[1])
            load_down(1)
            with sp.Fori(0, B - 1) as b:
                rest(b)
                load(b + 1, 0, 0)
                move(b, PAIRS // 2 - 1, 1)
                load_denominators(b)
                load(b + 1, 0, 1)
                store_s(b)
            rest(B - 1)

            def load_step(n, names):
                x, s_, f = operands(n)
                for name, tile in (("x", x), ("s", s_), ("ffn", f)):
                    if name in names and not (name == "s" and n >= OWN):
                        rows, place = step_rows(name, n, tile)
                        sp.dma_start(place, rows).then_inc(set_loaded[n % SETS], 16)

            def store_step(n):
                sp.wait_ge(*((pool_done, ONE + n + 1) if n < POOLS else (dve_done, ONE + n - POOLS + 1)))
                rows, place = step_rows("out", n, operands(n)[1])
                sp.dma_start(rows, place).then_inc(set_stored[n % SETS], 16)

            for u in range(2):
                sp.wait_ge(s_stored[u], ONE + 16 * (NT - NK) // 2)
            for u in range(2):
                sp.wait_ge(e_up_u[u], ONE + EP // 2)
                load_step(2 * u, ("x", "s"))
                load_step(2 * u + 1, ("x", "s"))
            move(B - 1, PAIRS // 2 - 1, 1)
            load_denominators(B - 1)
            sp.wait_ge(ey_full, ONE + EP)
            load_step(4, ("x", "s"))
            sp.wait_ge(scattered, 16 * (2 * EP + 3))
            for n in range(SETS):
                load_step(n, ("ffn",))
            for n in range(STEPS):
                store_step(n)
                if 1 <= n <= STEPS - SETS:
                    sp.wait_ge(set_stored[(n - 1) % SETS], ONE + 16 * ((n - 1) // SETS + 1))
                    load_step(n - 1 + SETS, ("x", "s", "ffn"))
            for q in range(SETS):
                sp.wait_ge(set_stored[q], ONE + 16 * len(range(q, STEPS, SETS)))
            for u in range(2):
                sp.wait_ge(o_moved_u[u], ONE + 64 * EP // 2)

        @block.gpsimd
        def _(pool):
            def gather(u, n):
                pool.wait_ge(index_ready, ONE + n)
                pool.sem_inc(passed, 1)
                nc.gpsimd.indirect_dma_start(out=xg[u][:], out_offset=None, in_=dram["xw"],
                                             in_offset=bass.IndirectOffsetOnAxis(ap=gi[u][:, 0:1], axis=0),
                                             bounds_check=T - 1).then_inc(x_gathered[u], 16)

            def scatter(u, e, n):
                if n is not None:
                    pool.wait_ge(scattered, 16 * n)
                    pool.sem_inc(passed, 1)
                nc.gpsimd.indirect_dma_start(out=dram["ffn"], out_offset=bass.IndirectOffsetOnAxis(ap=si[u][:, e:e + 1], axis=0),
                                             in_=ey[u][e * CAP:(e + 1) * CAP, :], in_offset=None,
                                             bounds_check=T + CAP - 1, compute_op=ALU.add).then_inc(scattered, 16)

            gather(0, 1)
            nc.gpsimd.memset(ey[1][:], 0.0).then_inc(made, 1)
            nc.gpsimd.iota(si[1][:].bitcast(I32), pattern=[[0, 2]], base=T, channel_multiplier=1).then_inc(made, 1)
            pool.wait_ge(made, ONE + 2)
            scatter(1, 0, None)
            nc.gpsimd.memset(den[:], 1.0)

            def pair(b, i, u):
                it, k, _, _ = numbers(b, i, u)
                for j in range(NK):
                    for h in range(2):
                        pool.wait_ge(squared[h], ONE + NK * it + j + 1)
                        pool.sem_inc(passed, 1)
                        d = a[h][j % 2][:, j * P:(j + 1) * P]
                        nc.gpsimd.affine_select(out=d, in_=d, compare_op=ALU.is_ge, fill=0.0, base=0,
                                                pattern=[[1, P]], channel_multiplier=-1).then_inc(masked[h], 1)
                    if j == 1:
                        pool.wait_ge(ey_ready, ONE + it)
                        scatter(1 - u, 0, 2 * it + 1)
                    if j == 4:
                        scatter(1 - u, 1, 2 * it + 2)
                    if j == 3:
                        gather(1 - u, it + 2)

            loop(pool, pair, lambda b, last: None)
            pool.wait_ge(ey_ready, ONE + EP)
            scatter(1, 0, 2 * EP + 1)
            scatter(1, 1, 2 * EP + 2)
            pool.wait_ge(scattered, 16 * (2 * EP + 3))
            for u in range(2):
                pool.wait_ge(x_gathered[u], 16 * (EP // 2 + 1 - u))
            for n in range(POOLS):
                combine(pool, nc.gpsimd, n, pool_product, pool_done)

        @block.scalar
        def _(act):
            def copy_o(it, u, k):
                act.wait_ge(o_full_u[u], ONE + k + 1)
                act.wait_ge(o_moved_u[u], ONE + 64 * k)
                for h in range(2):
                    nc.scalar.activation(o_raw[u][64 * h:64 * h + VW], O[64 * h:64 * h + VW], ACT.Copy).then_inc(o_copied, 1)

            def rden_hi(b, half):
                act.wait_ge(rden_done, ONE + RP * b + (half + 1) * RP // 2)
                part = slice(512 * half, 512 * (half + 1))
                nc.scalar.activation(rden_parts[0:2 * HEADS, part], rden[:, part], ACT.Copy).then_inc(rden_high, 1)

            def pair(b, i, u):
                it, k, first, start = numbers(b, i, u)
                for j in range(NK):
                    for h in range(2):
                        act.wait_ge(s_full[h], ONE + NK * it + j + 1)
                        nc.scalar.activation(a[h][j % 2][:, P * j:], S[h][:, P * j:], ACT.Square).then_inc(squared[h], 1)
                    if j == 0:
                        act.wait_ge(xgT_full, ONE + it + 1)
                        nc.scalar.activation(xgT[:], P1[:].rearrange("p (c t) -> p c t", c=C), ACT.Copy).then_inc(xgT_copied, 1)
                        if not first:
                            copy_o(it - 1, 1 - u, k - 1 + u)
                    if j == 4:
                        act.wait_ge(e_gate_full, ONE + it + 1)
                        nc.scalar.activation(esg[:], P1[:, 0:I], ACT.Silu).then_inc(e_silu_done, 1)
                    if j == 5:
                        act.wait_ge(ehT_full, ONE + it + 1)
                        nc.scalar.activation(ehT[:], P1[:, 0:IC * P].rearrange("p (c t) -> p c t", c=IC), ACT.Copy).then_inc(ehT_copied, 1)
                    if start and j in (5, 7):
                        rden_hi(b - 1, (j - 5) // 2)

            def sequence(b, last):
                def gate(n):
                    f = operands(n)[2]
                    act.wait_ge(set_loaded[n % SETS], ONE + 16 * loads_of(n))
                    nc.scalar.activation(f, f, ACT.Silu).then_inc(gated, 1)

                if last:
                    copy_o(EP - 1, 1, EP // 2 - 1)
                    gate(0)
                    gate(1)
                    rden_hi(b, 0)
                    rden_hi(b, 1)
                    gate(2)

                def cut(m):
                    act.wait_ge(normed, ONE + 2 * C * b + C * (m // TPG + 1))
                    if m >= TPG:
                        act.wait_ge(s_ready, ONE + NK * b + m - TPG + 1)
                    nc.scalar.activation(on_hi[:, m % TPG], oT[:, :, m * P:(m + 1) * P], ACT.Copy).then_inc(on_high, 1)

                for m in range(TPG):
                    cut(m)
                for m in range(NK):
                    act.wait_ge(s_ready, ONE + NK * b + m + 1)
                    half = slice(512 * (m % 2), 512 * (m % 2) + 512)
                    if last:
                        place = last_s[m // 2][:, half]
                    else:
                        act.wait_ge(s_stored[m % 2], ONE + 16 * (TPG * b + m // 2))
                        place = s_out[m % 2][:]
                    nc.scalar.activation(place, S[1][:, half], ACT.Copy).then_inc(s_copied, 1)
                    if m < TPG:
                        cut(m + TPG)
                    if last and m % 2:
                        gate(3 + m // 2)
                if last:
                    for n in range(3 + NK // 2, STEPS):
                        gate(n)

            loop(act, pair, sequence)

        @block.vector
        def _(dve):
            nc.vector.tensor_copy(gi[0][:], w["gather_from"][:, 0:1]).then_inc(index_ready, 1)

            def reciprocals(b, q):
                if q == 0:
                    dve.wait_ge(den_loaded, ONE + 16 * (b + 1))
                    dve.wait_ge(rden_high, ONE + 2 * b)
                part = slice(q * N // RP, (q + 1) * N // RP)
                nc.vector.reciprocal(rden[:, part], den[:, part]).then_inc(rden_done, 1)

            def rden_lo(b, half):
                dve.wait_ge(rden_high, ONE + 2 * b + half + 1)
                part = slice(512 * half, 512 * (half + 1))
                nc.vector.tensor_tensor(rden_parts[2 * HEADS:, part], rden[:, part], rden_parts[0:2 * HEADS, part].bitcast(F32),
                                        ALU.subtract).then_inc(rden_low, 1)

            def pair(b, i, u):
                it, k, first, start = numbers(b, i, u)
                for j in range(NK):
                    for h in range(2):
                        dve.wait_ge(masked[h], ONE + NK * it + j + 1)
                        part = a[h][j % 2][:, P * j:]
                        nc.vector.tensor_tensor(part, part, part, ALU.mult).then_inc(a_ready[h], 1)
                    if j == 2:
                        dve.wait_ge(x_gathered[u], 16 * (k + 1))
                        dve.wait_ge(scattered, 16 * (2 * it + 1))
                        nc.vector.tensor_copy(si[u][:], w["scatter_to"][:, bass.ds(2 * it, 2)])
                        for h in range(2):
                            part = slice(h * CAP, (h + 1) * CAP)
                            last = nc.vector.tensor_copy(wt[u][part, :], xg[u][part, bass.ds(2 * it + E + h, 1)])
                        last.then_inc(weight_ready, 1)
                        nc.vector.tensor_copy(gi[1 - u][:], w["gather_from"][:, bass.ds(it + 1, 1)]).then_inc(index_ready, 1)
                    if j == 4:
                        dve.wait_ge(e_silu_done, ONE + it + 1)
                        dve.wait_ge(e_up_u[u], ONE + k + 1)
                        dve.wait_ge(ehT_full, ONE + it)
                        nc.vector.tensor_tensor(eh[:], esg[:], P2[:, 0:I], ALU.mult).then_inc(e_hidden_done, 1)
                    if start and 2 <= j < 2 + RP:
                        reciprocals(b - 1, j - 2)
                    if start and j >= 6:
                        rden_lo(b - 1, j - 6)
                dve.wait_ge(ey_full, ONE + it + 1)
                dve.wait_ge(scattered, 16 * (2 * it + 1))
                dve.wait_ge(weight_ready, ONE + it + 1)
                nc.vector.tensor_scalar(ey[u][:], P2[:], wt[u][:, 0:1], None, ALU.mult).then_inc(ey_ready, 1)

            def sequence(b, last):
                if last:
                    for q in range(RP):
                        reciprocals(b, q)
                        if q >= 2:
                            rden_lo(b, q - 2)

                def normalise(n):
                    half, c = n // C, n % C
                    dve.wait_ge(spread, ONE + 2 * C * b + n + 1)
                    part = oT[:, c, 512 * half:512 * (half + 1)]
                    nc.vector.tensor_tensor(part, part, S[0][:, 512 * (c % 2):512 * (c % 2) + 512], ALU.mult).then_inc(normed, 1)

                def rest(m):
                    dve.wait_ge(on_high, ONE + 2 * C * b + m + 1)
                    nc.vector.tensor_tensor(on_lo[:, m % TPG], oT[:, :, m * P:(m + 1) * P], on_hi[:, m % TPG].bitcast(F32),
                                            ALU.subtract).then_inc(on_low_done, 1)

                for n in range(C):
                    normalise(n)
                for m in range(TPG):
                    rest(m)
                    normalise(C + m)
                for m in range(TPG, NK):
                    rest(m)
                if last:
                    for n in range(POOLS, STEPS):
                        combine(dve, nc.vector, n, dve_product, dve_done)

            loop(dve, pair, sequence)

        @block.tensor
        def _(pe):
            def scores(u, it, j, b, i, k):
                for h in range(2):
                    pe.wait_ge(squared[h], ONE + NK * it + j)
                    if j == 0 and isinstance(i, int) and i == 0 and u == 1:
                        pe.wait_ge(s_copied, ONE + NK * b)
                        pe.wait_ge(on_low_done, ONE + 2 * C * b)
                    for n0, n1 in pieces(j):
                        last = nc.tensor.matmul(S[h][:, n0:n1], ks[u][:, h, P * j:P * (j + 1)], qs[u][:, h, n0:n1], start=True, stop=True)
                    last.then_inc(s_full[h], 1)

            def values(u, it, j, k):
                for h in range(2):
                    pe.wait_ge(a_ready[h], ONE + NK * it + j + 1)
                if j == 0:
                    pe.wait_ge(o_copied, ONE + 2 * it)
                for n0, n1 in pieces(j):
                    for h in range(2):
                        last = nc.tensor.matmul(O[64 * h:64 * h + VW, n0:n1], vs[u][:, j, VW * h:VW * (h + 1)],
                                                a[h][j % 2][:, n0:n1], start=(j == 0), stop=(j == (3 if n0 < 512 else 7)))
                if j == NK - 1:
                    last.then_inc(o_full_u[u], 1)

            def expert(u, it, j, k):
                if j == 0:
                    pe.wait_ge(x_gathered[u], 16 * (k + 1))
                    pe.wait_ge(ehT_copied, ONE + it)
                    for c in range(C):
                        last = nc.tensor.transpose(P1[:, c * P:(c + 1) * P], xg[u][:, c:E:C], w["ident"][:])
                    last.then_inc(xgT_full, 1)
                elif j <= C:
                    c = j - 1
                    if c == 0:
                        pe.wait_ge(gu_loaded[u], ONE + 32 * (k + 1))
                        pe.wait_ge(xgT_copied, ONE + it + 1)
                        pe.wait_ge(ey_ready, ONE + it)
                    for out, wts, full in ((P1, wg[u], e_gate_full), (P2, wu[u], e_up_u[u])):
                        for h in range(2):
                            t = slice(h * CAP, (h + 1) * CAP)
                            last = nc.tensor.matmul(out[t, 0:I], xgT[:, c, t], wts[:, h, c], start=(c == 0), stop=(c == C - 1))
                        if c == C - 1:
                            last.then_inc(full, 1)
                elif j == 5:
                    pe.wait_ge(e_hidden_done, ONE + it + 1)
                    for c in range(IC):
                        last = nc.tensor.transpose(P1[:, c * P:(c + 1) * P], eh[:, c:I:IC], w["ident"][:])
                    last.then_inc(ehT_full, 1)
                else:
                    if j == 6:
                        pe.wait_ge(ehT_copied, ONE + it + 1)
                        pe.wait_ge(d_loaded, ONE + 16 * (it + 1))
                    for c in (0, 1) if j == 6 else (2,):
                        for h in range(2):
                            t = slice(h * CAP, (h + 1) * CAP)
                            last = nc.tensor.matmul(P2[t, :], ehT[:, c, t], wd[:, h, c], start=(c == 0), stop=(c == IC - 1))
                    if j == 7:
                        last.then_inc(ey_full, 1)

            def pair(b, i, u):
                it, k, first, _ = numbers(b, i, u)
                pe.wait_ge(qkv_loaded[u], ONE + 14 * 16 * (k + 1))
                for j in range(NK):
                    scores(u, it, j, b, i, k)
                    expert(u, it, j, k)
                    if j:
                        values(u, it, j - 1, k)
                    elif not first:
                        values(1 - u, it - 1, NK - 1, k - 1 + u)

            def sequence(b, last):
                if last:
                    values(1, EP - 1, NK - 1, EP // 2 - 1)
                for h in range(2):
                    pe.wait_ge(squared[h], ONE + NK * (PAIRS * (b + 1) + (not last)))

                def spread_out(n):
                    half, c = n // C, n % C
                    if c == 0:
                        pe.wait_ge(rden_low, ONE + 2 * b + half + 1)
                    if n >= 2:
                        pe.wait_ge(normed, ONE + 2 * C * b + n - 1)
                    nc.tensor.matmul(S[0][:, 512 * (c % 2):512 * (c % 2) + 512], sel[:, c], rden_parts[:, 512 * half:512 * (half + 1)],
                                     start=True, stop=True).then_inc(spread, 1)

                for n in range(C + 2):
                    spread_out(n)
                for m in range(NK):
                    pe.wait_ge(on_low_done, ONE + 2 * C * b + m + 1)
                    if m >= 2:
                        pe.wait_ge(s_copied, ONE + NK * b + m - 1)
                    out = S[1][:, 512 * (m % 2):512 * (m % 2) + 512]
                    hi, lo = on_hi[:, m % TPG], on_lo[:, m % TPG]
                    for c in range(C):
                        nc.tensor.matmul(out, hi[:, c], wo_hi[:, c], start=(c == 0), stop=False)
                        nc.tensor.matmul(out, hi[:, c], wo_lo[:, c], start=False, stop=False)
                        final = nc.tensor.matmul(out, lo[:, c], wo_hi[:, c], start=False, stop=(c == C - 1))
                    final.then_inc(s_ready, 1)
                    if m < C - 2:
                        spread_out(C + 2 + m)

            loop(pe, pair, sequence)


def build(nc, x, w_qkv, w_out, ln_scale, ln_bias, w_router, w_gate, w_up, w_down, w_sh_gate, w_sh_up, w_sh_down, out):
    cos, sin = rope_tables()
    scratch = lambda name, shape: nc.dram_tensor(name, shape, F32, kind="Internal").ap()
    dram = {
        "x": x.rearrange("b n e -> (b n) e"), "out": out.rearrange("b n e -> (b n) e"),
        "w_qkv": w_qkv, "w_out": w_out, "ln_scale": ln_scale, "ln_bias": ln_bias,
        "router": w_router, "w_gate": w_gate, "w_up": w_up, "w_down": w_down,
        "w_sh_gate": w_sh_gate, "w_sh_up": w_sh_up, "w_sh_down": w_sh_down,
        "cos": nc.inline_tensor(cos, "rope_cos").ap(), "sin": nc.inline_tensor(sin, "rope_sin").ap(),
        "xw": scratch("xw_rows", [T, XW]),
        "ffn": scratch("ffn_rows", [T + CAP, E]),
        "qT": scratch("qT_parts", [2, E, T]), "kT": scratch("kT_parts", [2, E, T]),
        "v": scratch("v_parts", [G, PAIRS, P, TPG * 2 * VW]),
        "den": scratch("denominators", [B, HEADS, N]), "s": scratch("attention_out", [T, E]),
    }
    with ExitStack() as keep:
        sb = lambda stack, name, shape, dt=F32: stack.enter_context(nc.sbuf_tensor(name, shape, dt))
        w = {"ident": sb(keep, "ident", [P, P]), "gather_from": sb(keep, "gather_from", [P, NE // 2 + 1], U32),
             "scatter_to": sb(keep, "scatter_to", [CAP, NE], U32), "oT": sb(keep, "oT", [P, C, N]),
             "found": sb(keep, "found", [P, CAP])}
        for half, name in enumerate(("mask", "ldiff")):
            w[name] = w["oT"][:].rearrange("p (h c) (a n) -> p h (c a) n", h=2, n=NE)[:, half]
        with ExitStack() as ctx:
            for k, n in (("qkv", C * 3 * E), ("gu", C * 2 * I), ("down", IC * E), ("router", C * NE)):
                w[k + "_hi"], w[k + "_lo"] = sb(ctx, k + "_hi", [P, n], F32R), sb(ctx, k + "_lo", [P, n], F32R)
            w |= {"cos": sb(ctx, "cos", [P, N // P, D]), "sin": sb(ctx, "sin", [P, N // P, D]),
                  "ln_scale": sb(ctx, "ln_scale_col", [P, 1]), "ln_bias": sb(ctx, "ln_bias_col", [P, 1]),
                  "minus_half": sb(ctx, "minus_half", [P, 2 * HEADS]),
                  "down": sb(ctx, "downcount", [P, 512]),
                  "x": sb(ctx, "x_group", [P, TPG, E]),
                  "stats": sb(ctx, "x_stats", [P, TPG, 6]), "mv": sb(ctx, "x_mean_var", [P, TPG, 2]),
                  "xvar": sb(ctx, "x_var", [P, TPG]), "xneg": sb(ctx, "x_minus_mean", [P, TPG]),
                  "xrstd": sb(ctx, "x_rstd", [P, TPG]), "xbias": sb(ctx, "x_bias", [P, TPG])}
            prepare(nc, dram, w)
            project(nc, dram, w)
        with ExitStack() as ctx:
            w |= attend_buffers(nc, ctx)
            list_tokens(nc, dram, w)
            attend(nc, dram, w)


_INS = ["L0_attn_x", "L0_attn_w_qkv", "L0_attn_w_out", "L0_attn_ln_scale", "L0_attn_ln_bias", "L0_ffn_w_router",
        "L0_ffn_w_gate", "L0_ffn_w_up", "L0_ffn_w_down", "L0_ffn_w_sh_gate", "L0_ffn_w_sh_up", "L0_ffn_w_sh_down"]


def kernel(**inputs):
    import numpy as _np
    import concourse.bacc as _bacc
    from concourse.bass_utils import run_bass_kernel_spmd as _run

    nc = _bacc.Bacc("TRN2", target_bir_lowering=False, num_devices=1)
    arrays, args = {}, []
    for name in _INS:
        a = _np.ascontiguousarray(inputs[name].T if name == "L0_ffn_w_router" else inputs[name])
        arrays[f"in_{name}"] = a
        args.append(nc.dram_tensor(f"in_{name}", a.shape, mybir.dt.from_np(a.dtype), kind="ExternalInput").ap())
    args.append(nc.dram_tensor("out_0", (B, N, E), F32, kind="ExternalOutput").ap())
    build(nc, *args)
    r = _run(nc, [arrays], core_ids=[0])
    return r.results[0]["out_0"]
```
